# Optimizing a Trainium2 kernel written in Bass

```python
import numpy as np
import jax
import jax.numpy as jnp

def _softmax(x, axis=-1):
    return jax.nn.softmax(x, axis=axis)

def _gelu(x):
    return jax.nn.gelu(x, approximate=True)

def _silu(x):
    return jax.nn.silu(x)

def _sigmoid(x):
    return jax.nn.sigmoid(x)

def _layernorm(x, axis=-1, eps=1e-05):
    m = jnp.mean(x, axis=axis, keepdims=True)
    v = jnp.var(x, axis=axis, keepdims=True)
    return (x - m) / jnp.sqrt(v + eps)

def _scatter_add(tgt, idx, src, axis=0):
    return tgt.at[idx].add(src)

def _segment_sum(src, seg, n):
    return jax.ops.segment_sum(src, seg, n)
kernel_name = 'mk_gps_d2_gnn_r8_732725'

def setup_inputs(seed: int=0):
    np.random.seed(seed)
    _w = jnp.asarray

    def _rec_inputs():
        import jax
        import jax.numpy as jnp
        _gk = jax.random.key(seed)
        x = -0.0001126 + 1 * jax.random.normal(jax.random.fold_in(_gk, 1), (1250, 768), jnp.float32)
        src = jax.random.randint(jax.random.fold_in(_gk, 2), (40000,), 0, 1250, jnp.int32)
        dst = jax.random.randint(jax.random.fold_in(_gk, 3), (40000,), 0, 1250, jnp.int32)
        _o = jnp.argsort(dst, stable=True)
        src = src[_o]
        dst = dst[_o]
        return (x, src, dst)
    x, src, dst = _rec_inputs()

    def _L0_gnn_setup():
        import jax, jax.numpy as jnp
        import numpy as np
        N_NODES = 1250
        N_EDGES = 10000
        IN_DIM, HID, OUT_DIM, HEADS = (768, 512, 768, 4)
        NEG_SLOPE = 0.2

        def _gat_layer(x, src, dst, W, a_src, a_dst, b, heads, d_out, concat):
            N = x.shape[0]
            h = (x @ W).reshape(N, heads, d_out)
            as_n = jnp.einsum('nhd,hd->nh', h, a_src)
            ad_n = jnp.einsum('nhd,hd->nh', h, a_dst)
            e = jax.nn.leaky_relu(as_n[src] + ad_n[dst], NEG_SLOPE)
            e_max = jax.lax.stop_gradient(jax.ops.segment_max(e, dst, num_segments=N))
            ex = jnp.exp(e - e_max[dst])
            denom = jax.ops.segment_sum(ex, dst, num_segments=N)
            alpha = ex / (denom[dst] + 1e-16)
            msg = alpha[:, :, None] * h[src]
            out = jax.ops.segment_sum(msg, dst, num_segments=N)
            out = out.reshape(N, heads * d_out) if concat else out.mean(axis=1)
            return out + b
        key = jax.random.key(seed)
        ks = jax.random.split(key, 10)
        g = 0.05
        return {'x': jax.random.normal(ks[0], (N_NODES, IN_DIM), jnp.float32), 'edge_index': jax.random.randint(ks[1], (2, N_EDGES), 0, N_NODES, jnp.int64), 'W1': jax.random.normal(ks[2], (IN_DIM, HEADS * HID), jnp.float32) * g, 'a1_src': jax.random.normal(ks[3], (HEADS, HID), jnp.float32) * g, 'a1_dst': jax.random.normal(ks[4], (HEADS, HID), jnp.float32) * g, 'b1': jnp.zeros((HEADS * HID,), jnp.float32), 'W2': jax.random.normal(ks[5], (HEADS * HID, OUT_DIM), jnp.float32) * g, 'a2_src': jax.random.normal(ks[6], (1, OUT_DIM), jnp.float32) * g, 'a2_dst': jax.random.normal(ks[7], (1, OUT_DIM), jnp.float32) * g, 'b2': jnp.zeros((OUT_DIM,), jnp.float32)}
    _L0_gnn_all = _L0_gnn_setup()
    _L0_gnn_in = {k: v for k, v in _L0_gnn_all.items() if k in ('W1', 'a1_src', 'a1_dst', 'b1', 'W2', 'a2_src', 'a2_dst', 'b2')}
    del _L0_gnn_all

    def _L0_mix_setup():
        import jax, jax.numpy as jnp
        import numpy as np
        B, N, C = (16, 512, 768)
        H, D, M = (12, 64, 256)
        key = jax.random.key(seed)
        ks = jax.random.split(key, 6)
        rf = jax.random.normal(ks[5], (M, D), jnp.float32)
        rf = rf / jnp.linalg.norm(rf, axis=1, keepdims=True)
        return {'x': jax.random.normal(ks[0], (B, N, C), jnp.float32), 'W_qkv': jax.random.normal(ks[1], (C, 3 * C), jnp.float32) * C ** (-0.5), 'b_qkv': jax.random.normal(ks[2], (3 * C,), jnp.float32) * 0.02, 'W_proj': jax.random.normal(ks[3], (C, C), jnp.float32) * C ** (-0.5), 'b_proj': jax.random.normal(ks[4], (C,), jnp.float32) * 0.02, 'random_features': rf}
    _L0_mix_all = _L0_mix_setup()
    _L0_mix_in = {k: v for k, v in _L0_mix_all.items() if k in ('W_qkv', 'b_qkv', 'W_proj', 'b_proj', 'random_features')}
    del _L0_mix_all

    def _L0_ffn_setup():
        import jax, jax.numpy as jnp
        import numpy as np
        B, S, D, F, E = (8, 256, 768, 384, 16)
        CAP = 64
        EPS = 1e-06

        def _switch_moe_block(x, ln_w, w_router, wi, wo):
            var = jnp.mean(jnp.square(x.astype(jnp.float32)), axis=-1, keepdims=True)
            normed = (x * jax.lax.rsqrt(var + EPS)).astype(x.dtype) * ln_w
            logits = jnp.einsum('bsd,de->bse', normed.astype(jnp.float32), w_router.astype(jnp.float32))
            probs = jax.nn.softmax(logits, axis=-1)
            expert_idx = jnp.argmax(probs, axis=-1)
            onehot = jax.nn.one_hot(expert_idx, E, dtype=jnp.float32)
            priority = jnp.cumsum(onehot, axis=1)
            keep = onehot * (priority <= CAP)
            pos = (priority - 1.0).astype(jnp.int32)
            dispatch = keep[..., None] * jax.nn.one_hot(pos, CAP, dtype=jnp.float32)
            expert_in = jnp.einsum('bsec,bsd->becd', dispatch, normed)
            h = jax.nn.relu(jnp.einsum('becd,edf->becf', expert_in, wi))
            expert_out = jnp.einsum('becf,efd->becd', h, wo)
            combined = jnp.einsum('bsec,becd->bsd', dispatch, expert_out)
            routed = jnp.sum(dispatch, axis=(2, 3)) > 0
            next_states = jnp.where(routed[..., None], combined.astype(x.dtype), normed)
            router_prob = jnp.max(probs, axis=-1, keepdims=True).astype(x.dtype)
            return x + router_prob * next_states
        key = jax.random.key(seed)
        k_x, k_r, k_wi, k_wo = jax.random.split(key, 4)
        x = jax.random.normal(k_x, (B, S, D), dtype=jnp.float32)
        ln_w = jnp.ones((D,), dtype=jnp.float32)
        w_router = jax.random.normal(k_r, (D, E), dtype=jnp.float32) * 0.02
        wi = jax.random.normal(k_wi, (E, D, F), dtype=jnp.float32) * D ** (-0.5)
        wo = jax.random.normal(k_wo, (E, F, D), dtype=jnp.float32) * F ** (-0.5)
        return {'x': x, 'ln_w': ln_w, 'w_router': w_router, 'wi': wi, 'wo': wo}
    _L0_ffn_all = _L0_ffn_setup()
    _L0_ffn_in = {k: v for k, v in _L0_ffn_all.items() if k in ('ln_w', 'w_router', 'wi', 'wo')}
    del _L0_ffn_all

    def _L1_gnn_setup():
        import jax, jax.numpy as jnp
        import numpy as np
        N_NODES = 1250
        key = jax.random.key(seed)
        k1, k2, k3 = jax.random.split(key, 3)
        x = jax.random.normal(k1, (N_NODES, 768), dtype=jnp.float32)
        edge_index = jax.random.randint(k2, (2, 12500), 0, N_NODES, dtype=jnp.int32)
        W = jax.random.normal(k3, (768, 768), dtype=jnp.float32) * (1.0 / np.sqrt(768))
        b = jnp.zeros((768,), dtype=jnp.float32)
        return {'x': x, 'edge_index': edge_index, 'W': W, 'b': b}
    _L1_gnn_all = _L1_gnn_setup()
    _L1_gnn_in = {k: v for k, v in _L1_gnn_all.items() if k in ('W', 'b')}
    del _L1_gnn_all

    def _L1_mix_setup():
        import jax, jax.numpy as jnp
        import numpy as np
        LN_EPS = 1e-05
        NORM_EPS = 1e-12

        def _layernorm(x, gamma, beta):
            mu = jnp.mean(x, axis=-1, keepdims=True)
            var = jnp.mean(jnp.square(x - mu), axis=-1, keepdims=True)
            return (x - mu) * jax.lax.rsqrt(var + LN_EPS) * gamma + beta

        def _l2norm(x):
            n = jnp.sqrt(jnp.sum(jnp.square(x), axis=-1, keepdims=True))
            return x / jnp.maximum(n, NORM_EPS)
        key = jax.random.key(seed)
        ks = jax.random.split(key, 4)
        B, N, C, E = (8, 512, 768, 768)
        x = jax.random.normal(ks[0], (B, N, C), dtype=jnp.float32)
        w_qkv = jax.random.normal(ks[1], (C, 3 * E), dtype=jnp.float32) * (1.0 / np.sqrt(C))
        w_proj = jax.random.normal(ks[2], (E, C), dtype=jnp.float32) * (1.0 / np.sqrt(E))
        ln_in_g = jnp.ones((C,), jnp.float32)
        ln_in_b = jnp.zeros((C,), jnp.float32)
        ln_out_g = jnp.ones((E,), jnp.float32)
        ln_out_b = jnp.zeros((E,), jnp.float32)
        return {'x': x, 'w_qkv': w_qkv, 'w_proj': w_proj, 'ln_in_g': ln_in_g, 'ln_in_b': ln_in_b, 'ln_out_g': ln_out_g, 'ln_out_b': ln_out_b}
    _L1_mix_all = _L1_mix_setup()
    _L1_mix_in = {k: v for k, v in _L1_mix_all.items() if k in ('w_qkv', 'w_proj', 'ln_in_g', 'ln_in_b', 'ln_out_g', 'ln_out_b')}
    del _L1_mix_all

    def _L1_ffn_setup():
        import jax, jax.numpy as jnp
        import numpy as np
        B, S, D, F, E = (2, 1024, 768, 384, 8)
        key = jax.random.key(seed)
        k0, k1, k2, k3, k4, k5 = jax.random.split(key, 6)
        scale = 0.02
        return {'hidden_states': jax.random.normal(k0, (B, S, D), dtype=jnp.float32), 'Wg': jax.random.normal(k1, (D, E), dtype=jnp.float32) * scale, 'W1': jax.random.normal(k2, (E, D, F), dtype=jnp.float32) * scale, 'b1': jnp.zeros((E, F), dtype=jnp.float32), 'W2': jax.random.normal(k3, (E, F, D), dtype=jnp.float32) * scale, 'b2': jnp.zeros((E, D), dtype=jnp.float32)}
    _L1_ffn_all = _L1_ffn_setup()
    _L1_ffn_in = {k: v for k, v in _L1_ffn_all.items() if k in ('Wg', 'W1', 'b1', 'W2', 'b2')}
    del _L1_ffn_all
    return {'x': x, 'src': src, 'dst': dst, 'L0_gnn_W1': _L0_gnn_in['W1'], 'L0_gnn_a1_src': _L0_gnn_in['a1_src'], 'L0_gnn_a1_dst': _L0_gnn_in['a1_dst'], 'L0_gnn_b1': _L0_gnn_in['b1'], 'L0_gnn_W2': _L0_gnn_in['W2'], 'L0_gnn_a2_src': _L0_gnn_in['a2_src'], 'L0_gnn_a2_dst': _L0_gnn_in['a2_dst'], 'L0_gnn_b2': _L0_gnn_in['b2'], 'L0_mix_W_qkv': _L0_mix_in['W_qkv'], 'L0_mix_b_qkv': _L0_mix_in['b_qkv'], 'L0_mix_W_proj': _L0_mix_in['W_proj'], 'L0_mix_b_proj': _L0_mix_in['b_proj'], 'L0_mix_random_features': _L0_mix_in['random_features'], 'L0_ffn_ln_w': _L0_ffn_in['ln_w'], 'L0_ffn_w_router': _L0_ffn_in['w_router'], 'L0_ffn_wi': _L0_ffn_in['wi'], 'L0_ffn_wo': _L0_ffn_in['wo'], 'L1_gnn_W': _L1_gnn_in['W'], 'L1_gnn_b': _L1_gnn_in['b'], 'L1_mix_w_qkv': _L1_mix_in['w_qkv'], 'L1_mix_w_proj': _L1_mix_in['w_proj'], 'L1_mix_ln_in_g': _L1_mix_in['ln_in_g'], 'L1_mix_ln_in_b': _L1_mix_in['ln_in_b'], 'L1_mix_ln_out_g': _L1_mix_in['ln_out_g'], 'L1_mix_ln_out_b': _L1_mix_in['ln_out_b'], 'L1_ffn_Wg': _L1_ffn_in['Wg'], 'L1_ffn_W1': _L1_ffn_in['W1'], 'L1_ffn_b1': _L1_ffn_in['b1'], 'L1_ffn_W2': _L1_ffn_in['W2'], 'L1_ffn_b2': _L1_ffn_in['b2']}

def reference(x, src, dst, L0_gnn_W1, L0_gnn_a1_src, L0_gnn_a1_dst, L0_gnn_b1, L0_gnn_W2, L0_gnn_a2_src, L0_gnn_a2_dst, L0_gnn_b2, L0_mix_W_qkv, L0_mix_b_qkv, L0_mix_W_proj, L0_mix_b_proj, L0_mix_random_features, L0_ffn_ln_w, L0_ffn_w_router, L0_ffn_wi, L0_ffn_wo, L1_gnn_W, L1_gnn_b, L1_mix_w_qkv, L1_mix_w_proj, L1_mix_ln_in_g, L1_mix_ln_in_b, L1_mix_ln_out_g, L1_mix_ln_out_b, L1_ffn_Wg, L1_ffn_W1, L1_ffn_b1, L1_ffn_W2, L1_ffn_b2):
    import jax
    import jax.numpy as jnp

    def _L0_gnn_ref(x, edge_index, W1, a1_src, a1_dst, b1, W2, a2_src, a2_dst, b2):
        import jax, jax.numpy as jnp
        import numpy as np
        N_NODES = 1250
        N_EDGES = 10000
        IN_DIM, HID, OUT_DIM, HEADS = (768, 512, 768, 4)
        NEG_SLOPE = 0.2

        def _gat_layer(x, src, dst, W, a_src, a_dst, b, heads, d_out, concat):
            N = x.shape[0]
            h = (x @ W).reshape(N, heads, d_out)
            as_n = jnp.einsum('nhd,hd->nh', h, a_src)
            ad_n = jnp.einsum('nhd,hd->nh', h, a_dst)
            e = jax.nn.leaky_relu(as_n[src] + ad_n[dst], NEG_SLOPE)
            e_max = jax.lax.stop_gradient(jax.ops.segment_max(e, dst, num_segments=N))
            ex = jnp.exp(e - e_max[dst])
            denom = jax.ops.segment_sum(ex, dst, num_segments=N)
            alpha = ex / (denom[dst] + 1e-16)
            msg = alpha[:, :, None] * h[src]
            out = jax.ops.segment_sum(msg, dst, num_segments=N)
            out = out.reshape(N, heads * d_out) if concat else out.mean(axis=1)
            return out + b
        N = x.shape[0]
        loops = jnp.arange(N, dtype=edge_index.dtype)
        src = jnp.concatenate([edge_index[0], loops])
        dst = jnp.concatenate([edge_index[1], loops])
        h = _gat_layer(x, src, dst, W1, a1_src, a1_dst, b1, HEADS, HID, True)
        h = jax.nn.elu(h)
        out = _gat_layer(h, src, dst, W2, a2_src, a2_dst, b2, 1, OUT_DIM, False)
        return out

    def _L0_mix_ref(x, W_qkv, b_qkv, W_proj, b_proj, random_features):
        import jax, jax.numpy as jnp
        import numpy as np
        B, N, C = (16, 512, 768)
        H, D, M = (12, 64, 256)
        b, n, c = x.shape
        qkv = (x @ W_qkv + b_qkv).reshape(b, n, 3, H, D)
        qkv = jnp.transpose(qkv, (2, 0, 3, 1, 4))
        q, k, v = (qkv[0], qkv[1], qkv[2])
        scale = D ** (-0.5)
        q = q * scale
        k = k * scale
        phi_q = jax.nn.relu(jnp.einsum('bhnd,md->bhnm', q, random_features))
        phi_k = jax.nn.relu(jnp.einsum('bhnd,md->bhnm', k, random_features))
        kv = jnp.einsum('bhnm,bhnd->bhmd', phi_k, v)
        attn = jnp.einsum('bhnm,bhmd->bhnd', phi_q, kv) / M
        out = jnp.transpose(attn, (0, 2, 1, 3)).reshape(b, n, c)
        return out @ W_proj + b_proj

    def _L0_ffn_ref(x, ln_w, w_router, wi, wo):
        import jax, jax.numpy as jnp
        import numpy as np
        B, S, D, F, E = (8, 256, 768, 384, 16)
        CAP = 64
        EPS = 1e-06

        def _switch_moe_block(x, ln_w, w_router, wi, wo):
            var = jnp.mean(jnp.square(x.astype(jnp.float32)), axis=-1, keepdims=True)
            normed = (x * jax.lax.rsqrt(var + EPS)).astype(x.dtype) * ln_w
            logits = jnp.einsum('bsd,de->bse', normed.astype(jnp.float32), w_router.astype(jnp.float32))
            probs = jax.nn.softmax(logits, axis=-1)
            expert_idx = jnp.argmax(probs, axis=-1)
            onehot = jax.nn.one_hot(expert_idx, E, dtype=jnp.float32)
            priority = jnp.cumsum(onehot, axis=1)
            keep = onehot * (priority <= CAP)
            pos = (priority - 1.0).astype(jnp.int32)
            dispatch = keep[..., None] * jax.nn.one_hot(pos, CAP, dtype=jnp.float32)
            expert_in = jnp.einsum('bsec,bsd->becd', dispatch, normed)
            h = jax.nn.relu(jnp.einsum('becd,edf->becf', expert_in, wi))
            expert_out = jnp.einsum('becf,efd->becd', h, wo)
            combined = jnp.einsum('bsec,becd->bsd', dispatch, expert_out)
            routed = jnp.sum(dispatch, axis=(2, 3)) > 0
            next_states = jnp.where(routed[..., None], combined.astype(x.dtype), normed)
            router_prob = jnp.max(probs, axis=-1, keepdims=True).astype(x.dtype)
            return x + router_prob * next_states
        return _switch_moe_block(x, ln_w, w_router, wi, wo)

    def _L1_gnn_ref(x, edge_index, W, b):
        import jax, jax.numpy as jnp
        import numpy as np
        N_NODES = 1250
        n = x.shape[0]
        loops = jnp.arange(n, dtype=edge_index.dtype)
        row = jnp.concatenate([edge_index[0], loops])
        col = jnp.concatenate([edge_index[1], loops])
        ones = jnp.ones(row.shape[0], dtype=x.dtype)
        deg = jax.ops.segment_sum(ones, col, num_segments=n)
        dinv = jnp.where(deg > 0, jax.lax.rsqrt(deg), 0.0)
        norm = dinv[row] * dinv[col]
        h = x @ W
        msg = h[row] * norm[:, None]
        out = jax.ops.segment_sum(msg, col, num_segments=n) + b
        return out

    def _L1_mix_ref(x, w_qkv, w_proj, ln_in_g, ln_in_b, ln_out_g, ln_out_b):
        import jax, jax.numpy as jnp
        import numpy as np
        LN_EPS = 1e-05
        NORM_EPS = 1e-12

        def _layernorm(x, gamma, beta):
            mu = jnp.mean(x, axis=-1, keepdims=True)
            var = jnp.mean(jnp.square(x - mu), axis=-1, keepdims=True)
            return (x - mu) * jax.lax.rsqrt(var + LN_EPS) * gamma + beta

        def _l2norm(x):
            n = jnp.sqrt(jnp.sum(jnp.square(x), axis=-1, keepdims=True))
            return x / jnp.maximum(n, NORM_EPS)
        h = _layernorm(x, ln_in_g, ln_in_b)
        qkv = h @ w_qkv
        q, k, v = jnp.split(qkv, 3, axis=-1)
        phi_q = _l2norm(q)
        phi_k = _l2norm(k)
        kv = jnp.sum(phi_k * v, axis=1)
        attn = phi_q * kv[:, None, :]
        out = _layernorm(attn, ln_out_g, ln_out_b) @ w_proj
        return out

    def _L1_ffn_ref(hidden_states, Wg, W1, b1, W2, b2):
        import jax, jax.numpy as jnp
        import numpy as np
        B, S, D, F, E = (2, 1024, 768, 384, 8)
        b, s, d = hidden_states.shape
        e = W1.shape[0]
        x = hidden_states.reshape(-1, d)
        logits = x @ Wg
        probs = jax.nn.softmax(logits, axis=-1)
        gate = jnp.max(probs, axis=-1)
        expert_idx = jnp.argmax(probs, axis=-1)
        h = jax.nn.silu(jnp.einsum('td,edf->etf', x, W1) + b1[:, None, :])
        y = jnp.einsum('etf,efd->etd', h, W2) + b2[:, None, :]
        combine = jax.nn.one_hot(expert_idx, e, dtype=x.dtype) * gate[:, None]
        out = jnp.einsum('te,etd->td', combine, y)
        return out.reshape(b, s, d)
    edge_index = jnp.stack([src, dst])
    xn = _layernorm(x, axis=-1)
    x = x + _L0_gnn_ref(xn, edge_index, L0_gnn_W1, L0_gnn_a1_src, L0_gnn_a1_dst, L0_gnn_b1, L0_gnn_W2, L0_gnn_a2_src, L0_gnn_a2_dst, L0_gnn_b2) + _L0_mix_ref(xn[None], L0_mix_W_qkv, L0_mix_b_qkv, L0_mix_W_proj, L0_mix_b_proj, L0_mix_random_features)[0]
    x = x + _L0_ffn_ref(_layernorm(x, axis=-1)[None], L0_ffn_ln_w, L0_ffn_w_router, L0_ffn_wi, L0_ffn_wo)[0]
    xn = _layernorm(x, axis=-1)
    x = x + _L1_gnn_ref(xn, edge_index, L1_gnn_W, L1_gnn_b) + _L1_mix_ref(xn[None], L1_mix_w_qkv, L1_mix_w_proj, L1_mix_ln_in_g, L1_mix_ln_in_b, L1_mix_ln_out_g, L1_mix_ln_out_b)[0]
    x = x + _L1_ffn_ref(_layernorm(x, axis=-1)[None], L1_ffn_Wg, L1_ffn_W1, L1_ffn_b1, L1_ffn_W2, L1_ffn_b2)[0]
    return x

_drawn_inputs = setup_inputs


def setup_inputs(seed=0):
    import zlib

    import numpy as np

    out = dict(_drawn_inputs(seed))
    spreads = {'L0_gnn_b1': (0.0, 0.1),
     'L0_gnn_b2': (0.0, 0.1),
     'L0_ffn_ln_w': (1.0, 0.2),
     'L1_gnn_b': (0.0, 0.1),
     'L1_mix_ln_in_g': (1.0, 0.2),
     'L1_mix_ln_in_b': (0.0, 0.1),
     'L1_mix_ln_out_g': (1.0, 0.2),
     'L1_mix_ln_out_b': (0.0, 0.1),
     'L1_ffn_b1': (0.0, 0.8),
     'L1_ffn_b2': (0.0, 0.776)}
    factors = {'L1_ffn_Wg': 3.629, 'L1_ffn_W1': 4.738, 'L1_ffn_W2': 4.516}
    for name, (base, spread) in spreads.items():
        noise = np.random.default_rng([zlib.crc32(name.encode()), seed]).standard_normal(out[name].shape)
        drawn = base * np.exp(spread * noise) if base else spread * noise
        out[name] = jnp.asarray(drawn.astype(out[name].dtype))
    for name, factor in factors.items():
        out[name] = (out[name] * factor).astype(out[name].dtype)
    return out
```

```python
from contextlib import ExitStack

import concourse.bass as bass
from concourse import mybir

F32 = mybir.dt.float32
BF16 = mybir.dt.bfloat16
I32 = mybir.dt.int32
ALU = mybir.AluOpType
ACT = mybir.ActivationFunctionType
AX = mybir.AxisListType.X


N = 1250
TP = 125
T = N // TP
D = 768
KD = D // 128
HALF = D // 2
NE = 40000
GE = 500
NG = NE // GE
QG = GE // TP
WIN = 50
NW = N // WIN
BIAS = 2 * NG
H1, HID = 4, 512
FC = HID // 128
IC = 250
NC = N // IC
TC = IC // TP
MH, MD, MM = 12, 64, 256
COLS = ((0, 500), (500, 500), (1000, 250))
E0, F0, CAP = 16, 384, 64
E1, F1 = 8, 384
F0C = F0 // 128
SLOTS = E0 * CAP
BANKS = 6
BIG = 1.0e30


def pe_groups():
    def transposed(name):
        return [("T", name, t, i) for t in range(T) for i in range(2)]

    def rows(name):
        return [(name, t, i) for t in range(T) for i in range(2)]

    g = transposed("xn")
    g += rows("v") + [("rfT",)]
    for p in range(MH // 2):
        g += [("q", p, c) for c in range(3)] + [("k", p, c) for c in range(3)]
        for s in range(2):
            g += [("phiq", p, s, m, c) for m in range(2) for c in range(3)]
            g += [("phik", p, s, i) for i in range(T // 2)]
        g += [("kv", p, s) for s in range(2)]
        g += [("at", p, c) for c in range(3)]
    g += rows("proj")
    g += [("edgeT", 0), ("edgeT", 1), ("groupB",), ("tables",)]
    g += [("deg",), ("coef1",)]
    g += [("max1", h, i) for h in range(H1) for i in range(3)]
    for h in range(H1):
        g += [("h1", h, t) for t in range(T)]
        for c in range(NC):
            g += [("den1", h, c)] + [("agg1", h, c, f) for f in range(FC)]
            if c:
                g += [("w2", h, (c - 1) * TC + t, i) for t in range(TC) for i in range(2)]
        g += [("w2", h, (NC - 1) * TC + t, i) for t in range(TC) for i in range(2)]
    g += [("max2", i) for i in range(3)]
    for c in range(NC):
        g += [("den2", c)] + [("agg2", c * TC + t, i) for t in range(TC) for i in range(2)]
    g += transposed("m0")
    g += [("logits0",), ("order0",)]
    for e in range(0, E0, 2):
        g += [("einT", e, i) for i in range(2)]
        for d in range(2):
            g += [("eh", e + d)] + [("eo", e + d, i) for i in range(2)]
    g += transposed("x2")
    g += rows("gcnh") + rows("gcn")
    g += transposed("hn")
    for t in range(T):
        g += [("mk", t, i) for i in range(2)] + [("mv", t, i) for i in range(2)]
    g += [("kvsum", i) for i in range(2)]
    g += rows("mq")
    g += transposed("on") + rows("mproj")
    g += transposed("m1")
    g += [("logits1",), ("gateT",)]
    for e in range(E1):
        g += [("fh", e, f, c) for f in range(F0C) for c in range(3)]
        g += [("fo", e, t, i) for t in range(T) for i in range(2)]
    g += rows("b2")
    return g


GROUPS = pe_groups()
AT = {key: n for n, key in enumerate(GROUPS)}
assert len(AT) == len(GROUPS)


class Steps:

    def __init__(self, eng, own):
        self.eng, self.own, self.count, self.last = eng, own, {}, None

    def __call__(self, ins, signal=None):
        if isinstance(signal, tuple):
            sem, n = signal
        else:
            sem = self.own if signal is None else signal
            n = self.count.get(id(sem), 0) + 1
            self.count[id(sem)] = n
        ins.then_inc(sem, 1)
        self.last = (sem, n)
        return ins

    def settle(self):
        self.eng.wait_ge(*self.last)


def build(nc, x, src, dst, W1, a1_src, a1_dst, b1, W2, a2_src, a2_dst, b2, Wqkv, bqkv, Wp, bp, rf,
          ln_w, w_router, wi, wo, Wg1, bg1, w_qkv, w_proj, in_g, in_b, out_g, out_b, Wg, F1w, F1b, F2w, F2b, out):
    with ExitStack() as ctx:
        def sb(name, words, dt=F32):
            return ctx.enter_context(nc.sbuf_tensor(name, [128, words], dt))

        sems = {}

        def sem(name):
            if name not in sems:
                sems[name] = ctx.enter_context(nc.semaphore(name))
            return sems[name]

        CTt = sb("CTt", T * N)
        RTt = sb("RTt", KD * N)
        R1t = sb("R1t", T * D)
        R2t = sb("R2t", T * D)
        WK = sb("WK", 15720)
        MISC = sb("MISC", 2120)
        PS = [ctx.enter_context(nc.psum_tensor(f"bank{i}", [128, 512], F32)) for i in range(8)]

        def wk(at, n, pattern=None, parts=128, base=WK, **kw):
            v = base[0:parts, at:at + n]
            return v.rearrange(pattern, **kw) if pattern else v

        CT = CTt[:, :].rearrange("p (t n) -> p t n", t=T)
        RT = RTt[:, :].rearrange("p (k n) -> p k n", k=KD)
        R1 = R1t[:, :].rearrange("p (t d) -> p t d", t=T)
        R2 = R2t[:, :].rearrange("p (t d) -> p t d", t=T)

        used = [0]

        def misc(n, pattern=None, **kw):
            a = used[0]
            used[0] += n
            assert used[0] <= 2120, used
            v = MISC[:, a:a + n]
            return v.rearrange(pattern, **kw) if pattern else v

        ident = misc(128)
        ones = misc(128)
        upto = misc(128)
        kvpad = misc(512, "p (s m d) -> p s m d", s=2, m=2)
        rfp = misc(512, "p (s m) -> p s m", s=2)
        bqk = misc(12)
        b1c = misc(16)
        dinv = misc(10)
        stat = misc(T * 12, "p (t n) -> p t n", t=T)
        mv = misc(T * 2, "p (t n) -> p t n", t=T)
        rstd = misc(T)
        AS = misc(80, "p (t n) -> p t n", t=T)
        AS2 = misc(80, "p (t n) -> p t n", t=T)
        Mx = misc(40, "p (h t) -> p h t", h=4)
        Ac = misc(40, "p (h t) -> p h t", h=4)
        Bc = misc(40, "p (h t) -> p h t", h=4)
        small = misc(60)
        rd2 = misc(2)

        filled_sem, own_v, own_a, own_g = sem("bank_filled"), sem("vector_step"), sem("scalar_step"), sem("pool_step")
        emptied_sem = [sem(f"bank_emptied{b}") for b in range(BANKS)]

        def bank(*key):
            return PS[AT[key] % BANKS]

        def filled(eng, *key):
            eng.wait_ge(filled_sem, AT[key] + 1)

        def emptied(eng, *key):
            eng.wait_ge(emptied_sem[AT[key] % BANKS], AT[key] // BANKS + 1)

        def all_emptied(eng, *key):
            for n in range(max(0, AT[key] - BANKS + 1), AT[key] + 1):
                emptied(eng, *GROUPS[n])

        def freed(*key):
            return emptied_sem[AT[key] % BANKS], AT[key] // BANKS + 1

        scr_xm = nc.dram_tensor("scr_xm", (N, D), F32).ap()
        scr_in = nc.dram_tensor("scr_in", (SLOTS, D), F32).ap()
        scr_out = nc.dram_tensor("scr_out", (SLOTS, D), F32).ap()

        def node_rows(a):
            return a.rearrange("(t p) d -> p t d", p=TP)

        def kchunks(a):
            return a.rearrange("(k p) n -> p k n", p=128)

        def row(a):
            return a.rearrange("(a n) -> a n", a=1)

        qT, kT = wk(0, 1250), wk(1250, 1250)
        rfn = wk(0, 512, "p (s m d) -> p s m d", s=2, m=2)
        PQ = wk(2500, 5000, "p (s m n) -> p s m n", s=2, m=2)
        PK = wk(7500, 5120, "p (s t m) -> p s t m", s=2, t=T)
        bv_row = wk(7500, 768)
        Wqk = [wk(12620 + 1536 * i, 1536, "p (k w n) -> p k w n", k=KD, w=2) for i in range(2)]
        bias_rows = wk(0, 1536, "p (i d) -> p i d", i=2)
        ATt = CTt[:, 0:7500].rearrange("p (k n) -> p k n", k=KD)
        Wv = CTt[:, 7500:12108].rearrange("p (k n) -> p k n", k=KD)
        nat_i = WK[0:NG, 0:1000].bitcast(I32).rearrange("p (a e) -> p a e", a=2)
        nat = wk(1000, 1000, "p (a e) -> p a e", NG, a=2)
        keys = wk(2000, 1000, "p (a e) -> p a e", NG, a=2)
        tdiv = wk(3000, 500, None, NG)
        gmm = wk(3500, 2, None, NG)
        tab = wk(3510, 16, None, NW)
        iota_i = WK[:, 3600:4100].bitcast(I32)
        iota = wk(4100, 500)
        cutI = wk(4600, 80, None, NW)
        cutJ = wk(4700, 80, None, NW)
        cutK = wk(4800, 80, None, NW)
        trow_i = WK[0:1, 4900:4980].bitcast(I32)
        trow = WK[0:1, 5040:5066]
        iota_c_i = WK[:, 4980:4981].bitcast(I32)
        iota_c = wk(4984, 2)
        upper = wk(5000, 32, None, 32)
        KL = wk(5100, 640, "p (a q g) -> p a q g", a=2, q=QG)
        oh_lo = [WK[:, 5800 + 64 * i:5864 + 64 * i].bitcast(BF16) for i in range(QG)]
        oh_key = [WK[:, 6100 + 250 * i:6350 + 250 * i].bitcast(BF16) for i in range(QG)]
        zero_bf = WK[:, 7100:7350].bitcast(BF16)
        degp = wk(7400, 1250)
        arow = wk(0, 4096, "p (a n) -> p a n", a=2)
        W1s = [wk(4096 + 3072 * i, 3072, "p (k n) -> p k n", k=KD) for i in range(2)]
        junk = wk(10240, 768)
        wa = wk(11100, 48, "p (k n) -> p k n", k=KD)
        maxacc = wk(0, 5000, "p (h n) -> p h n", h=4)
        maskt = wk(5000, 1250)
        Hh = wk(0, 5120, "p (t n) -> p t n", t=T)
        Pm = [wk(5120 + 2500 * i, 2500, "p (t n) -> p t n", t=T) for i in range(2)]
        H1T = [wk(10120 + 1000 * i, 1000, "p (f n) -> p f n", f=FC) for i in range(2)]
        U = wk(12120, 2500, "p (t n) -> p t n", t=T)
        rden = [wk(14620 + 250 * i, 250) for i in range(2)]
        Sp = [wk(15120 + 250 * i, 250) for i in range(2)]
        W1h = R1t[:, 0:3072].rearrange("p (k n) -> p k n", k=KD)
        W2h = R1t[:, 3072:6144].rearrange("p (k n) -> p k n", k=FC)
        elu_z = R1t[:, 6144:6394]
        elu_m = R1t[:, 6394:6644]
        elu_r = R1t[:, 6644:6894]
        a2row = wk(0, 1536, "p (a n) -> p a n", a=2)
        junk2 = wk(1536, 768)
        max2a, mask2 = wk(2304, 1250), wk(3554, 1250)
        lnw_row = wk(0, 768)
        router = wk(768, 96, "p (k e) -> p k e", k=KD)
        G0 = wk(900, 160, "p (t e) -> p t e", t=T)
        G1 = wk(1060, 160, "p (t e) -> p t e", t=T)
        G2 = wk(1220, 160, "p (t e) -> p t e", t=T)
        G3 = wk(1380, 160, "p (t e) -> p t e", t=T)
        ebase = wk(1540, 160, "p (t e) -> p t e", t=T)
        esort = wk(1700, 160, "p (t e) -> p t e", t=T)
        gcol = wk(1860, 120, "p (c t) -> p c t", c=12)
        e_i = WK[:, 1980:2140].bitcast(I32)
        slot_s = WK[:, 2140:2150].bitcast(I32)
        slot_g = WK[:, 2150:2160].bitcast(I32)
        zero_row = wk(2200, 768)
        ein = wk(3000, 768)
        einT = wk(3768, 768, "p (k n) -> p k n", k=KD)
        hE = [wk(4540 + 192 * i, 192, "p (f n) -> p f n", f=F0C) for i in range(2)]
        oE = [wk(4930 + 768 * i, 768) for i in range(2)]
        EW = [wk(6500 + 4608 * i, 4608) for i in range(2)]
        wiE = [w[:, 0:2304].rearrange("p (k n) -> p k n", k=KD) for w in EW]
        woE = [w[:, 2304:4608].rearrange("p (k n) -> p k n", k=F0C) for w in EW]
        gath = [wk(6500 + 768 * i, 768) for i in range(2)]
        gH = wk(0, 7680, "p (t d) -> p t d", t=T)
        gW = wk(7680, 4608, "p (k n) -> p k n", k=KD)
        grow = wk(12300, 768)
        wqv = [CTt[:, 4608 * i:4608 * i + 4608].rearrange("p (k n) -> p k n", k=KD) for i in range(2)]
        wq2 = wk(0, 4608, "p (k n) -> p k n", k=KD)
        wpr = wk(4608, 4608, "p (k n) -> p k n", k=KD)
        kt_ = [wk(9216 + 768 * i, 768) for i in range(2)]
        sq_ = wk(10752, 768)
        psum_row = wk(11520, 768)
        kvb = wk(12288, 768)
        grow2 = wk(13056, 1536, "p (a n) -> p a n", a=2)
        prodsum = wk(14592, 768)
        FW = [CTt[:, 4608 * i:4608 * i + 4608] for i in range(2)]
        w1E = [w[:, 0:2304].rearrange("p (k n) -> p k n", k=KD) for w in FW]
        w2E = [w[:, 2304:4608].rearrange("p (k n) -> p k n", k=F0C) for w in FW]
        hF = wk(0, 3750, "p (f n) -> p f n", f=F0C)
        wgE = wk(3750, 48, "p (k e) -> p k e", k=KD)
        L0 = wk(3800, 80, "p (t e) -> p t e", t=T)
        L1 = wk(3880, 80, "p (t e) -> p t e", t=T)
        L2 = wk(3960, 80, "p (t e) -> p t e", t=T)
        esort1 = wk(4040, 80, "p (t e) -> p t e", t=T)
        lcol = wk(4120, 40, "p (c t) -> p c t", c=4)
        gateT = wk(4200, 1250, None, E1)
        b2E = wk(5500, 768, None, E1)
        b1E = wk(6300, 24, "p (e f) -> p e f", e=E1)

        block = ctx.enter_context(nc.Block())

        @block.sync
        def _(sp):
            def load(o, i, s):
                sp.dma_start(o, i).then_inc(sem(s), 16)

            def after(*key):
                filled(sp, *key)

            for t in range(T):
                load(R1[0:TP, t, :], x[t * TP:(t + 1) * TP, :], "in_x")
            load(Wv, kchunks(Wqkv[:, 2 * D:3 * D]), "in_Wv")
            load(bv_row, row(bqkv[2 * D:3 * D]).to_broadcast([128, D]), "in_bv")
            sp.wait_ge(sem("pads"), 1)
            for s in range(2):
                load(rfn[:, s, :, s * MD:(s + 1) * MD], rf.rearrange("(m p) d -> p m d", p=128), "in_rf")
            with nc.allow_non_contiguous_dma(reason="columns of a short vector"):
                load(bqk, bqkv[0:2 * D].rearrange("(k p) -> p k", p=128), "in_bqk")
                load(b1c, b1.rearrange("(k p) -> p k", p=128), "in_b1")
            for p in range(MH // 2):
                if p >= 2:
                    after("k", p - 2, 2)
                for w in range(2):
                    load(Wqk[p % 2][:, :, w, :], kchunks(Wqkv[:, w * D + 128 * p:w * D + 128 * p + 128]), f"in_Wqk{p % 2}")
            after("v", T - 1, 1)
            load(Wv, kchunks(Wp), "in_Wp")
            after("at", 5, 2)
            load(bias_rows[:, 0, :], row(bp).to_broadcast([128, D]), "in_bias")
            load(bias_rows[:, 1, :], row(b2).to_broadcast([128, D]), "in_bias")
            all_emptied(sp, "proj", T - 1, 1)
            sp.wait_ge(sem("bias_added"), T)
            load(nat_i[:, 0, :], src.rearrange("(g e) -> g e", g=NG), "in_edges")
            load(nat_i[:, 1, :], dst.rearrange("(g e) -> g e", g=NG), "in_edges")
            sp.dma_start(node_rows(scr_xm), R1[0:TP, :, :]).then_inc(sem("xm_kept"), 16)
            emptied(sp, "deg")
            load(arow[:, 0, :], row(a1_src.rearrange("h d -> (h d)")).to_broadcast([128, 2048]), "in_a1")
            load(arow[:, 1, :], row(a1_dst.rearrange("h d -> (h d)")).to_broadcast([128, 2048]), "in_a1")
            for h in range(H1):
                if h >= 2:
                    sp.wait_ge(sem("W1_folded"), h - 1)
                load(W1s[h % 2], kchunks(W1[:, h * HID:(h + 1) * HID]), f"in_W1s{h % 2}")
            sp.wait_ge(sem("xm_kept"), 16)
            for h in range(H1):
                if h:
                    after("w2", h - 1, T - 1, 1)
                load(W1h, kchunks(W1[:, h * HID:(h + 1) * HID]), "in_W1h")
                load(W2h, W2[h * HID:(h + 1) * HID, :].rearrange("(k p) n -> p k n", p=128), "in_W2h")
            after("w2", H1 - 1, T - 1, 1)
            load(a2row[:, 0, :], a2_src.to_broadcast([128, D]), "in_a2")
            load(a2row[:, 1, :], a2_dst.to_broadcast([128, D]), "in_a2")
            all_emptied(sp, "w2", H1 - 1, T - 1, 1)
            load(R1[0:TP, :, :], node_rows(scr_xm), "xm_back")
            all_emptied(sp, "agg2", T - 1, 1)
            load(lnw_row, row(ln_w).to_broadcast([128, D]), "in_lnw")
            load(router, kchunks(w_router), "in_router")
            sp.wait_ge(sem("zeros_set"), 1)
            for i in range(SLOTS // 128):
                sp.dma_start(scr_in[i * 128:(i + 1) * 128, :], zero_row).then_inc(sem("slots_zeroed"), 16)
            for e in range(E0):
                if e >= 2:
                    after("eo", e - 2, 1)
                if e % 2 == 0:
                    if e:
                        after("einT", e - 2, 1)
                    else:
                        sp.wait_ge(sem("scattered"), 16 * T)
                load(wiE[e % 2], kchunks(wi[e]), f"in_we{e % 2}")
                load(woE[e % 2], kchunks(wo[e]), f"in_we{e % 2}")
                if e % 2 == 0:
                    load(ein, scr_in[e * CAP:(e + 2) * CAP, :], "in_ein")
            sp.wait_ge(sem("switch_done"), 1)
            load(gW, kchunks(Wg1), "in_gW")
            load(grow, row(bg1).to_broadcast([128, D]), "in_gb")
            after("gcn", T - 1, 1)
            load(wqv[0], kchunks(w_qkv[:, D:2 * D]), "in_wk")
            load(wqv[1], kchunks(w_qkv[:, 2 * D:3 * D]), "in_wv")
            load(wq2, kchunks(w_qkv[:, 0:D]), "in_wq")
            load(wpr, kchunks(w_proj), "in_wp")
            all_emptied(sp, "gcn", T - 1, 1)
            load(grow2[:, 0, :], row(in_g).to_broadcast([128, D]), "in_ln")
            load(grow2[:, 1, :], row(in_b).to_broadcast([128, D]), "in_ln")
            sp.wait_ge(sem("hn_rows"), T)
            load(grow2[:, 0, :], row(out_g).to_broadcast([128, D]), "in_ln")
            load(grow2[:, 1, :], row(out_b).to_broadcast([128, D]), "in_ln")
            all_emptied(sp, "mproj", T - 1, 1)
            load(wgE, kchunks(Wg), "in_wg")
            load(b2E, F2b, "in_b2E")
            for e in range(E1):
                with nc.allow_non_contiguous_dma(reason="columns of a short vector"):
                    sp.dma_start(b1E[:, e, :], F1b[e].rearrange("(f p) -> p f", p=128)).then_inc(sem("in_b1E"), 16)
            for e in range(E1):
                if e >= 2:
                    after("fo", e - 2, T - 1, 1)
                load(w1E[e % 2], kchunks(F1w[e]), f"in_fe{e % 2}")
                load(w2E[e % 2], kchunks(F2w[e]), f"in_fe{e % 2}")
            all_emptied(sp, "b2", T - 1, 1)
            sp.dma_start(node_rows(out), R1[0:TP, :, :]).then_inc(sem("out_stored"), 16)
            sp.wait_ge(sem("out_stored"), 16)

        @block.tensor
        def _(pe):
            nth = [0]

            def group(*key):
                n = nth[0]
                assert GROUPS[n] == key, (GROUPS[n], key)
                nth[0] += 1
                if n >= BANKS:
                    pe.wait_ge(emptied_sem[n % BANKS], n // BANKS)
                return PS[n % BANKS]

            def mm(o, lhsT, rhs, first, last):
                return nc.tensor.matmul(o, lhsT, rhs, start=first, stop=last)

            def close(ins):
                ins.then_inc(filled_sem, 1)

            def transposed(name, rows_sem, rows_at=1):
                for t in range(T):
                    pe.wait_ge(rows_sem, rows_at * (t + 1))
                    for i in range(2):
                        ps = group("T", name, t, i)
                        for j in range(3):
                            k = 3 * i + j
                            ins = nc.tensor.transpose(ps[:, j * TP:(j + 1) * TP], R2[0:TP, t, k * 128:(k + 1) * 128], ident[0:TP, 0:TP])
                        close(ins)

            def rows(name, t, w, lhs=RT):
                for i in range(2):
                    ps = group(name, t, i)
                    for k in range(KD):
                        ins = mm(ps[0:TP, 0:HALF], lhs[:, k, t * TP:(t + 1) * TP], w[:, k, i * HALF:(i + 1) * HALF], k == 0, k == KD - 1)
                    close(ins)

            pe.wait_ge(sem("consts"), 3)
            transposed("xn", sem("xn_rows"))
            all_emptied(pe, "T", "xn", T - 1, 1)
            pe.wait_ge(sem("in_Wv"), 16)
            for t in range(T):
                rows("v", t, Wv)
            pe.wait_ge(sem("in_rf"), 32)
            ps = group("rfT")
            for s in range(2):
                for m in range(2):
                    ins = nc.tensor.transpose(ps[:, (2 * s + m) * 128:(2 * s + m + 1) * 128], rfn[:, s, m, :], ident)
            close(ins)
            for p in range(MH // 2):
                pe.wait_ge(sem(f"in_Wqk{p % 2}"), 32 * (p // 2 + 1))
                for w, name in enumerate("qk"):
                    for c, (c0, cn) in enumerate(COLS):
                        ps = group(name, p, c)
                        for k in range(KD):
                            ins = mm(ps[:, 0:cn], Wqk[p % 2][:, k, w, :], RT[:, k, c0:c0 + cn], k == 0, k == KD - 1)
                        close(ins)
                all_emptied(pe, "k", p, 2)
                for s in range(2):
                    for m in range(2):
                        for c, (c0, cn) in enumerate(COLS):
                            ps = group("phiq", p, s, m, c)
                            close(mm(ps[:, 0:cn], rfp[:, s, m * 128:(m + 1) * 128], qT[:, c0:c0 + cn], True, True))
                    for i in range(T // 2):
                        ps = group("phik", p, s, i)
                        for j in range(2):
                            t = 2 * i + j
                            ins = mm(ps[0:TP, j * MM:(j + 1) * MM], kT[:, t * TP:(t + 1) * TP], rfp[:, s, :], True, True)
                        close(ins)
                for s in range(2):
                    all_emptied(pe, "phik", p, s, T // 2 - 1)
                    if p == 0 and s == 0:
                        all_emptied(pe, "v", T - 1, 1)
                    ps = group("kv", p, s)
                    for m in range(2):
                        for t in range(T):
                            ins = mm(ps[:, m * MD:(m + 1) * MD], PK[0:TP, s, t, m * 128:(m + 1) * 128],
                                     R2[0:TP, t, (2 * p + s) * MD:(2 * p + s + 1) * MD], t == 0, t == T - 1)
                    close(ins)
                all_emptied(pe, "kv", p, 1)
                for s in range(2):
                    all_emptied(pe, "phiq", p, s, 1, 2)
                for c, (c0, cn) in enumerate(COLS):
                    ps = group("at", p, c)
                    for s in range(2):
                        for m in range(2):
                            ins = mm(ps[:, 0:cn], kvpad[:, s, m, :], PQ[:, s, m, c0:c0 + cn], s + m == 0, s + m == 2)
                    close(ins)
            all_emptied(pe, "at", 5, 2)
            pe.wait_ge(sem("in_Wp"), 16)
            for t in range(T):
                rows("proj", t, Wv, ATt)

            pe.wait_ge(sem("edge_keys"), 1)
            for a in range(2):
                ps = group("edgeT", a)
                for q in range(QG):
                    ins = nc.tensor.transpose(ps[0:TP, q * NG:(q + 1) * NG], keys[:, a, q * TP:(q + 1) * TP], ident[0:NG, 0:NG])
                close(ins)
            ps = group("groupB")
            for a in range(2):
                ins = mm(ps[0:NW, a * NG:(a + 1) * NG], gmm[:, a:a + 1].to_broadcast([NG, NW]), ident[0:NG, 0:NG], True, True)
            close(ins)
            pe.wait_ge(sem("window_cols"), 1)
            ps = group("tables")
            for a in range(2):
                mm(ps[0:1, a * NW:(a + 1) * NW], tab[:, a:a + 1], ident[0:NW, 0:NW], True, True)
            close(mm(ps[0:1, 2 * NW:3 * NW], tab[:, 2:3], upper[0:NW, 0:NW], True, True))
            pe.wait_ge(sem("window_table"), 1)
            pe.wait_ge(sem("iota_set"), 1)
            pe.sem_inc(sem("onehots_used"), BIAS + 2)
            for w in range(NW):
                ps = PS[6 + w % 2]
                if w >= 2:
                    pe.wait_ge(sem("window_emptied"), w - 1)
                g0 = pe.value_load(trow_i[0:1, w:w + 1], min_val=0, max_val=NG - 1)
                g1 = pe.value_load(trow_i[0:1, NW + w:NW + w + 1], min_val=1, max_val=NG)
                base = pe.value_load(trow_i[0:1, 2 * NW + w:2 * NW + w + 1], min_val=0, max_val=2 * NG * NW + BIAS)
                nc.tensor.matmul(ps[0:TP, 0:500], zero_bf[0:TP, 0:TP], zero_bf[0:TP, 0:500], start=True, stop=False)
                with pe.Fori(g0, g1) as g:
                    for half in range(2):
                        pe.wait_ge(sem("onehots_ready"), base + g * 2 + (half + 1))
                        for q in range(2 * half, 2 * half + 2):
                            ins = nc.tensor.matmul(ps[0:TP, 0:500], oh_lo[q][0:TP, 0:TP], oh_key[q][0:TP, 0:500], start=False, stop=False)
                        ins.then_inc(sem("onehots_used"), 1)
                nc.tensor.matmul(ps[0:TP, 0:500], zero_bf[0:TP, 0:TP], zero_bf[0:TP, 0:500], start=False, stop=True).then_inc(sem("window_filled"), 1)
            pe.wait_ge(sem("deg_parts"), 1)
            ps = group("deg")
            for t in range(T):
                ins = mm(ps[0:TP, t:t + 1], degp[0:TP, t * TP:(t + 1) * TP], ones[0:TP, 0:1], True, True)
            close(ins)

            pe.wait_ge(sem("W1_folded"), H1)
            ps = group("coef1")
            for t in range(T):
                for k in range(KD):
                    ins = mm(ps[0:TP, t * 8:t * 8 + 8], RT[:, k, t * TP:(t + 1) * TP], wa[:, k, :], k == 0, k == KD - 1)
            close(ins)

            def max_tiles(i, acc, *key):
                ps = group(*key)
                for j, t in enumerate(range(4 * i, min(4 * i + 4, T))):
                    ins = nc.tensor.transpose(ps[0:TP, j * TP:(j + 1) * TP], acc[0:TP, t * TP:(t + 1) * TP], ident[0:TP, 0:TP])
                close(ins)

            pe.wait_ge(sem("max_rows"), 1)
            for h in range(H1):
                for i in range(3):
                    max_tiles(i, maxacc[:, h, :], "max1", h, i)

            def coef_rows(u, h, c):
                if u >= 2:
                    pe.wait_ge(sem("coef_used"), u - 1)
                ps = PS[6 + u % 2]
                for a, col in enumerate((Ac, Bc)):
                    for t in range(TC):
                        tt = c * TC + t
                        ins = mm(ps[0:TP, (a * TC + t) * TP:(a * TC + t + 1) * TP], col[0:TP, h, tt:tt + 1].to_broadcast([TP, TP]),
                                 ident[0:TP, 0:TP], True, True)
                ins.then_inc(sem("coef_rows"), 1)

            pe.wait_ge(sem("coef_cols"), 1)
            coef_rows(0, 0, 0)
            for h in range(H1):
                pe.wait_ge(sem("in_W1h"), 16 * (h + 1))
                for t in range(T):
                    ps = group("h1", h, t)
                    for k in range(KD):
                        ins = mm(ps[0:TP, :], RT[:, k, t * TP:(t + 1) * TP], W1h[:, k, :], k == 0, k == KD - 1)
                    close(ins)
                all_emptied(pe, "h1", h, T - 1)
                pe.wait_ge(sem("in_W2h"), 16 * (h + 1))

                def w2(c):
                    all_emptied(pe, "agg1", h, c, FC - 1)
                    pe.wait_ge(sem("elu_done"), FC * (h * NC + c + 1))
                    for t in range(TC):
                        for i in range(2):
                            ps = group("w2", h, c * TC + t, i)
                            for f in range(FC):
                                ins = mm(ps[0:TP, 0:HALF], H1T[c % 2 if h % 2 == 0 else (c + 1) % 2][:, f, t * TP:(t + 1) * TP],
                                         W2h[:, f, i * HALF:(i + 1) * HALF], f == 0, f == FC - 1)
                            close(ins)

                for c in range(NC):
                    u = h * NC + c
                    if u + 1 < H1 * NC:
                        coef_rows(u + 1, (u + 1) // NC, (u + 1) % NC)
                    pe.wait_ge(sem("P_sums"), u + 1)
                    ps = group("den1", h, c)
                    close(mm(ps[:, 0:IC], ones[0:TP, :], Sp[u % 2][0:TP, :], True, True))
                    pe.wait_ge(sem("P_ready"), u + 1)
                    for f in range(FC):
                        ps = group("agg1", h, c, f)
                        for j in range(T):
                            ins = mm(ps[:, 0:IC], Hh[0:TP, j, f * 128:(f + 1) * 128], Pm[u % 2][0:TP, j, :], j == 0, j == T - 1)
                        close(ins)
                    if c:
                        w2(c - 1)
                w2(NC - 1)

            pe.wait_ge(sem("max_rows"), 2)
            for i in range(3):
                max_tiles(i, max2a, "max2", i)
            pe.wait_ge(sem("coef_cols"), 2)
            coef_rows(H1 * NC, 0, 0)
            for c in range(NC):
                u = H1 * NC + c
                if c + 1 < NC:
                    coef_rows(u + 1, 0, c + 1)
                pe.wait_ge(sem("P_sums"), u + 1)
                ps = group("den2", c)
                for t in range(TC):
                    ins = mm(ps[0:TP, t:t + 1], Sp[u % 2][0:TP, t * TP:(t + 1) * TP], ones[0:TP, 0:1], True, True)
                close(ins)
                pe.wait_ge(sem("P_ready"), u + 1)
                for t in range(TC):
                    for i in range(2):
                        ps = group("agg2", c * TC + t, i)
                        for j in range(T):
                            ins = mm(ps[0:TP, 0:HALF], Pm[u % 2][0:TP, j, t * TP:(t + 1) * TP],
                                     R2[0:TP, j, i * HALF:(i + 1) * HALF], j == 0, j == T - 1)
                        close(ins)

            transposed("m0", sem("normed_rows"))
            all_emptied(pe, "T", "m0", T - 1, 1)
            pe.wait_ge(sem("in_router"), 16)
            ps = group("logits0")
            for t in range(T):
                for k in range(KD):
                    ins = mm(ps[0:TP, t * E0:(t + 1) * E0], RT[:, k, t * TP:(t + 1) * TP], router[:, k, :], k == 0, k == KD - 1)
            close(ins)
            pe.wait_ge(sem("onehot0"), 1)
            ps = group("order0")
            oh = G1[0:TP, :, :].rearrange("p t e -> p (t e)")
            mm(ps[0:TP, 0:160], upto[0:TP, 0:TP], oh, True, True)
            close(mm(ps[0:TP, 160:320], ones[0:TP, 0:TP], oh, True, True))
            for e in range(0, E0, 2):
                pe.wait_ge(sem("in_ein"), 16 * (e // 2 + 1))
                for i in range(2):
                    ps = group("einT", e, i)
                    for j in range(3):
                        k = 3 * i + j
                        ins = nc.tensor.transpose(ps[:, j * 128:(j + 1) * 128], ein[:, k * 128:(k + 1) * 128], ident[:, :])
                    close(ins)
                all_emptied(pe, "einT", e, 1)
                for d in range(2):
                    pe.wait_ge(sem(f"in_we{d}"), 32 * (e // 2 + 1))
                    ps = group("eh", e + d)
                    for f in range(F0C):
                        for k in range(KD):
                            ins = mm(ps[:, f * CAP:(f + 1) * CAP], wiE[d][:, k, f * 128:(f + 1) * 128], einT[:, k, d * CAP:(d + 1) * CAP], k == 0, k == KD - 1)
                    close(ins)
                    emptied(pe, "eh", e + d)
                    for i in range(2):
                        ps = group("eo", e + d, i)
                        for f in range(F0C):
                            ins = mm(ps[0:CAP, 0:HALF], hE[d][:, f, :], woE[d][:, f, i * HALF:(i + 1) * HALF], f == 0, f == F0C - 1)
                        close(ins)

            transposed("x2", sem("x2_rows"))
            all_emptied(pe, "T", "x2", T - 1, 1)
            pe.wait_ge(sem("in_gW"), 16)
            for t in range(T):
                rows("gcnh", t, gW)
            all_emptied(pe, "gcnh", T - 1, 1)
            for t in range(T):
                for i in range(2):
                    ps = group("gcn", t, i)
                    for j in range(T):
                        ins = mm(ps[0:TP, 0:HALF], CT[0:TP, j, t * TP:(t + 1) * TP], gH[0:TP, j, i * HALF:(i + 1) * HALF], j == 0, j == T - 1)
                    close(ins)

            transposed("hn", sem("hn_rows"))
            all_emptied(pe, "T", "hn", T - 1, 1)
            pe.wait_ge(sem("in_wk"), 16)
            pe.wait_ge(sem("in_wv"), 16)
            for t in range(T):
                rows("mk", t, wqv[0])
                rows("mv", t, wqv[1])
            pe.wait_ge(sem("kv_rows"), 1)
            for i in range(2):
                ps = group("kvsum", i)
                close(mm(ps[0:TP, 0:HALF], ones[0:TP, 0:TP], prodsum[0:TP, i * HALF:(i + 1) * HALF], True, True))
            pe.wait_ge(sem("in_wq"), 16)
            for t in range(T):
                rows("mq", t, wq2)
            transposed("on", sem("on_rows"))
            all_emptied(pe, "T", "on", T - 1, 1)
            pe.wait_ge(sem("in_wp"), 16)
            for t in range(T):
                rows("mproj", t, wpr)

            transposed("m1", sem("m1_rows"))
            all_emptied(pe, "T", "m1", T - 1, 1)
            pe.wait_ge(sem("in_wg"), 16)
            ps = group("logits1")
            for t in range(T):
                for k in range(KD):
                    ins = mm(ps[0:TP, t * E1:(t + 1) * E1], RT[:, k, t * TP:(t + 1) * TP], wgE[:, k, :], k == 0, k == KD - 1)
            close(ins)
            pe.wait_ge(sem("gates"), 1)
            ps = group("gateT")
            for t in range(T):
                if t < 4:
                    ins = nc.tensor.transpose(ps[0:E1, t * TP:(t + 1) * TP], L1[0:TP, t, :], ident[0:TP, 0:TP])
            close(ins)
            for t in range(4, T):
                ps6 = PS[6 + (t >= 8)]
                ins = nc.tensor.transpose(ps6[0:E1, (t % 4) * TP:(t % 4 + 1) * TP], L1[0:TP, t, :], ident[0:TP, 0:TP])
            ins.then_inc(sem("gates_turned"), 1)
            for e in range(E1):
                pe.wait_ge(sem(f"in_fe{e % 2}"), 32 * (e // 2 + 1))
                for f in range(F0C):
                    for c, (c0, cn) in enumerate(COLS):
                        ps = group("fh", e, f, c)
                        for k in range(KD):
                            ins = mm(ps[:, 0:cn], w1E[e % 2][:, k, f * 128:(f + 1) * 128], RT[:, k, c0:c0 + cn], k == 0, k == KD - 1)
                        close(ins)
                all_emptied(pe, "fh", e, F0C - 1, 2)
                for t in range(T):
                    for i in range(2):
                        ps = group("fo", e, t, i)
                        for f in range(F0C):
                            ins = mm(ps[0:TP, 0:HALF], hF[:, f, t * TP:(t + 1) * TP], w2E[e % 2][:, f, i * HALF:(i + 1) * HALF], f == 0, f == F0C - 1)
                        close(ins)
            pe.wait_ge(sem("gateT_ready"), 1)
            pe.wait_ge(sem("in_b2E"), 16)
            for t in range(T):
                for i in range(2):
                    ps = group("b2", t, i)
                    close(mm(ps[0:TP, 0:HALF], gateT[:, t * TP:(t + 1) * TP], b2E[:, i * HALF:(i + 1) * HALF], True, True))
            assert nth[0] == len(GROUPS)

        @block.scalar
        def _(act):
            do = Steps(act, own_a)
            A = nc.scalar.activation

            def turned(name):
                for t in range(T):
                    for i in range(2):
                        filled(act, "T", name, t, i)
                        do(A(RT[:, 3 * i:3 * i + 3, t * TP:(t + 1) * TP], bank("T", name, t, i)[:, 0:375].rearrange("p (k n) -> p k n", k=3), ACT.Copy),
                           freed("T", name, t, i))

            def root(at):
                act.wait_ge(sem("variances"), at)
                do(A(rstd[0:TP, :], rstd[0:TP, :], ACT.Sqrt), sem("roots"))

            root(1)
            turned("xn")
            filled(act, "rfT")
            do(A(rfp, bank("rfT").rearrange("p (s m) -> p s m", s=2), ACT.Copy), freed("rfT"))
            act.wait_ge(sem("in_bqk"), 16)
            act.wait_ge(sem("bqk_scaled"), 1)
            for p in range(MH // 2):
                for w, name in enumerate("qk"):
                    for c, (c0, cn) in enumerate(COLS):
                        filled(act, name, p, c)
                        do(A((qT, kT)[w][:, c0:c0 + cn], bank(name, p, c)[:, 0:cn], ACT.Identity, bias=bqk[:, w * 6 + p:w * 6 + p + 1], scale=MD ** -0.5), freed(name, p, c))
                for s in range(2):
                    for m in range(2):
                        for c, (c0, cn) in enumerate(COLS):
                            filled(act, "phiq", p, s, m, c)
                            do(A(PQ[:, s, m, c0:c0 + cn], bank("phiq", p, s, m, c)[:, 0:cn], ACT.Relu), freed("phiq", p, s, m, c))
                for c, (c0, cn) in enumerate(COLS):
                    filled(act, "at", p, c)
                    do(A(ATt[:, p, c0:c0 + cn], bank("at", p, c)[:, 0:cn], ACT.Copy), freed("at", p, c))
            all_emptied(act, "proj", T - 1, 1)
            for w in range(NW):
                act.wait_ge(sem("window_filled"), w + 1)
                do(A(CT[0:TP, :, w * WIN:(w + 1) * WIN], PS[6 + w % 2][0:TP, 0:500].rearrange("p (i t) -> p t i", t=T), ACT.Copy), sem("window_emptied"))
            act.wait_ge(sem("deg_copied"), 1)
            do(A(dinv[0:TP, :], dinv[0:TP, :], ACT.Sqrt), sem("deg_root"))

            def scores(u, col):
                ps = PS[6 + u % 2]
                act.wait_ge(sem("coef_rows"), u + 1)
                if u:
                    act.wait_ge(sem("P_ready"), u)
                for t in range(T):
                    do(A(U[0:TP, t, :], ps[0:TP, IC:2 * IC], ACT.Identity, bias=AS2[0:TP, t, col:col + 1]), sem("lower_lines"))
                act.wait_ge(sem("exponents"), u + 1)
                do(A(U[0:TP, :, :], U[0:TP, :, :], ACT.Exp), sem("exps"))

            act.wait_ge(sem("coef_cols"), 1)
            for h in range(H1):
                if h == 0:
                    scores(0, 0)
                for t in range(T):
                    filled(act, "h1", h, t)
                    do(A(Hh[0:TP, t, :], bank("h1", h, t)[0:TP, :], ACT.Copy), freed("h1", h, t))
                for c in range(NC):
                    u = h * NC + c
                    if u + 1 < H1 * NC:
                        scores(u + 1, (u + 1) // NC)
                    for f in range(FC):
                        n = u * FC + f
                        act.wait_ge(sem("elu_in"), n + 1)
                        do(A(elu_m[:, :], elu_m[:, :], ACT.Exp))
                        do(A(elu_r[:, :], elu_z[:, :], ACT.Relu, bias=b1c[:, h * FC + f:h * FC + f + 1]), sem("elu_parts"))
            act.wait_ge(sem("coef_cols"), 2)
            for c in range(NC):
                scores(H1 * NC + c, 0)
            root(2)
            root(3)
            turned("m0")
            act.wait_ge(sem("shifted0"), 1)
            do(A(G2[0:TP, :, :], G0[0:TP, :, :], ACT.Exp), sem("exp0"))
            for e in range(0, E0, 2):
                for i in range(2):
                    filled(act, "einT", e, i)
                    do(A(einT[:, 3 * i:3 * i + 3, :], bank("einT", e, i)[:, 0:384].rearrange("p (k n) -> p k n", k=3), ACT.Copy), freed("einT", e, i))
                for d in range(2):
                    filled(act, "eh", e + d)
                    do(A(hE[d], bank("eh", e + d)[:, 0:192].rearrange("p (k n) -> p k n", k=3), ACT.Relu), freed("eh", e + d))
            root(4)
            turned("x2")
            for t in range(T):
                for i in range(2):
                    filled(act, "gcnh", t, i)
                    do(A(gH[0:TP, t, i * HALF:(i + 1) * HALF], bank("gcnh", t, i)[0:TP, 0:HALF], ACT.Copy, scale=dinv[0:TP, t:t + 1]), freed("gcnh", t, i))
            root(5)
            turned("hn")
            for t in range(T):
                act.wait_ge(sem("k_sums"), t + 1)
                do(A(small[0:TP, t:t + 1], small[0:TP, t:t + 1], ACT.Sqrt), sem("k_norms"))
            for t in range(T):
                act.wait_ge(sem("q_sums"), t + 1)
                do(A(small[0:TP, 10 + t:11 + t], small[0:TP, 10 + t:11 + t], ACT.Sqrt), sem("q_norms"))
            root(6)
            turned("on")
            root(7)
            turned("m1")
            act.wait_ge(sem("shifted1"), 1)
            do(A(L2[0:TP, :, :], L0[0:TP, :, :], ACT.Exp), sem("exp1"))
            act.wait_ge(sem("in_b1E"), 16 * E1)
            for e in range(E1):
                for f in range(F0C):
                    for c, (c0, cn) in enumerate(COLS):
                        filled(act, "fh", e, f, c)
                        do(A(hF[:, f, c0:c0 + cn], bank("fh", e, f, c)[:, 0:cn], ACT.Silu, bias=b1E[:, e, f:f + 1]), freed("fh", e, f, c))

        @block.gpsimd
        def _(pool):
            do = Steps(pool, own_g)
            g = nc.gpsimd
            do(g.memset(ones, 1.0), sem("consts"))
            do(g.memset(ident, 0.0))
            do.settle()
            do(g.affine_select(out=ident, in_=ident, compare_op=ALU.not_equal, fill=1.0, base=0, pattern=[[-1, 128]], channel_multiplier=1), sem("consts"))
            do(g.memset(upto, 1.0))
            do.settle()
            do(g.affine_select(out=upto, in_=upto, compare_op=ALU.is_ge, fill=0.0, base=0, pattern=[[1, 128]], channel_multiplier=-1), sem("consts"))
            do(g.memset(rfn, 0.0), sem("pads"))
            pool.wait_ge(sem("in_bias"), 32)
            for t in range(T):
                all_emptied(pool, "proj", t, 1)
                do(g.tensor_tensor(R1[0:TP, t, :], R1[0:TP, t, :], bias_rows[0:TP, 0, :], ALU.add))
                do.settle()
                do(g.tensor_tensor(R1[0:TP, t, :], R1[0:TP, t, :], bias_rows[0:TP, 1, :], ALU.add), sem("bias_added"))
            pool.wait_ge(sem("in_edges"), 32)
            do(g.iota(iota_i, [[1, 500]], base=0, channel_multiplier=0), sem("iotas"))
            do(g.iota(iota_c_i, [[0, 1]], base=0, channel_multiplier=WIN), sem("iotas"))
            do(g.memset(upper, 1.0))
            do.settle()
            do(g.affine_select(out=upper, in_=upper, compare_op=ALU.is_ge, fill=0.0, base=-1, pattern=[[1, 32]], channel_multiplier=-1), sem("iotas"))
            do(g.memset(zero_bf, 0.0), sem("iota_set"))

            def sums(u):
                pool.wait_ge(sem("P_ready"), u + 1)
                if u >= 2:
                    v = u - 2
                    filled(pool, *(("den1", v // NC, v % NC) if v < H1 * NC else ("den2", v - H1 * NC)))
                P, S = Pm[u % 2], Sp[u % 2]
                do(g.tensor_tensor(S[0:TP, :], P[0:TP, 0, :], P[0:TP, 1, :], ALU.add))
                for t in range(2, T):
                    do.settle()
                    do(g.tensor_tensor(S[0:TP, :], S[0:TP, :], P[0:TP, t, :], ALU.add), sem("P_sums") if t == T - 1 else None)

            for u in range(H1 * NC):
                sums(u)
            for c in range(NC):
                sums(H1 * NC + c)
            all_emptied(pool, "agg2", T - 1, 1)
            do(g.memset(zero_row, 0.0), sem("zeros_set"))
            do(g.iota(e_i, [[0, T], [-1, E0]], base=E0, channel_multiplier=0), sem("iotas"))
            for t in range(T):
                pool.wait_ge(sem("y_rows"), t + 1)
                do(g.tensor_tensor(R1[0:TP, t, :], R1[0:TP, t, :], R2[0:TP, t, :], ALU.add), sem("y_added"))
            pool.wait_ge(sem("slots"), 1)
            pool.wait_ge(sem("slots_zeroed"), 16 * (SLOTS // 128))
            for t in range(T):
                g.indirect_dma_start(scr_in, bass.IndirectOffsetOnAxis(ap=slot_s[0:TP, t:t + 1], axis=0), R2[0:TP, t, :], None,
                                     bounds_check=SLOTS - 1, oob_is_err=False).then_inc(sem("scattered"), 16)
            for e in range(E0):
                for i in range(2):
                    emptied(pool, "eo", e, i)
                pool.dma_start(scr_out[e * CAP:(e + 1) * CAP, :], oE[e % 2][0:CAP, :]).then_inc(sem(f"out_kept{e % 2}"), 16)
            pool.wait_ge(sem("out_kept0"), 16 * E0 // 2)
            pool.wait_ge(sem("out_kept1"), 16 * E0 // 2)
            filled(pool, "eo", E0 - 1, 1)
            for t in range(T):
                if t >= 2:
                    pool.wait_ge(sem("gathered_used"), t - 1)
                g.indirect_dma_start(gath[t % 2][0:TP, :], None, scr_out, bass.IndirectOffsetOnAxis(ap=slot_g[0:TP, t:t + 1], axis=0),
                                     bounds_check=SLOTS - 1, oob_is_err=False).then_inc(sem(f"gathered{t % 2}"), 16)
            all_emptied(pool, "mproj", T - 1, 1)
            do(g.iota(WK[:, 4040:4120].bitcast(I32), [[0, T], [-1, E1]], base=E1, channel_multiplier=0), sem("iotas"))

        @block.vector
        def _(v):
            do = Steps(v, own_v)
            V = nc.vector

            def norm_rows(source, at, eps, rows_sem, rms=False, scale_row=None, ready=None, extra=None):
                for t in range(T):
                    if ready:
                        ready(t)
                    for i in range(2):
                        do(V.bn_stats(stat[0:TP, t, 6 * i:6 * i + 6], source[0:TP, t, i * HALF:(i + 1) * HALF]))
                    do.settle()
                    do(V.bn_aggr(mv[0:TP, t, :], stat[0:TP, t, :]))
                do.settle()
                if rms:
                    do(V.tensor_tensor(rstd[0:TP, :], mv[0:TP, :, 0], mv[0:TP, :, 0], ALU.mult))
                    do.settle()
                    do(V.tensor_tensor(rstd[0:TP, :], rstd[0:TP, :], mv[0:TP, :, 1], ALU.add))
                    do.settle()
                    do(V.tensor_scalar(rstd[0:TP, :], rstd[0:TP, :], eps, None, ALU.add), sem("variances"))
                else:
                    do(V.tensor_scalar(rstd[0:TP, :], mv[0:TP, :, 1], eps, None, ALU.add), sem("variances"))
                v.wait_ge(sem("roots"), at)
                do(V.reciprocal(rstd[0:TP, :], rstd[0:TP, :]))
                do.settle()
                for t in range(T):
                    if rms:
                        v.wait_ge(sem("y_added"), t + 1)
                        do(V.scalar_tensor_tensor(R2[0:TP, t, :], R2[0:TP, t, :], rstd[0:TP, t:t + 1], scale_row, ALU.mult, ALU.mult), rows_sem)
                    elif extra:
                        do(V.tensor_scalar(R2[0:TP, t, :], source[0:TP, t, :], mv[0:TP, t, 0:1], rstd[0:TP, t:t + 1], ALU.subtract, ALU.mult))
                        do.settle()
                        do(V.tensor_tensor(R2[0:TP, t, :], R2[0:TP, t, :], extra[0:TP, 0, :], ALU.mult))
                        do.settle()
                        do(V.tensor_tensor(R2[0:TP, t, :], R2[0:TP, t, :], extra[0:TP, 1, :], ALU.add), rows_sem)
                    else:
                        do(V.tensor_scalar(R2[0:TP, t, :], source[0:TP, t, :], mv[0:TP, t, 0:1], rstd[0:TP, t:t + 1], ALU.subtract, ALU.mult), rows_sem)

            do(V.memset(kvpad, 0.0), sem("kv_zero"))
            v.wait_ge(sem("in_x"), 16 * T)
            norm_rows(R1, 1, 1e-5, sem("xn_rows"))
            v.wait_ge(sem("in_bqk"), 16)
            do(V.tensor_scalar(bqk, bqk, MD ** -0.5, None, ALU.mult), sem("bqk_scaled"))
            v.wait_ge(sem("in_bv"), 16)
            filled(v, "T", "xn", T - 1, 1)
            for t in range(T):
                for i in range(2):
                    filled(v, "v", t, i)
                    do(V.tensor_tensor(R2[0:TP, t, i * HALF:(i + 1) * HALF], bank("v", t, i)[0:TP, 0:HALF], bv_row[0:TP, i * HALF:(i + 1) * HALF], ALU.add), freed("v", t, i))
            do.settle()
            for p in range(MH // 2):
                for s in range(2):
                    for i in range(T // 2):
                        filled(v, "phik", p, s, i)
                        do(V.tensor_scalar(PK[0:TP, s, 2 * i:2 * i + 2, :], bank("phik", p, s, i)[0:TP, :].rearrange("p (t m) -> p t m", t=2), 0.0, None, ALU.max), freed("phik", p, s, i))
                for s in range(2):
                    filled(v, "kv", p, s)
                    do(V.tensor_scalar(kvpad[:, s, :, s * MD:(s + 1) * MD], bank("kv", p, s)[:, 0:128].rearrange("p (m d) -> p m d", m=2), 1.0 / MM, None, ALU.mult), freed("kv", p, s))
            for t in range(T):
                for i in range(2):
                    filled(v, "proj", t, i)
                    do(V.tensor_tensor(R1[0:TP, t, i * HALF:(i + 1) * HALF], R1[0:TP, t, i * HALF:(i + 1) * HALF], bank("proj", t, i)[0:TP, 0:HALF], ALU.add), freed("proj", t, i))

            v.wait_ge(sem("bias_added"), T)
            v.wait_ge(sem("in_edges"), 32)
            do(V.tensor_copy(nat, nat_i))
            do.settle()
            do(V.tensor_scalar(tdiv, nat[:, 0, :], float(TP), None, ALU.is_ge))
            for m in range(2, T):
                do.settle()
                do(V.scalar_tensor_tensor(tdiv, nat[:, 0, :], float(TP * m), tdiv, ALU.is_ge, ALU.add))
            do.settle()
            do(V.scalar_tensor_tensor(keys[:, 0, :], nat[:, 1, :], float(T), tdiv, ALU.mult, ALU.add))
            do(V.scalar_tensor_tensor(keys[:, 1, :], tdiv, -float(TP), nat[:, 0, :], ALU.mult, ALU.add))
            do(V.tensor_reduce(gmm[:, 0:1], nat[:, 1, :], AX, ALU.min))
            do(V.tensor_reduce(gmm[:, 1:2], nat[:, 1, :], AX, ALU.max), sem("edge_keys"))
            v.wait_ge(sem("iotas"), 3)
            do(V.tensor_copy(iota, iota_i))
            do(V.tensor_copy(iota_c[:, 0:1], iota_c_i))
            for a in range(2):
                filled(v, "edgeT", a)
                do(V.tensor_copy(KL[0:TP, a, :, :], bank("edgeT", a)[0:TP, 0:320].rearrange("p (q g) -> p q g", q=QG)), freed("edgeT", a))
            do.settle()
            do(V.tensor_scalar(iota_c[:, 1:2], iota_c[:, 0:1], float(WIN), None, ALU.add))
            filled(v, "groupB")
            do.settle()
            ps = bank("groupB")
            do(V.tensor_scalar(cutI, ps[0:NW, 0:NG], iota_c[0:NW, 1:2], None, ALU.is_lt))
            do.settle()
            do(V.scalar_tensor_tensor(cutI, ps[0:NW, NG:2 * NG], iota_c[0:NW, 0:1], cutI, ALU.is_ge, ALU.mult), freed("groupB"))
            do(V.tensor_scalar(cutJ, iota[0:NW, 0:NG], -1.0, float(NG - 1), ALU.mult, ALU.add))
            do.settle()
            do(V.tensor_tensor(cutJ, cutJ, cutI, ALU.mult))
            do(V.scalar_tensor_tensor(cutK, iota[0:NW, 0:NG], 1.0, cutI, ALU.add, ALU.mult))
            do.settle()
            do(V.tensor_reduce(tab[:, 3:4], cutJ, AX, ALU.max))
            do(V.tensor_reduce(tab[:, 4:5], cutK, AX, ALU.max))
            do.settle()
            do(V.tensor_scalar(tab[:, 0:1], tab[:, 3:4], -1.0, float(NG - 1), ALU.mult, ALU.add))
            do.settle()
            do(V.scalar_tensor_tensor(tab[:, 1:2], tab[:, 0:1], 1.0, tab[:, 4:5], ALU.add, ALU.max))
            do.settle()
            do(V.tensor_tensor(tab[:, 2:3], tab[:, 1:2], tab[:, 0:1], ALU.subtract), sem("window_cols"))
            filled(v, "tables")
            ps = bank("tables")
            do(V.tensor_copy(trow_i[:, 0:2 * NW], ps[0:1, 0:2 * NW]))
            do(V.tensor_scalar(trow[:, 0:NW], ps[0:1, 0:NW], -2.0, float(BIAS), ALU.mult, ALU.add))
            do.settle()
            do(V.scalar_tensor_tensor(trow_i[:, 2 * NW:3 * NW], ps[0:1, 2 * NW:3 * NW], 2.0, trow[:, 0:NW], ALU.mult, ALU.add), freed("tables"))
            do.settle()
            do(V.tensor_copy(tab[0:1, 5:6], tab[0:1, 4:5]), sem("window_table"))
            v.sem_inc(sem("onehots_ready"), BIAS)
            for w in range(NW):
                g0 = v.value_load(trow_i[0:1, w:w + 1], min_val=0, max_val=NG - 1)
                g1 = v.value_load(trow_i[0:1, NW + w:NW + w + 1], min_val=1, max_val=NG)
                base = v.value_load(trow_i[0:1, 2 * NW + w:2 * NW + w + 1], min_val=0, max_val=2 * NG * NW + BIAS)
                if w:
                    do(V.tensor_copy(tab[0:1, 5:6], tab[0:1, 4:5]))
                    do.settle()
                    do(V.tensor_scalar(KL[0:TP, 0, :, :], KL[0:TP, 0, :, :], -float(WIN * T), None, ALU.add))
                do.settle()
                with v.Fori(g0, g1) as g:
                    for half in range(2):
                        v.wait_ge(sem("onehots_used"), base + g * 2 + (half + 1))
                        for q in range(2 * half, 2 * half + 2):
                            V.tensor_scalar(oh_lo[q][0:TP, 0:TP], iota[0:TP, 0:TP], KL[0:TP, 1, q, bass.ds(g, 1)], None, ALU.is_equal)
                            ins = V.tensor_scalar(oh_key[q][0:TP, 0:500], iota[0:TP, 0:500], KL[0:TP, 0, q, bass.ds(g, 1)], None, ALU.is_equal)
                        ins.then_inc(sem("onehots_ready"), 1)
            v.wait_ge(sem("window_emptied"), NW)
            for t in range(T):
                do(V.tensor_tensor(CT[0:TP, t, t * TP:(t + 1) * TP], CT[0:TP, t, t * TP:(t + 1) * TP], ident[0:TP, 0:TP], ALU.add))
            do.settle()
            do(V.tensor_reduce(degp[0:TP, :], CT[0:TP, :, :].rearrange("p t n -> p n t"), AX, ALU.add), sem("deg_parts"))
            filled(v, "deg")
            do(V.tensor_copy(dinv[0:TP, :], bank("deg")[0:TP, 0:T]), sem("deg_copied"))
            v.wait_ge(sem("deg_root"), 1)
            do(V.reciprocal(dinv[0:TP, :], dinv[0:TP, :]), freed("deg"))

            v.wait_ge(sem("in_a1"), 32)
            for h in range(H1):
                v.wait_ge(sem(f"in_W1s{h % 2}"), 16 * (h // 2 + 1))
                for k in range(KD):
                    for a in range(2):
                        if k + a or h:
                            do.settle()
                        do(V.tensor_tensor_reduce(junk[:, 0:HID], W1s[h % 2][:, k, :], arow[:, a, h * HID:(h + 1) * HID], 1.0, 0.0,
                                                  ALU.mult, ALU.add, wa[:, k, 4 * a + h:4 * a + h + 1]), sem("W1_folded") if k == KD - 1 and a else None)
            filled(v, "coef1")
            do(V.tensor_copy(AS[0:TP, :, :], bank("coef1")[0:TP, 0:80].rearrange("p (t n) -> p t n", t=T)))
            do(V.tensor_scalar(AS2[0:TP, :, :], bank("coef1")[0:TP, 0:80].rearrange("p (t n) -> p t n", t=T), 0.2, None, ALU.mult), freed("coef1"))
            do.settle()

            def neighbour_max(acc, mask, cols):
                for t in range(T):
                    do(V.tensor_scalar(mask[0:TP, :], CT[0:TP, t, :], 0.0, -BIG, ALU.is_equal, ALU.mult))
                    do.settle()
                    for a, col in zip(acc, cols):
                        if t == 0:
                            do(V.tensor_scalar(a[0:TP, :], mask[0:TP, :], AS[0:TP, t, col:col + 1], None, ALU.add))
                        else:
                            do(V.scalar_tensor_tensor(a[0:TP, :], mask[0:TP, :], AS[0:TP, t, col:col + 1], a[0:TP, :], ALU.add, ALU.max))
                    do.settle()

            def coef_columns(h, key, dcol):
                for i in range(3):
                    filled(v, *key, i)
                    n = min(4, T - 4 * i)
                    do(V.tensor_reduce(Mx[0:TP, h, 4 * i:4 * i + n], bank(*key, i)[0:TP, 0:n * TP].rearrange("p (t n) -> p t n", t=n), AX, ALU.max), freed(*key, i))
                do.settle()
                do(V.tensor_tensor(Mx[0:TP, h, :], Mx[0:TP, h, :], AS[0:TP, :, dcol], ALU.add))
                do.settle()
                do(V.scalar_tensor_tensor(Mx[0:TP, h, :], Mx[0:TP, h, :], 0.2, Mx[0:TP, h, :], ALU.mult, ALU.max))
                do.settle()
                do(V.tensor_tensor(Ac[0:TP, h, :], AS[0:TP, :, dcol], Mx[0:TP, h, :], ALU.subtract))
                return do(V.tensor_tensor(Bc[0:TP, h, :], AS2[0:TP, :, dcol], Mx[0:TP, h, :], ALU.subtract))

            neighbour_max([maxacc[:, h, :] for h in range(H1)], maskt, range(H1))
            do(V.tensor_copy(small[0:TP, 0:1], AS[0:TP, 0, 0:1]), sem("max_rows"))
            for h in range(H1):
                coef_columns(h, ("max1", h), 4 + h)
            do.settle()
            do(V.tensor_copy(small[0:TP, 0:1], AS[0:TP, 0, 0:1]), sem("coef_cols"))

            def weights(u, col):
                ps = PS[6 + u % 2]
                v.wait_ge(sem("lower_lines"), (u + 1) * T)
                for t in range(T):
                    s = sem("exponents") if t == T - 1 else None
                    do(V.scalar_tensor_tensor(U[0:TP, t, :], ps[0:TP, 0:IC], AS[0:TP, t, col:col + 1], U[0:TP, t, :], ALU.add, ALU.max), s)
                do(V.tensor_copy(small[0:TP, 1:2], small[0:TP, 0:1]), sem("coef_used"))
                v.wait_ge(sem("exps"), u + 1)
                if u >= 2:
                    w = u - 2
                    filled(v, *(("agg1", w // NC, w % NC, FC - 1) if w < H1 * NC else ("agg2", (w - H1 * NC) * TC + TC - 1, 1)))
                    v.wait_ge(sem("P_sums"), w + 1)
                P = Pm[u % 2]
                c = u % NC
                do(V.scalar_tensor_tensor(P[0:TP, :, :], U[0:TP, :, :], 1.0, CT[0:TP, :, c * IC:(c + 1) * IC], ALU.min, ALU.mult), sem("P_ready"))

            def elu(h, c, f):
                u = h * NC + c
                n = u * FC + f
                filled(v, "agg1", h, c, f)
                if n:
                    v.wait_ge(sem("elu_parts"), n)
                do(V.tensor_tensor(elu_z[:, :], bank("agg1", h, c, f)[:, 0:IC], rden[u % 2][:, :], ALU.mult), freed("agg1", h, c, f))
                do.settle()
                do(V.tensor_scalar(elu_m[:, :], elu_z[:, :], b1c[:, h * FC + f:h * FC + f + 1], 0.0, ALU.add, ALU.min), sem("elu_in"))
                v.wait_ge(sem("elu_parts"), n + 1)
                do(V.scalar_tensor_tensor(H1T[u % 2][:, f, :], elu_m[:, :], -1.0, elu_r[:, :], ALU.add, ALU.add), sem("elu_done"))
                do.settle()

            def w2_rows(h, c):
                for t in range(c * TC, (c + 1) * TC):
                    for i in range(2):
                        filled(v, "w2", h, t, i)
                        o, ps = R2[0:TP, t, i * HALF:(i + 1) * HALF], bank("w2", h, t, i)[0:TP, 0:HALF]
                        if h == 0:
                            do(V.tensor_copy(o, ps), freed("w2", h, t, i))
                        else:
                            do(V.tensor_tensor(o, o, ps, ALU.add), freed("w2", h, t, i))

            v.wait_ge(sem("in_b1"), 16)
            weights(0, 0)
            for h in range(H1):
                for c in range(NC):
                    u = h * NC + c
                    if u + 1 < H1 * NC:
                        weights(u + 1, (u + 1) // NC)
                    filled(v, "den1", h, c)
                    do(V.tensor_scalar(rden[u % 2][:, :], bank("den1", h, c)[:, 0:IC], 1e-16, None, ALU.add), freed("den1", h, c))
                    do.settle()
                    do(V.reciprocal(rden[u % 2][:, :], rden[u % 2][:, :]))
                    do.settle()
                    for f in range(FC):
                        elu(h, c, f)
                    if c:
                        w2_rows(h, c - 1)
                w2_rows(h, NC - 1)

            v.wait_ge(sem("in_a2"), 32)
            for t in range(T):
                for a in range(2):
                    do.settle()
                    do(V.tensor_tensor_reduce(junk2[0:TP, :], R2[0:TP, t, :], a2row[0:TP, a, :], 1.0, 0.0, ALU.mult, ALU.add, AS[0:TP, t, 4 * a:4 * a + 1]))
            do.settle()
            do(V.tensor_scalar(AS2[0:TP, :, :], AS[0:TP, :, :], 0.2, None, ALU.mult))
            do.settle()
            neighbour_max([max2a], mask2, [0])
            do(V.tensor_copy(small[0:TP, 0:1], AS[0:TP, 0, 0:1]), sem("max_rows"))
            coef_columns(0, ("max2",), 4)
            do.settle()
            do(V.tensor_copy(small[0:TP, 0:1], AS[0:TP, 0, 0:1]), sem("coef_cols"))
            v.wait_ge(sem("xm_back"), 16)
            weights(H1 * NC, 0)
            for c in range(NC):
                if c + 1 < NC:
                    weights(H1 * NC + c + 1, 0)
                filled(v, "den2", c)
                do(V.tensor_scalar(rd2[0:TP, :], bank("den2", c)[0:TP, 0:TC], 1e-16, None, ALU.add), freed("den2", c))
                do.settle()
                do(V.reciprocal(rd2[0:TP, :], rd2[0:TP, :]))
                do.settle()
                for t in range(TC):
                    for i in range(2):
                        tt = c * TC + t
                        filled(v, "agg2", tt, i)
                        o = R1[0:TP, tt, i * HALF:(i + 1) * HALF]
                        do(V.scalar_tensor_tensor(o, bank("agg2", tt, i)[0:TP, 0:HALF], rd2[0:TP, t:t + 1], o, ALU.mult, ALU.add), freed("agg2", tt, i))
                do.settle()

            norm_rows(R1, 2, 1e-5, sem("y_rows"))
            do.settle()
            v.wait_ge(sem("in_lnw"), 16)
            norm_rows(R2, 3, 1e-6, sem("normed_rows"), rms=True, scale_row=lnw_row[0:TP, :])
            filled(v, "logits0")
            lg = bank("logits0")[0:TP, 0:160].rearrange("p (t e) -> p t e", t=T)

            def wide(col, n):
                return col.unsqueeze(2).to_broadcast([TP, T, n])

            g0, g1_, g2, g3 = (a[0:TP] for a in (G0, G1, G2, G3))
            eb, es, gc = ebase[0:TP], esort[0:TP], gcol[0:TP]
            do(V.tensor_copy(g3, lg), freed("logits0"))
            do.settle()
            do(V.tensor_reduce(gc[:, 0, :], g3, AX, ALU.max))
            v.wait_ge(sem("iotas"), 4)
            do(V.tensor_copy(es, e_i[0:TP].rearrange("p (t e) -> p t e", t=T)))
            do.settle()
            do(V.tensor_tensor(g0, g3, wide(gc[:, 0, :], E0), ALU.subtract), sem("shifted0"))
            do(V.tensor_scalar(eb, es, -float(CAP), float(CAP * E0), ALU.mult, ALU.add))
            do(V.tensor_tensor(g1_, g3, wide(gc[:, 0, :], E0), ALU.is_equal))
            do.settle()
            do(V.tensor_tensor(g1_, g1_, es, ALU.mult))
            do.settle()
            do(V.tensor_reduce(gc[:, 1, :], g1_, AX, ALU.max))
            do.settle()
            do(V.tensor_tensor(g1_, es, wide(gc[:, 1, :], E0), ALU.is_equal), sem("onehot0"))
            v.wait_ge(sem("exp0"), 1)
            do(V.tensor_reduce(gc[:, 2, :], g2, AX, ALU.add))
            do.settle()
            do(V.reciprocal(gc[:, 3, :], gc[:, 2, :]))
            filled(v, "order0")
            ps = bank("order0")
            do(V.memset(g0[:, 0, :], 0.0))
            for t in range(1, T):
                do.settle()
                do(V.tensor_tensor(g0[:, t, :], g0[:, t - 1, :], ps[0:TP, 160 + (t - 1) * E0:160 + t * E0], ALU.add))
            do.settle()
            do(V.tensor_tensor(g3, g0, ps[0:TP, 0:160].rearrange("p (t e) -> p t e", t=T), ALU.add), freed("order0"))
            do.settle()
            do(V.tensor_tensor(g3, g3, g1_, ALU.mult))
            do(V.tensor_tensor(g2, eb, g1_, ALU.mult))
            do.settle()
            do(V.tensor_reduce(gc[:, 4, :], g3, AX, ALU.add))
            do(V.tensor_reduce(gc[:, 5, :], g2, AX, ALU.add))
            do.settle()
            do(V.tensor_scalar(gc[:, 6, :], gc[:, 4, :], float(CAP), None, ALU.is_le))
            do(V.scalar_tensor_tensor(gc[:, 7, :], gc[:, 4, :], -1.0, gc[:, 5, :], ALU.add, ALU.add))
            do.settle()
            do(V.tensor_scalar(gc[:, 8, :], gc[:, 6, :], -1.0, 1.0, ALU.mult, ALU.add))
            do(V.tensor_tensor(gc[:, 9, :], gc[:, 7, :], gc[:, 6, :], ALU.mult))
            do(V.tensor_tensor(gc[:, 10, :], gc[:, 6, :], gc[:, 3, :], ALU.mult))
            do.settle()
            do(V.scalar_tensor_tensor(gc[:, 7, :], gc[:, 8, :], float(4 * SLOTS), gc[:, 9, :], ALU.mult, ALU.add))
            do(V.tensor_tensor(gc[:, 11, :], gc[:, 8, :], gc[:, 3, :], ALU.mult))
            do.settle()
            do(V.tensor_copy(slot_g[0:TP, :], gc[:, 9, :]))
            do(V.tensor_copy(slot_s[0:TP, :], gc[:, 7, :]), sem("slots"))
            v.wait_ge(sem("scattered"), 16 * T)
            for t in range(T):
                do(V.scalar_tensor_tensor(R1[0:TP, t, :], R2[0:TP, t, :], gc[:, 11, t:t + 1], R1[0:TP, t, :], ALU.mult, ALU.add))
            for e in range(E0):
                if e >= 2:
                    v.wait_ge(sem(f"out_kept{e % 2}"), 16 * (e // 2))
                for i in range(2):
                    filled(v, "eo", e, i)
                    do(V.tensor_copy(oE[e % 2][0:CAP, i * HALF:(i + 1) * HALF], bank("eo", e, i)[0:CAP, 0:HALF]), freed("eo", e, i))
            do.settle()
            for t in range(T):
                v.wait_ge(sem(f"gathered{t % 2}"), 16 * (t // 2 + 1))
                do(V.scalar_tensor_tensor(R1[0:TP, t, :], gath[t % 2][0:TP, :], gc[:, 10, t:t + 1], R1[0:TP, t, :], ALU.mult, ALU.add), sem("gathered_used"))
            do.settle()
            do(V.tensor_copy(small[0:TP, 0:1], small[0:TP, 1:2]), sem("switch_done"))

            norm_rows(R1, 4, 1e-5, sem("x2_rows"))
            v.wait_ge(sem("in_gb"), 16)
            for t in range(T):
                do(V.tensor_tensor(R1[0:TP, t, :], R1[0:TP, t, :], grow[0:TP, :], ALU.add))
            do.settle()
            for t in range(T):
                for i in range(2):
                    filled(v, "gcn", t, i)
                    o = R1[0:TP, t, i * HALF:(i + 1) * HALF]
                    do(V.scalar_tensor_tensor(o, bank("gcn", t, i)[0:TP, 0:HALF], dinv[0:TP, t:t + 1], o, ALU.mult, ALU.add), freed("gcn", t, i))

            v.wait_ge(sem("in_ln"), 32)
            norm_rows(R2, 5, 1e-5, sem("hn_rows"), extra=grow2)
            for t in range(T):
                kk = kt_[0]
                for i in range(2):
                    filled(v, "mk", t, i)
                    do(V.tensor_copy(kk[0:TP, i * HALF:(i + 1) * HALF], bank("mk", t, i)[0:TP, 0:HALF]), freed("mk", t, i))
                do.settle()
                do(V.tensor_tensor_reduce(sq_[0:TP, :], kk[0:TP, :], kk[0:TP, :], 1.0, 0.0, ALU.mult, ALU.add, small[0:TP, t:t + 1]), sem("k_sums"))
                v.wait_ge(sem("k_norms"), t + 1)
                do(V.tensor_scalar(small[0:TP, t:t + 1], small[0:TP, t:t + 1], 1e-12, None, ALU.max))
                do.settle()
                do(V.reciprocal(small[0:TP, t:t + 1], small[0:TP, t:t + 1]))
                do.settle()
                for i in range(2):
                    filled(v, "mv", t, i)
                    o = prodsum if t == 0 else psum_row
                    do(V.scalar_tensor_tensor(o[0:TP, i * HALF:(i + 1) * HALF], kk[0:TP, i * HALF:(i + 1) * HALF], small[0:TP, t:t + 1],
                                              bank("mv", t, i)[0:TP, 0:HALF], ALU.mult, ALU.mult), freed("mv", t, i))
                do.settle()
                if t:
                    do(V.tensor_tensor(prodsum[0:TP, :], prodsum[0:TP, :], psum_row[0:TP, :], ALU.add), sem("kv_rows") if t == T - 1 else None)
                    do.settle()
            for i in range(2):
                filled(v, "kvsum", i)
                do(V.tensor_copy(kvb[0:TP, i * HALF:(i + 1) * HALF], bank("kvsum", i)[0:TP, 0:HALF]), freed("kvsum", i))
            do.settle()
            filled(v, "T", "hn", T - 1, 1)
            for t in range(T):
                qq = kt_[1]
                for i in range(2):
                    filled(v, "mq", t, i)
                    do(V.tensor_copy(qq[0:TP, i * HALF:(i + 1) * HALF], bank("mq", t, i)[0:TP, 0:HALF]), freed("mq", t, i))
                do.settle()
                do(V.tensor_tensor_reduce(sq_[0:TP, :], qq[0:TP, :], qq[0:TP, :], 1.0, 0.0, ALU.mult, ALU.add, small[0:TP, 10 + t:11 + t]), sem("q_sums"))
                v.wait_ge(sem("q_norms"), t + 1)
                do(V.tensor_scalar(small[0:TP, 10 + t:11 + t], small[0:TP, 10 + t:11 + t], 1e-12, None, ALU.max))
                do.settle()
                do(V.reciprocal(small[0:TP, 10 + t:11 + t], small[0:TP, 10 + t:11 + t]))
                do.settle()
                do(V.scalar_tensor_tensor(R2[0:TP, t, :], qq[0:TP, :], small[0:TP, 10 + t:11 + t], kvb[0:TP, :], ALU.mult, ALU.mult))
                do.settle()
            v.wait_ge(sem("in_ln"), 64)
            norm_rows(R2, 6, 1e-5, sem("on_rows"), extra=grow2)
            for t in range(T):
                for i in range(2):
                    filled(v, "mproj", t, i)
                    o = R1[0:TP, t, i * HALF:(i + 1) * HALF]
                    do(V.tensor_tensor(o, o, bank("mproj", t, i)[0:TP, 0:HALF], ALU.add), freed("mproj", t, i))
            do.settle()

            norm_rows(R1, 7, 1e-5, sem("m1_rows"))
            filled(v, "logits1")
            l0, l1, l2, e1_, lc = L0[0:TP], L1[0:TP], L2[0:TP], esort1[0:TP], lcol[0:TP]
            do(V.tensor_copy(l1, bank("logits1")[0:TP, 0:80].rearrange("p (t e) -> p t e", t=T)), freed("logits1"))
            do.settle()
            do(V.tensor_reduce(lc[:, 0, :], l1, AX, ALU.max))
            v.wait_ge(sem("iotas"), 5)
            do(V.tensor_copy(e1_, WK[0:TP, 4040:4120].bitcast(I32).rearrange("p (t e) -> p t e", t=T)))
            do.settle()
            do(V.tensor_tensor(l0, l1, wide(lc[:, 0, :], E1), ALU.subtract), sem("shifted1"))
            do(V.tensor_tensor(l1, l1, wide(lc[:, 0, :], E1), ALU.is_equal))
            do.settle()
            do(V.tensor_tensor(l1, l1, e1_, ALU.mult))
            do.settle()
            do(V.tensor_reduce(lc[:, 1, :], l1, AX, ALU.max))
            do.settle()
            v.wait_ge(sem("exp1"), 1)
            do(V.tensor_tensor(l1, e1_, wide(lc[:, 1, :], E1), ALU.is_equal))
            do(V.tensor_reduce(lc[:, 2, :], l2, AX, ALU.add))
            do.settle()
            do(V.reciprocal(lc[:, 3, :], lc[:, 2, :]))
            do.settle()
            do(V.tensor_tensor(l1, l1, wide(lc[:, 3, :], E1), ALU.mult), sem("gates"))
            filled(v, "gateT")
            do(V.tensor_copy(gateT[:, 0:500], bank("gateT")[0:E1, 0:500]), freed("gateT"))
            v.wait_ge(sem("gates_turned"), 1)
            do(V.tensor_copy(gateT[:, 500:1000], PS[6][0:E1, 0:500]))
            do(V.tensor_copy(gateT[:, 1000:1250], PS[7][0:E1, 0:250]), sem("gateT_ready"))
            do.settle()
            for e in range(E1):
                for t in range(T):
                    for i in range(2):
                        filled(v, "fo", e, t, i)
                        o = R1[0:TP, t, i * HALF:(i + 1) * HALF]
                        do(V.scalar_tensor_tensor(o, bank("fo", e, t, i)[0:TP, 0:HALF], l1[:, t, e:e + 1], o, ALU.mult, ALU.add), freed("fo", e, t, i))
                do.settle()
            for t in range(T):
                for i in range(2):
                    filled(v, "b2", t, i)
                    o = R1[0:TP, t, i * HALF:(i + 1) * HALF]
                    do(V.tensor_tensor(o, o, bank("b2", t, i)[0:TP, 0:HALF], ALU.add), freed("b2", t, i))


_INS = ["x", "src", "dst", "L0_gnn_W1", "L0_gnn_a1_src", "L0_gnn_a1_dst", "L0_gnn_b1", "L0_gnn_W2", "L0_gnn_a2_src",
        "L0_gnn_a2_dst", "L0_gnn_b2", "L0_mix_W_qkv", "L0_mix_b_qkv", "L0_mix_W_proj", "L0_mix_b_proj",
        "L0_mix_random_features", "L0_ffn_ln_w", "L0_ffn_w_router", "L0_ffn_wi", "L0_ffn_wo", "L1_gnn_W", "L1_gnn_b",
        "L1_mix_w_qkv", "L1_mix_w_proj", "L1_mix_ln_in_g", "L1_mix_ln_in_b", "L1_mix_ln_out_g", "L1_mix_ln_out_b",
        "L1_ffn_Wg", "L1_ffn_W1", "L1_ffn_b1", "L1_ffn_W2", "L1_ffn_b2"]


def kernel(**inputs):
    import numpy as _np
    import concourse.bacc as _bacc
    from concourse import mybir as _mybir
    from concourse.bass_utils import run_bass_kernel_spmd as _run

    nc = _bacc.Bacc("TRN2", target_bir_lowering=False, num_devices=1)
    arrays, args = {}, []
    for name in _INS:
        a = _np.ascontiguousarray(inputs[name])
        arrays[f"in_{name}_dram"] = a
        args.append(nc.dram_tensor(f"in_{name}_dram", a.shape, _mybir.dt.from_np(a.dtype), kind="ExternalInput").ap())
    args.append(nc.dram_tensor("out_0_dram", (1250, 768), _mybir.dt.float32, kind="ExternalOutput").ap())
    build(nc, *args)
    r = _run(nc, [arrays], core_ids=[0])
    return r.results[0]["out_0_dram"]
```

```python
from contextlib import ExitStack

import concourse.bass as bass
from concourse import mybir

F32 = mybir.dt.float32
F16 = mybir.dt.float16
I32 = mybir.dt.int32
ALU = mybir.AluOpType
ACT = mybir.ActivationFunctionType
AX = mybir.AxisListType.X


N = 1250
TP = 125
T = N // TP
D = 768
KD = D // 128
HALF = D // 2
NE = 40000
GE = 500
NG = NE // GE
QG = GE // TP
WIN = 50
NW = N // WIN
BIAS = 2 * NG
H1, HID = 4, 512
FC = HID // 128
IC = 250
NC = N // IC
TC = IC // TP
MH, MD, MM = 12, 64, 256
KV_SCALE = MD ** -0.5 * MD ** -0.5 / MM
COLS = ((0, 500), (500, 500), (1000, 250))
E0, F0, CAP = 16, 384, 64
E1, F1 = 8, 384
BLK = 128
MINB = -(-N // BLK)
MAXB = E1 + (N - E1) // BLK
F0C = F0 // 128
SLOTS = E0 * CAP
BANKS = 6
BIG = 1.0e30


def pe_groups():
    def transposed(name):
        return [("T", name, t, i) for t in range(T) for i in range(2)]

    def rows(name):
        return [(name, t, i) for t in range(T) for i in range(2)]

    g = transposed("xn")
    g += rows("v") + [("rfT",)]
    for p in range(MH // 2):
        g += [("q", p, c) for c in range(3)] + [("k", p, c) for c in range(3)]
        for s in range(2):
            g += [("phiq", p, s, m, c) for m in range(2) for c in range(3)]
            g += [("phik", p, s, i) for i in range(T // 2)]
        g += [("kv", p, s) for s in range(2)]
        g += [("at", p, c) for c in range(3)]
    g += rows("proj")
    g += [("edgeT", 0), ("edgeT", 1), ("groupB",), ("tables",)]
    g += [("deg",), ("coef1",)]
    g += [("max1", h, i) for h in range(H1) for i in range(3)]
    for h in range(H1):
        g += [("h1", h, t) for t in range(T)]
        for c in range(NC):
            g += [("den1", h, c)] + [("agg1", h, c, f) for f in range(FC)]
            if c:
                g += [("w2", h, (c - 1) * TC + t, i) for t in range(TC) for i in range(2)]
        g += [("w2", h, (NC - 1) * TC + t, i) for t in range(TC) for i in range(2)]
    g += [("max2", i) for i in range(3)]
    for c in range(NC):
        g += [("den2", c)] + [("agg2", c * TC + t, i) for t in range(TC) for i in range(2)]
    g += transposed("m0")
    g += [("logits0",), ("order0",)]
    for e in range(0, E0, 2):
        g += [("einT", e, i) for i in range(2)]
        for d in range(2):
            g += [("eh", e + d)] + [("eo", e + d, i) for i in range(2)]
    g += transposed("x2")
    g += rows("gcnh") + rows("gcn")
    g += transposed("hn")
    for t in range(T):
        g += [("mk", t, i) for i in range(2)] + [("mv", t, i) for i in range(2)]
    g += [("kvsum", i) for i in range(2)]
    g += rows("mq")
    g += transposed("on") + rows("mproj")
    g += transposed("m1")
    g += [("logits1",), ("order1",)]
    return g


GROUPS = pe_groups()
AT = {key: n for n, key in enumerate(GROUPS)}
SPLIT = {key: n for n, key in enumerate(k for k in GROUPS if k[0] in ("T", "rfT", "q", "k", "phiq", "phik", "kv", "at", "h1", "gcnh"))}
assert len(AT) == len(GROUPS)


class Steps:

    def __init__(self, eng, own):
        self.eng, self.own, self.count, self.last = eng, own, {}, None

    def __call__(self, ins, signal=None):
        if isinstance(signal, tuple):
            sem, n = signal
        else:
            sem = self.own if signal is None else signal
            n = self.count.get(id(sem), 0) + 1
            self.count[id(sem)] = n
        ins.then_inc(sem, 1)
        self.last = (sem, n)
        return ins

    def settle(self):
        self.eng.wait_ge(*self.last)


def build(nc, x, src, dst, W1, a1_src, a1_dst, b1, W2, a2_src, a2_dst, b2, Wqkv, bqkv, Wp, bp, rf,
          ln_w, w_router, wi, wo, Wg1, bg1, w_qkv, w_proj, in_g, in_b, out_g, out_b, Wg, F1w, F1b, F2w, F2b, out):
    with ExitStack() as ctx:
        def sb(name, words, dt=F32):
            return ctx.enter_context(nc.sbuf_tensor(name, [128, words], dt))

        sems = {}

        def sem(name):
            if name not in sems:
                sems[name] = ctx.enter_context(nc.semaphore(name))
            return sems[name]

        CTt = sb("CTt", T * N)
        RTt = sb("RTt", KD * N)
        R1t = sb("R1t", T * D)
        R2t = sb("R2t", T * D)
        WK = sb("WK", 15720)
        MISC = sb("MISC", 2120)
        PS = [ctx.enter_context(nc.psum_tensor(f"bank{i}", [128, 512], F32)) for i in range(8)]

        def wk(at, n, pattern=None, parts=128, base=WK, **kw):
            v = base[0:parts, at:at + n]
            return v.rearrange(pattern, **kw) if pattern else v

        CT = CTt[:, :].rearrange("p (t n) -> p t n", t=T)

        def parts(view, pattern=None, **kw):
            h = view.bitcast(F16)
            n = view.shape[1]
            pair = (h[:, 0:n], h[:, n:2 * n])
            return tuple(a.rearrange(pattern, **kw) for a in pair) if pattern else pair

        def at2(pair, *index):
            return tuple(a[index] for a in pair)

        RT = parts(RTt[:, :], "p (k n) -> p k n", k=KD)
        R1 = R1t[:, :].rearrange("p (t d) -> p t d", t=T)
        R2 = R2t[:, :].rearrange("p (t d) -> p t d", t=T)

        used = [0]

        def misc(n, pattern=None, **kw):
            a = used[0]
            used[0] += n
            assert used[0] <= 2120, used
            v = MISC[:, a:a + n]
            return v.rearrange(pattern, **kw) if pattern else v

        ident = misc(128)
        ones = misc(128)
        upto = misc(128)
        late = MISC[:, used[0]:used[0] + 1024]
        kvpad = parts(misc(512), "p (s m d) -> p s m d", s=2, m=2)
        rfp = parts(misc(512), "p (s m) -> p s m", s=2)
        bqk = misc(12)
        b1c = misc(16)
        dinv = misc(10)
        stat = misc(T * 12, "p (t n) -> p t n", t=T)
        mv = misc(T * 2, "p (t n) -> p t n", t=T)
        rstd = misc(T)
        AS = misc(80, "p (t n) -> p t n", t=T)
        AS2 = misc(80, "p (t n) -> p t n", t=T)
        Mx = misc(40, "p (h t) -> p h t", h=4)
        Ac = misc(40, "p (h t) -> p h t", h=4)
        Bc = misc(40, "p (h t) -> p h t", h=4)
        small = misc(60)
        rd2 = misc(2)

        filled_sem, own_v, own_a, own_g = sem("bank_filled"), sem("vector_step"), sem("scalar_step"), sem("pool_step")
        emptied_sem = [sem(f"bank_emptied{b}") for b in range(BANKS)]

        def bank(*key):
            return PS[AT[key] % BANKS]

        def filled(eng, *key):
            eng.wait_ge(filled_sem, AT[key] + 1)

        def emptied(eng, *key):
            eng.wait_ge(emptied_sem[AT[key] % BANKS], AT[key] // BANKS + 1)

        def all_emptied(eng, *key):
            for n in range(max(0, AT[key] - BANKS + 1), AT[key] + 1):
                emptied(eng, *GROUPS[n])

        def agg_done(eng, u):
            filled(eng, *(("agg1", u // NC, u % NC, FC - 1) if u < H1 * NC else ("agg2", (u - H1 * NC) * TC + TC - 1, 1)))

        def turned_bank(b):
            return b[:, 0:3 * TP].rearrange("p (k n) -> p k n", k=3)

        def phik_bank(b):
            return b[0:TP, :].rearrange("p (t m) -> p t m", t=2)

        def kv_bank(b):
            return b[:, 0:2 * MD].rearrange("p (m d) -> p m d", m=2)

        def freed(*key):
            return emptied_sem[AT[key] % BANKS], AT[key] // BANKS + 1

        scr_xm = nc.dram_tensor("scr_xm", (N, D), F32).ap()
        scr_in = nc.dram_tensor("scr_in", (SLOTS, D), F32).ap()
        scr_in1 = nc.dram_tensor("scr_in1", ((MAXB + 1) * BLK, D), F32).ap()
        scr_out1 = nc.dram_tensor("scr_out1", (MAXB * BLK, D), F32).ap()
        scr_out = nc.dram_tensor("scr_out", (SLOTS, D), F32).ap()

        def node_rows(a):
            return a.rearrange("(t p) d -> p t d", p=TP)

        def kchunks(a):
            return a.rearrange("(k p) n -> p k n", p=128)

        def row(a):
            return a.rearrange("(a n) -> a n", a=1)

        qT, kT = parts(wk(0, 1250)), parts(wk(1250, 1250))
        rfn = wk(0, 512, "p (s m d) -> p s m d", s=2, m=2)
        PQ = parts(wk(2500, 5000), "p (s m n) -> p s m n", s=2, m=2)
        PK = parts(wk(7500, 5120), "p (s t m) -> p s t m", s=2, t=T)
        bv_row = wk(7500, 768)
        v_tmp = wk(8300, HALF)
        Wqk = [parts(wk(12620 + 768 * w, 768), "p (k n) -> p k n", k=KD) for w in range(2)]
        stages0 = [wk(14156 + 768 * i, 768) for i in range(2)]
        bias_rows = wk(0, 1536, "p (i d) -> p i d", i=2)
        ATt = parts(CTt[:, 0:7500], "p (k n) -> p k n", k=KD)
        Wv = parts(CTt[:, 7500:12108], "p (k n) -> p k n", k=KD)
        Vr = [parts(R2t[:, t * D:(t + 1) * D]) for t in range(T)]
        nat_i = WK[0:NG, 0:1000].bitcast(I32).rearrange("p (a e) -> p a e", a=2)
        nat = wk(1000, 1000, "p (a e) -> p a e", NG, a=2)
        keys = wk(2000, 1000, "p (a e) -> p a e", NG, a=2)
        tdiv = wk(3000, 500, None, NG)
        gmm = wk(3500, 2, None, NG)
        tab = wk(3510, 16, None, NW)
        iota_i = WK[:, 3600:4100].bitcast(I32)
        iota = wk(4100, 500)
        cutI = wk(4600, 80, None, NW)
        cutJ = wk(4700, 80, None, NW)
        cutK = wk(4800, 80, None, NW)
        trow_i = WK[0:1, 4900:4980].bitcast(I32)
        trow = WK[0:1, 5040:5066]
        iota_c_i = WK[:, 4980:4981].bitcast(I32)
        iota_c = wk(4984, 2)
        upper = wk(5000, 32, None, 32)
        KL = wk(5100, 640, "p (a q g) -> p a q g", a=2, q=QG)
        oh_lo = [WK[:, 5800 + 64 * i:5864 + 64 * i].bitcast(F16) for i in range(QG)]
        oh_key = [WK[:, 6100 + 250 * i:6350 + 250 * i].bitcast(F16) for i in range(QG)]
        zero_bf = WK[:, 7100:7350].bitcast(F16)
        iota16 = WK[:, 8700:8950].bitcast(F16)
        degp = wk(7400, 1250)
        arow = wk(0, 4096, "p (a n) -> p a n", a=2)
        W1s = [wk(4096 + 3072 * i, 3072, "p (k n) -> p k n", k=KD) for i in range(2)]
        junk = wk(10240, 768)
        wa = wk(11100, 48, "p (k n) -> p k n", k=KD)
        wa2 = parts(wk(11200, 48), "p (k n) -> p k n", k=KD)
        maxacc = wk(0, 5000, "p (h n) -> p h n", h=4)
        maskt = wk(5000, 1250)
        Hh = parts(wk(0, 5120), "p (t n) -> p t n", t=T)
        Pm = [parts(wk(5120 + 2500 * i, 2500), "p (t n) -> p t n", t=T) for i in range(2)]
        H1T = [parts(wk(10120 + 1000 * i, 1000), "p (f n) -> p f n", f=FC) for i in range(2)]
        U = wk(12120, 2500, "p (t n) -> p t n", t=T)
        rden = [wk(14620 + 250 * i, 250) for i in range(2)]
        Sp = [wk(15120 + 250 * i, 250) for i in range(2)]
        W1h = parts(R1t[:, 0:3072], "p (k n) -> p k n", k=KD)
        W2h = parts(R1t[:, 3072:6144], "p (k n) -> p k n", k=FC)
        elu_z = R1t[:, 6144:6394]
        elu_m = R1t[:, 6394:6644]
        elu_r = R1t[:, 6644:6894]
        stages1 = [R1t[:, 6900:7668]]
        h2_tmp = [wk(2304 + 768 * i, 768) for i in range(2)]
        H2 = [parts(R2t[:, t * D:(t + 1) * D]) for t in range(T)]
        a2row = wk(0, 1536, "p (a n) -> p a n", a=2)
        junk2 = wk(1536, 768)
        max2a, mask2 = wk(12120, 1250), wk(13370, 1250)
        lnw_row = wk(0, 768)
        router_in = wk(768, 96)
        router = parts(late[:, 0:96], "p (k e) -> p k e", k=KD)
        G0 = wk(900, 160, "p (t e) -> p t e", t=T)
        G1 = wk(1060, 160, "p (t e) -> p t e", t=T)
        G2 = wk(1220, 160, "p (t e) -> p t e", t=T)
        G3 = wk(1380, 160, "p (t e) -> p t e", t=T)
        ebase = wk(1540, 160, "p (t e) -> p t e", t=T)
        esort = wk(1700, 160, "p (t e) -> p t e", t=T)
        gcol = wk(1860, 120, "p (c t) -> p c t", c=12)
        e_i = WK[:, 1980:2140].bitcast(I32)
        slot_s = WK[:, 2140:2150].bitcast(I32)
        slot_g = WK[:, 2150:2160].bitcast(I32)
        zero_row = wk(2200, 768)
        ein = wk(3000, 768)
        einT = wk(3768, 768, "p (k n) -> p k n", k=KD)
        hE = [wk(4540 + 192 * i, 192, "p (f n) -> p f n", f=F0C) for i in range(2)]
        oE = [wk(4930 + 768 * i, 768) for i in range(2)]
        EW = [wk(6500 + 4608 * i, 4608) for i in range(2)]
        wiE = [w[:, 0:2304].rearrange("p (k n) -> p k n", k=KD) for w in EW]
        woE = [w[:, 2304:4608].rearrange("p (k n) -> p k n", k=F0C) for w in EW]
        gath = [wk(6500 + 768 * i, 768) for i in range(2)]
        gH = [parts(wk(D * t, D)) for t in range(T)]
        gW = parts(wk(7680, 4608), "p (k n) -> p k n", k=KD)
        grow = wk(12300, 768)
        stages2 = [wk(13100 + 768 * i, 768) for i in range(2)]
        ct_tmp = late[:, 144:144 + N // 2]
        CT2 = [parts(CTt[:, i * N // 2:(i + 1) * N // 2]) for i in range(2 * T)]
        wqv = [parts(CTt[:, 4608 * i:4608 * i + 4608], "p (k n) -> p k n", k=KD) for i in range(2)]
        wq2 = parts(wk(0, 4608), "p (k n) -> p k n", k=KD)
        wpr = parts(wk(4608, 4608), "p (k n) -> p k n", k=KD)
        kt_ = [wk(9216 + 768 * i, 768) for i in range(2)]
        sq_ = wk(10752, 768)
        psum_row = wk(11520, 768)
        kvb = wk(12288, 768)
        grow2 = CTt[:, 9300:10836].rearrange("p (a n) -> p a n", a=2)
        prodsum = CTt[:, 10900:11668]
        FW = [CTt[:, 4608 * i:4608 * i + 4608] for i in range(2)]
        w1E = [w[:, 0:2304].rearrange("p (k n) -> p k n", k=KD) for w in FW]
        w2E = [w[:, 2304:4608].rearrange("p (k n) -> p k n", k=F0C) for w in FW]
        b2row = wk(0, 6144, "p (e d) -> p e d", e=E1)
        xb = wk(6144, 768)
        xbT = wk(6912, 768, "p (k n) -> p k n", k=KD)
        hB = wk(7680, 384, "p (f n) -> p f n", f=F0C)
        oB = wk(8064, 768)
        wgE_in = wk(8840, 48)
        wgE = parts(late[:, 96:144], "p (k e) -> p k e", k=KD)
        b1E = wk(8900, 24, "p (e f) -> p e f", e=E1)
        L0 = wk(9000, 80, "p (t e) -> p t e", t=T)
        L1 = wk(9080, 80, "p (t e) -> p t e", t=T)
        L2 = wk(9160, 80, "p (t e) -> p t e", t=T)
        L3 = wk(9240, 80, "p (t e) -> p t e", t=T)
        esort1 = wk(9320, 80, "p (t e) -> p t e", t=T)
        e1_i = WK[:, 9400:9480].bitcast(I32)
        lcol = wk(9480, 60, "p (c t) -> p c t", c=6)
        cnt1 = wk(9540, 8)
        nblk = wk(9550, 8)
        first1 = wk(9560, 9)
        first_i = WK[:, 9570:9579].bitcast(I32)
        slot1 = WK[:, 9580:9590].bitcast(I32)
        tick = wk(9592, 1)
        zero1 = wk(9600, 768)
        gath1 = [wk(10400 + 768 * i, 768) for i in range(2)]

        pieces = []
        piece_after = {}

        def weight(name, srcs, dests, stages, tag, after=None):
            for (a, d) in zip(srcs, dests):
                i = len([1 for p in pieces if p[4][0] == tag]) % len(stages)
                if after:
                    piece_after[len(pieces)] = after
                pieces.append((name, a, d, stages[i], (tag, i)))

        def last_piece(name):
            return max(n for n, p in enumerate(pieces) if p[0] == name)

        def by_k(w, n=KD):
            return [w[k * 128:(k + 1) * 128, :] for k in range(n)]

        def part_k(pair, n=KD):
            return [at2(pair, slice(None), k) for k in range(n)]

        weight("Wv", by_k(Wqkv[:, 2 * D:3 * D]), part_k(Wv), stages0, "a")
        for p in range(MH // 2):
            for w in range(2):
                weight(("Wqk", p), [kchunks(Wqkv[:, w * D + 128 * p:w * D + 128 * p + 128])], [Wqk[w]], stages0, "a", ("k", p - 1, 2) if p else None)
            if p == 0:
                weight("Wp", by_k(Wp), part_k(Wv), stages0, "a", ("v", T - 1, 1))
        for h in range(H1):
            weight(("W1h", h), by_k(W1[:, h * HID:(h + 1) * HID]), part_k(W1h), stages1, "b", ("h1", h - 1, T - 1) if h else None)
            weight(("W2h", h), by_k(W2[h * HID:(h + 1) * HID, :], FC), part_k(W2h, FC), stages1, "b", ("w2", h - 1, T - 1, 1) if h else None)
        weight("router", [kchunks(w_router)], [router], [router_in], "c")
        weight("gW", by_k(Wg1), part_k(gW), stages2, "d")
        for name, c0, dest in (("wk", D, wqv[0]), ("wv", 2 * D, wqv[1]), ("wq", 0, wq2)):
            weight(name, by_k(w_qkv[:, c0:c0 + D]), part_k(dest), stages2, "d", ("gcn", T - 1, 1))
        weight("wpr", by_k(w_proj), part_k(wpr), stages2, "d", ("gcn", T - 1, 1))
        weight("wg", [kchunks(Wg)], [wgE], [wgE_in], "e")

        def shaped(view, like):
            n = 1
            for x_ in like.shape[1:]:
                n *= x_
            v = view[:, 0:n]
            return v.rearrange("p (k n) -> p k n", n=like.shape[-1]) if len(like.shape) == 3 else v

        block = ctx.enter_context(nc.Block())

        @block.sync
        def _(sp):
            def load(o, i, s):
                sp.dma_start(o, i).then_inc(sem(s), 16)

            next_piece = [0]

            def load_pieces(*names):
                for name in names:
                    while next_piece[0] < len(pieces) and pieces[next_piece[0]][0] == name:
                        n = next_piece[0]
                        next_piece[0] += 1
                        _, a, _, stage, place = pieces[n]
                        before = [m for m in range(n) if pieces[m][4] == place]
                        if before:
                            sp.wait_ge(sem("weights_split"), before[-1] + 1)
                        load(shaped(stage, a), a, f"weight_in_{place[0]}{place[1]}")

            def after(*key):
                filled(sp, *key)

            for t in range(T):
                sp.dma_start(R1[0:TP, t, :], x[t * TP:(t + 1) * TP, :]).then_inc(sem(f"in_x{t}"), 16)
            load(bv_row, row(bqkv[2 * D:3 * D]).to_broadcast([128, D]), "in_bv")
            sp.wait_ge(sem("pads"), 1)
            for s in range(2):
                load(rfn[:, s, :, s * MD:(s + 1) * MD], rf.rearrange("(m p) d -> p m d", p=128), "in_rf")
            with nc.allow_non_contiguous_dma(reason="columns of a short vector"):
                load(bqk, bqkv[0:2 * D].rearrange("(k p) -> p k", p=128), "in_bqk")
                load(b1c, b1.rearrange("(k p) -> p k", p=128), "in_b1")
            load_pieces("Wv", ("Wqk", 0), "Wp", *[("Wqk", p) for p in range(1, MH // 2)])
            after("at", 5, 2)
            load(bias_rows[:, 0, :], row(bp).to_broadcast([128, D]), "in_bias")
            load(bias_rows[:, 1, :], row(b2).to_broadcast([128, D]), "in_bias")
            all_emptied(sp, "proj", T - 1, 1)
            sp.wait_ge(sem("bias_added"), T)
            load(nat_i[:, 0, :], src.rearrange("(g e) -> g e", g=NG), "in_edges")
            load(nat_i[:, 1, :], dst.rearrange("(g e) -> g e", g=NG), "in_edges")
            sp.dma_start(node_rows(scr_xm), R1[0:TP, :, :]).then_inc(sem("xm_kept"), 16)
            emptied(sp, "deg")
            load(arow[:, 0, :], row(a1_src.rearrange("h d -> (h d)")).to_broadcast([128, 2048]), "in_a1")
            load(arow[:, 1, :], row(a1_dst.rearrange("h d -> (h d)")).to_broadcast([128, 2048]), "in_a1")
            for h in range(H1):
                if h >= 2:
                    sp.wait_ge(sem("W1_folded"), h - 1)
                load(W1s[h % 2], kchunks(W1[:, h * HID:(h + 1) * HID]), f"in_W1s{h % 2}")
            sp.wait_ge(sem("xm_kept"), 16)
            for h in range(H1):
                load_pieces(("W1h", h), ("W2h", h))
            after("w2", H1 - 1, T - 1, 1)
            load(a2row[:, 0, :], a2_src.to_broadcast([128, D]), "in_a2")
            load(a2row[:, 1, :], a2_dst.to_broadcast([128, D]), "in_a2")
            all_emptied(sp, "w2", H1 - 1, T - 1, 1)
            load(R1[0:TP, :, :], node_rows(scr_xm), "xm_back")
            all_emptied(sp, "agg2", T - 1, 1)
            load(lnw_row, row(ln_w).to_broadcast([128, D]), "in_lnw")
            load_pieces("router")
            sp.wait_ge(sem("zeros_set"), 1)
            for i in range(SLOTS // 128):
                sp.dma_start(scr_in[i * 128:(i + 1) * 128, :], zero_row).then_inc(sem("slots_zeroed"), 16)
            for e in range(E0):
                if e >= 2:
                    after("eo", e - 2, 1)
                if e % 2 == 0:
                    if e:
                        after("einT", e - 2, 1)
                    else:
                        sp.wait_ge(sem("scattered"), 16 * T)
                load(wiE[e % 2], kchunks(wi[e]), f"in_we{e % 2}")
                load(woE[e % 2], kchunks(wo[e]), f"in_we{e % 2}")
                if e % 2 == 0:
                    load(ein, scr_in[e * CAP:(e + 2) * CAP, :], "in_ein")
            sp.wait_ge(sem("switch_done"), 1)
            load_pieces("gW")
            load(grow, row(bg1).to_broadcast([128, D]), "in_gb")
            load_pieces("wk", "wv", "wq", "wpr")
            all_emptied(sp, "gcn", T - 1, 1)
            load(grow2[:, 0, :], row(in_g).to_broadcast([128, D]), "in_ln")
            load(grow2[:, 1, :], row(in_b).to_broadcast([128, D]), "in_ln")
            sp.wait_ge(sem("hn_rows"), T)
            load(grow2[:, 0, :], row(out_g).to_broadcast([128, D]), "in_ln")
            load(grow2[:, 1, :], row(out_b).to_broadcast([128, D]), "in_ln")
            all_emptied(sp, "mproj", T - 1, 1)
            load_pieces("wg")
            for e in range(E1):
                with nc.allow_non_contiguous_dma(reason="columns of a short vector"):
                    sp.dma_start(b1E[:, e, :], F1b[e].rearrange("(f p) -> p f", p=128)).then_inc(sem("in_b1E"), 16)
                load(b2row[:, e, :], F2b[e:e + 1, :].to_broadcast([128, D]), "in_b2E")
            sp.wait_ge(sem("zeros1_set"), 1)
            for i in range(MAXB + 1):
                sp.dma_start(scr_in1[i * BLK:(i + 1) * BLK, :], zero1).then_inc(sem("blocks_zeroed"), 16)
            for i in range(MINB, MAXB):
                sp.dma_start(scr_out1[i * BLK:(i + 1) * BLK, :], zero1).then_inc(sem("blocks_zeroed"), 16)
            sp.wait_ge(sem("scattered1"), 16 * T)
            load(xb, scr_in1[0:BLK, :], "in_xb")
            blocks = sp.value_load(first_i[0:1, E1:E1 + 1], min_val=E1, max_val=MAXB)
            with sp.Fori(1, blocks + 1) as b:
                sp.wait_ge(sem("block_turned"), b)
                sp.dma_start(xb, scr_in1[bass.ds(b * BLK, BLK), :]).then_inc(sem("in_xb"), 16)
            sp.wait_ge(sem("out_rows"), T)
            sp.dma_start(node_rows(out), R1[0:TP, :, :]).then_inc(sem("out_stored"), 16)
            sp.wait_ge(sem("out_stored"), 16)

        @block.tensor
        def _(pe):
            nth = [0]

            def group(*key):
                n = nth[0]
                assert GROUPS[n] == key, (GROUPS[n], key)
                nth[0] += 1
                if n >= BANKS:
                    pe.wait_ge(emptied_sem[n % BANKS], n // BANKS)
                return PS[n % BANKS]

            def mm(o, lhsT, rhs, first, last):
                return nc.tensor.matmul(o, lhsT, rhs, start=first, stop=last)

            def mm3(o, lhsT, rhs, first, last):
                nc.tensor.matmul(o, lhsT[0], rhs[0], start=first, stop=False)
                nc.tensor.matmul(o, lhsT[0], rhs[1], start=False, stop=False)
                return nc.tensor.matmul(o, lhsT[1], rhs[0], start=False, stop=last)

            def split(name):
                pe.wait_ge(sem("weights_split"), last_piece(name) + 1)

            def close(ins):
                ins.then_inc(filled_sem, 1)

            def transposed(name, rows_sem, rows_at=1):
                for t in range(T):
                    pe.wait_ge(rows_sem, rows_at * (t + 1))
                    for i in range(2):
                        ps = group("T", name, t, i)
                        for j in range(3):
                            k = 3 * i + j
                            ins = nc.tensor.transpose(ps[:, j * TP:(j + 1) * TP], R2[0:TP, t, k * 128:(k + 1) * 128], ident[0:TP, 0:TP])
                        close(ins)

            def rows(name, t, w, lhs=RT):
                for i in range(2):
                    ps = group(name, t, i)
                    for k in range(KD):
                        ins = mm3(ps[0:TP, 0:HALF], at2(lhs, slice(None), k, slice(t * TP, (t + 1) * TP)),
                                  at2(w, slice(None), k, slice(i * HALF, (i + 1) * HALF)), k == 0, k == KD - 1)
                    close(ins)

            pe.wait_ge(sem("consts"), 3)
            transposed("xn", sem("xn_rows"))
            all_emptied(pe, "T", "xn", T - 1, 1)
            split("Wv")
            for t in range(T):
                rows("v", t, Wv)
            pe.wait_ge(sem("in_rf"), 32)
            ps = group("rfT")
            for s in range(2):
                for m in range(2):
                    ins = nc.tensor.transpose(ps[:, (2 * s + m) * 128:(2 * s + m + 1) * 128], rfn[:, s, m, :], ident)
            close(ins)
            for p in range(MH // 2):
                split(("Wqk", p))
                for w, name in enumerate("qk"):
                    for c, (c0, cn) in enumerate(COLS):
                        ps = group(name, p, c)
                        for k in range(KD):
                            ins = mm3(ps[:, 0:cn], at2(Wqk[w], slice(None), k), at2(RT, slice(None), k, slice(c0, c0 + cn)), k == 0, k == KD - 1)
                        close(ins)
                all_emptied(pe, "k", p, 2)
                for s in range(2):
                    for m in range(2):
                        for c, (c0, cn) in enumerate(COLS):
                            ps = group("phiq", p, s, m, c)
                            close(mm3(ps[:, 0:cn], at2(rfp, slice(None), s, slice(m * 128, (m + 1) * 128)), at2(qT, slice(None), slice(c0, c0 + cn)), True, True))
                    for i in range(T // 2):
                        ps = group("phik", p, s, i)
                        for j in range(2):
                            t = 2 * i + j
                            ins = mm3(ps[0:TP, j * MM:(j + 1) * MM], at2(kT, slice(None), slice(t * TP, (t + 1) * TP)), at2(rfp, slice(None), s), True, True)
                        close(ins)
                for s in range(2):
                    all_emptied(pe, "phik", p, s, T // 2 - 1)
                    if p == 0 and s == 0:
                        pe.wait_ge(sem("v_split"), 2 * T)
                    ps = group("kv", p, s)
                    for m in range(2):
                        for t in range(T):
                            ins = mm3(ps[:, m * MD:(m + 1) * MD], at2(PK, slice(0, TP), s, t, slice(m * 128, (m + 1) * 128)),
                                      at2(Vr[t], slice(0, TP), slice((2 * p + s) * MD, (2 * p + s + 1) * MD)), t == 0, t == T - 1)
                    close(ins)
                all_emptied(pe, "kv", p, 1)
                for s in range(2):
                    all_emptied(pe, "phiq", p, s, 1, 2)
                for c, (c0, cn) in enumerate(COLS):
                    ps = group("at", p, c)
                    for s in range(2):
                        for m in range(2):
                            ins = mm3(ps[:, 0:cn], at2(kvpad, slice(None), s, m), at2(PQ, slice(None), s, m, slice(c0, c0 + cn)), s + m == 0, s + m == 2)
                    close(ins)
            all_emptied(pe, "at", 5, 2)
            split("Wp")
            for t in range(T):
                rows("proj", t, Wv, ATt)

            pe.wait_ge(sem("edge_keys"), 1)
            for a in range(2):
                ps = group("edgeT", a)
                for q in range(QG):
                    ins = nc.tensor.transpose(ps[0:TP, q * NG:(q + 1) * NG], keys[:, a, q * TP:(q + 1) * TP], ident[0:NG, 0:NG])
                close(ins)
            ps = group("groupB")
            for a in range(2):
                ins = mm(ps[0:NW, a * NG:(a + 1) * NG], gmm[:, a:a + 1].to_broadcast([NG, NW]), ident[0:NG, 0:NG], True, True)
            close(ins)
            pe.wait_ge(sem("window_cols"), 1)
            ps = group("tables")
            for a in range(2):
                mm(ps[0:1, a * NW:(a + 1) * NW], tab[:, a:a + 1], ident[0:NW, 0:NW], True, True)
            close(mm(ps[0:1, 2 * NW:3 * NW], tab[:, 2:3], upper[0:NW, 0:NW], True, True))
            pe.wait_ge(sem("window_table"), 1)
            pe.wait_ge(sem("iota_set"), 1)
            pe.sem_inc(sem("onehots_used"), BIAS + 2)
            for w in range(NW):
                ps = PS[6 + w % 2]
                if w >= 2:
                    pe.wait_ge(sem("window_emptied"), w - 1)
                g0 = pe.value_load(trow_i[0:1, w:w + 1], min_val=0, max_val=NG - 1)
                g1 = pe.value_load(trow_i[0:1, NW + w:NW + w + 1], min_val=1, max_val=NG)
                base = pe.value_load(trow_i[0:1, 2 * NW + w:2 * NW + w + 1], min_val=0, max_val=2 * NG * NW + BIAS)
                nc.tensor.matmul(ps[0:TP, 0:500], zero_bf[0:TP, 0:TP], zero_bf[0:TP, 0:500], start=True, stop=False)
                with pe.Fori(g0, g1) as g:
                    for half in range(2):
                        pe.wait_ge(sem("onehots_ready"), base + g * 2 + (half + 1))
                        for q in range(2 * half, 2 * half + 2):
                            ins = nc.tensor.matmul(ps[0:TP, 0:500], oh_lo[q][0:TP, 0:TP], oh_key[q][0:TP, 0:500], start=False, stop=False)
                        ins.then_inc(sem("onehots_used"), 1)
                nc.tensor.matmul(ps[0:TP, 0:500], zero_bf[0:TP, 0:TP], zero_bf[0:TP, 0:500], start=False, stop=True).then_inc(sem("window_filled"), 1)
            pe.wait_ge(sem("deg_parts"), 1)
            ps = group("deg")
            for t in range(T):
                ins = mm(ps[0:TP, t:t + 1], degp[0:TP, t * TP:(t + 1) * TP], ones[0:TP, 0:1], True, True)
            close(ins)

            pe.wait_ge(sem("fold_split"), 1)
            ps = group("coef1")
            for t in range(T):
                for k in range(KD):
                    ins = mm3(ps[0:TP, t * 8:t * 8 + 8], at2(RT, slice(None), k, slice(t * TP, (t + 1) * TP)), at2(wa2, slice(None), k), k == 0, k == KD - 1)
            close(ins)

            def max_tiles(i, acc, *key):
                ps = group(*key)
                for j, t in enumerate(range(4 * i, min(4 * i + 4, T))):
                    ins = nc.tensor.transpose(ps[0:TP, j * TP:(j + 1) * TP], acc[0:TP, t * TP:(t + 1) * TP], ident[0:TP, 0:TP])
                close(ins)

            pe.wait_ge(sem("max_rows"), 1)
            for h in range(H1):
                for i in range(3):
                    max_tiles(i, maxacc[:, h, :], "max1", h, i)

            def coef_rows(u, h, c):
                if u >= 2:
                    pe.wait_ge(sem("coef_used"), u - 1)
                ps = PS[6 + u % 2]
                for a, col in enumerate((Ac, Bc)):
                    for t in range(TC):
                        tt = c * TC + t
                        ins = mm(ps[0:TP, (a * TC + t) * TP:(a * TC + t + 1) * TP], col[0:TP, h, tt:tt + 1].to_broadcast([TP, TP]),
                                 ident[0:TP, 0:TP], True, True)
                ins.then_inc(sem("coef_rows"), 1)

            pe.wait_ge(sem("coef_cols"), 1)
            coef_rows(0, 0, 0)
            for h in range(H1):
                split(("W1h", h))
                for t in range(T):
                    ps = group("h1", h, t)
                    for k in range(KD):
                        ins = mm3(ps[0:TP, :], at2(RT, slice(None), k, slice(t * TP, (t + 1) * TP)), at2(W1h, slice(None), k), k == 0, k == KD - 1)
                    close(ins)
                all_emptied(pe, "h1", h, T - 1)

                def w2(c):
                    split(("W2h", h))
                    all_emptied(pe, "agg1", h, c, FC - 1)
                    pe.wait_ge(sem("elu_done"), FC * (h * NC + c + 1))
                    for t in range(TC):
                        for i in range(2):
                            ps = group("w2", h, c * TC + t, i)
                            for f in range(FC):
                                ins = mm3(ps[0:TP, 0:HALF], at2(H1T[(h * NC + c) % 2], slice(None), f, slice(t * TP, (t + 1) * TP)),
                                          at2(W2h, slice(None), f, slice(i * HALF, (i + 1) * HALF)), f == 0, f == FC - 1)
                            close(ins)

                for c in range(NC):
                    u = h * NC + c
                    if u + 1 < H1 * NC:
                        coef_rows(u + 1, (u + 1) // NC, (u + 1) % NC)
                    pe.wait_ge(sem("P_sums"), u + 1)
                    ps = group("den1", h, c)
                    close(mm(ps[:, 0:IC], ones[0:TP, :], Sp[u % 2][0:TP, :], True, True))
                    pe.wait_ge(sem("P_high"), u + 1)
                    pe.wait_ge(sem("P_low"), u + 1)
                    for f in range(FC):
                        ps = group("agg1", h, c, f)
                        for j in range(T):
                            ins = mm3(ps[:, 0:IC], at2(Hh, slice(0, TP), j, slice(f * 128, (f + 1) * 128)), at2(Pm[u % 2], slice(0, TP), j), j == 0, j == T - 1)
                        close(ins)
                    if c:
                        w2(c - 1)
                w2(NC - 1)

            pe.wait_ge(sem("max_rows"), 2)
            for i in range(3):
                max_tiles(i, max2a, "max2", i)
            pe.wait_ge(sem("coef_cols"), 2)
            coef_rows(H1 * NC, 0, 0)
            for c in range(NC):
                u = H1 * NC + c
                if c + 1 < NC:
                    coef_rows(u + 1, 0, c + 1)
                pe.wait_ge(sem("P_sums"), u + 1)
                ps = group("den2", c)
                for t in range(TC):
                    ins = mm(ps[0:TP, t:t + 1], Sp[u % 2][0:TP, t * TP:(t + 1) * TP], ones[0:TP, 0:1], True, True)
                close(ins)
                pe.wait_ge(sem("P_high"), u + 1)
                pe.wait_ge(sem("P_low"), u + 1)
                pe.wait_ge(sem("h2_split"), T)
                for t in range(TC):
                    for i in range(2):
                        ps = group("agg2", c * TC + t, i)
                        for j in range(T):
                            ins = mm3(ps[0:TP, 0:HALF], at2(Pm[u % 2], slice(0, TP), j, slice(t * TP, (t + 1) * TP)),
                                      at2(H2[j], slice(0, TP), slice(i * HALF, (i + 1) * HALF)), j == 0, j == T - 1)
                        close(ins)

            transposed("m0", sem("normed_rows"))
            all_emptied(pe, "T", "m0", T - 1, 1)
            split("router")
            ps = group("logits0")
            for t in range(T):
                for k in range(KD):
                    ins = mm3(ps[0:TP, t * E0:(t + 1) * E0], at2(RT, slice(None), k, slice(t * TP, (t + 1) * TP)), at2(router, slice(None), k), k == 0, k == KD - 1)
            close(ins)
            pe.wait_ge(sem("onehot0"), 1)
            ps = group("order0")
            oh = G1[0:TP, :, :].rearrange("p t e -> p (t e)")
            mm(ps[0:TP, 0:160], upto[0:TP, 0:TP], oh, True, True)
            close(mm(ps[0:TP, 160:320], ones[0:TP, 0:TP], oh, True, True))
            for e in range(0, E0, 2):
                pe.wait_ge(sem("in_ein"), 16 * (e // 2 + 1))
                for i in range(2):
                    ps = group("einT", e, i)
                    for j in range(3):
                        k = 3 * i + j
                        ins = nc.tensor.transpose(ps[:, j * 128:(j + 1) * 128], ein[:, k * 128:(k + 1) * 128], ident[:, :])
                    close(ins)
                all_emptied(pe, "einT", e, 1)
                for d in range(2):
                    pe.wait_ge(sem(f"in_we{d}"), 32 * (e // 2 + 1))
                    ps = group("eh", e + d)
                    for f in range(F0C):
                        for k in range(KD):
                            ins = mm(ps[:, f * CAP:(f + 1) * CAP], wiE[d][:, k, f * 128:(f + 1) * 128], einT[:, k, d * CAP:(d + 1) * CAP], k == 0, k == KD - 1)
                    close(ins)
                    emptied(pe, "eh", e + d)
                    for i in range(2):
                        ps = group("eo", e + d, i)
                        for f in range(F0C):
                            ins = mm(ps[0:CAP, 0:HALF], hE[d][:, f, :], woE[d][:, f, i * HALF:(i + 1) * HALF], f == 0, f == F0C - 1)
                        close(ins)

            transposed("x2", sem("x2_rows"))
            all_emptied(pe, "T", "x2", T - 1, 1)
            split("gW")
            for t in range(T):
                rows("gcnh", t, gW)
            all_emptied(pe, "gcnh", T - 1, 1)
            pe.wait_ge(sem("counts_split"), 2 * T)
            for t in range(T):
                for i in range(2):
                    ps = group("gcn", t, i)
                    for j in range(T):
                        ins = mm3(ps[0:TP, 0:HALF], at2(CT2[2 * j + t // (T // 2)], slice(0, TP), slice(t % (T // 2) * TP, (t % (T // 2) + 1) * TP)),
                                  at2(gH[j], slice(0, TP), slice(i * HALF, (i + 1) * HALF)), j == 0, j == T - 1)
                    close(ins)

            transposed("hn", sem("hn_rows"))
            all_emptied(pe, "T", "hn", T - 1, 1)
            split("wv")
            for t in range(T):
                rows("mk", t, wqv[0])
                rows("mv", t, wqv[1])
            pe.wait_ge(sem("kv_rows"), 1)
            for i in range(2):
                ps = group("kvsum", i)
                close(mm(ps[0:TP, 0:HALF], ones[0:TP, 0:TP], prodsum[0:TP, i * HALF:(i + 1) * HALF], True, True))
            split("wq")
            for t in range(T):
                rows("mq", t, wq2)
            transposed("on", sem("on_rows"))
            all_emptied(pe, "T", "on", T - 1, 1)
            split("wpr")
            for t in range(T):
                rows("mproj", t, wpr)

            transposed("m1", sem("m1_rows"))
            all_emptied(pe, "T", "m1", T - 1, 1)
            split("wg")
            ps = group("logits1")
            for t in range(T):
                for k in range(KD):
                    ins = mm3(ps[0:TP, t * E1:(t + 1) * E1], at2(RT, slice(None), k, slice(t * TP, (t + 1) * TP)), at2(wgE, slice(None), k), k == 0, k == KD - 1)
            close(ins)
            pe.wait_ge(sem("onehot1"), 1)
            ps = group("order1")
            oh = L1[0:TP, :, :].rearrange("p t e -> p (t e)")
            mm(ps[0:TP, 0:80], upto[0:TP, 0:TP], oh, True, True)
            close(mm(ps[0:TP, 80:160], ones[0:TP, 0:TP], oh, True, True))
            emptied(pe, "order1")

            def turn_block():
                for i in range(2):
                    for j in range(3):
                        k = 3 * i + j
                        ins = nc.tensor.transpose(PS[i][:, j * BLK:(j + 1) * BLK], xb[:, k * 128:(k + 1) * 128], ident)
                ins.then_inc(sem("block_turned"), 1)

            pe.wait_ge(sem("in_xb"), 16)
            turn_block()
            pe.wait_ge(sem("blocks_known"), 1)
            for e in range(E1):
                b0 = pe.value_load(first_i[0:1, e:e + 1], min_val=e, max_val=MAXB - 1)
                b1_ = pe.value_load(first_i[0:1, e + 1:e + 2], min_val=e + 1, max_val=MAXB)
                pe.wait_ge(sem(f"in_fe{e % 2}"), 32 * (e // 2 + 1))
                with pe.Fori(b0, b1_) as b:
                    pe.wait_ge(sem("block_T_ready"), b + 1)
                    for f in range(F0C):
                        for k in range(KD):
                            ins = mm(PS[2][:, f * BLK:(f + 1) * BLK], w1E[e % 2][:, k, f * 128:(f + 1) * 128], xbT[:, k, :], k == 0, k == KD - 1)
                    ins.then_inc(sem("block_h"), 1)
                    pe.wait_ge(sem("in_xb"), b * 16 + 32)
                    turn_block()
                    pe.wait_ge(sem("block_h_ready"), b + 1)
                    pe.wait_ge(sem("block_out_emptied"), b + 1)
                    for i in range(2):
                        for f in range(F0C):
                            ins = mm(PS[4 + i][:, 0:HALF], hB[:, f, :], w2E[e % 2][:, f, i * HALF:(i + 1) * HALF], f == 0, f == F0C - 1)
                    ins.then_inc(sem("block_out"), 1)
            assert nth[0] == len(GROUPS)

        @block.scalar
        def _(act):
            do = Steps(act, own_a)
            A = nc.scalar.activation

            def high(key, o, view, func=ACT.Copy, **kw):
                filled(act, *key)
                assert SPLIT[key] == do.count.get(id(sem("high_made")), 0), key
                do(A(o, view(bank(*key)), func, **kw), sem("high_made"))

            def turned(name):
                for t in range(T):
                    for i in range(2):
                        high(("T", name, t, i), RT[0][:, 3 * i:3 * i + 3, t * TP:(t + 1) * TP], turned_bank)

            def root(at):
                act.wait_ge(sem("variances"), at)
                do(A(rstd[0:TP, :], rstd[0:TP, :], ACT.Sqrt), sem("roots"))

            root(1)
            turned("xn")
            high(("rfT",), rfp[0], lambda b: b.rearrange("p (s m) -> p s m", s=2))
            act.wait_ge(sem("in_bqk"), 16)
            for p in range(MH // 2):
                for w, name in enumerate("qk"):
                    for c, (c0, cn) in enumerate(COLS):
                        high((name, p, c), (qT, kT)[w][0][:, c0:c0 + cn], lambda b: b[:, 0:cn], ACT.Identity, bias=bqk[:, w * 6 + p:w * 6 + p + 1])
                for s in range(2):
                    for m in range(2):
                        for c, (c0, cn) in enumerate(COLS):
                            high(("phiq", p, s, m, c), PQ[0][:, s, m, c0:c0 + cn], lambda b: b[:, 0:cn], ACT.Relu)
                    for i in range(T // 2):
                        high(("phik", p, s, i), PK[0][0:TP, s, 2 * i:2 * i + 2, :], phik_bank, ACT.Relu)
                for s in range(2):
                    if p + s == 0:
                        act.wait_ge(sem("pads"), 2)
                    high(("kv", p, s), kvpad[0][:, s, :, s * MD:(s + 1) * MD], kv_bank, scale=KV_SCALE)
                for c, (c0, cn) in enumerate(COLS):
                    high(("at", p, c), ATt[0][:, p, c0:c0 + cn], lambda b: b[:, 0:cn])
            all_emptied(act, "proj", T - 1, 1)
            for w in range(NW):
                act.wait_ge(sem("window_filled"), w + 1)
                do(A(CT[0:TP, :, w * WIN:(w + 1) * WIN], PS[6 + w % 2][0:TP, 0:500].rearrange("p (i t) -> p t i", t=T), ACT.Copy), sem("window_emptied"))
            act.wait_ge(sem("deg_copied"), 1)
            do(A(dinv[0:TP, :], dinv[0:TP, :], ACT.Sqrt), sem("deg_root"))

            def scores(u, col):
                ps = PS[6 + u % 2]
                act.wait_ge(sem("coef_rows"), u + 1)
                if u:
                    act.wait_ge(sem("P_sums"), u)
                    act.wait_ge(sem("P_low"), u)
                for t in range(T):
                    do(A(U[0:TP, t, :], ps[0:TP, IC:2 * IC], ACT.Identity, bias=AS2[0:TP, t, col:col + 1]), sem("lower_lines"))
                act.wait_ge(sem("exponents"), u + 1)
                do(A(U[0:TP, :, :], U[0:TP, :, :], ACT.Exp), sem("exps"))
                act.wait_ge(sem("P_ready"), u + 1)
                if u >= 2:
                    agg_done(act, u - 2)
                do(A(Pm[u % 2][0][0:TP, :, :], U[0:TP, :, :], ACT.Copy), sem("P_high"))

            act.wait_ge(sem("coef_cols"), 1)
            for h in range(H1):
                if h == 0:
                    scores(0, 0)
                for t in range(T):
                    high(("h1", h, t), Hh[0][0:TP, t, :], lambda b: b[0:TP, :])
                for c in range(NC):
                    u = h * NC + c
                    if u + 1 < H1 * NC:
                        scores(u + 1, (u + 1) // NC)
                    for f in range(FC):
                        n = u * FC + f
                        act.wait_ge(sem("elu_in"), n + 1)
                        do(A(elu_m[:, :], elu_m[:, :], ACT.Exp))
                        do(A(elu_r[:, :], elu_z[:, :], ACT.Relu, bias=b1c[:, h * FC + f:h * FC + f + 1]), sem("elu_parts"))
            act.wait_ge(sem("coef_cols"), 2)
            for c in range(NC):
                scores(H1 * NC + c, 0)
            root(2)
            root(3)
            turned("m0")
            act.wait_ge(sem("shifted0"), 1)
            do(A(G2[0:TP, :, :], G0[0:TP, :, :], ACT.Exp), sem("exp0"))
            for e in range(0, E0, 2):
                for i in range(2):
                    filled(act, "einT", e, i)
                    do(A(einT[:, 3 * i:3 * i + 3, :], bank("einT", e, i)[:, 0:384].rearrange("p (k n) -> p k n", k=3), ACT.Copy), freed("einT", e, i))
                for d in range(2):
                    filled(act, "eh", e + d)
                    do(A(hE[d], bank("eh", e + d)[:, 0:192].rearrange("p (k n) -> p k n", k=3), ACT.Relu), freed("eh", e + d))
            root(4)
            turned("x2")
            for t in range(T):
                for i in range(2):
                    high(("gcnh", t, i), gH[t][0][0:TP, i * HALF:(i + 1) * HALF], lambda b: b[0:TP, 0:HALF], scale=dinv[0:TP, t:t + 1])
            root(5)
            turned("hn")
            for t in range(T):
                act.wait_ge(sem("k_sums"), t + 1)
                do(A(small[0:TP, t:t + 1], small[0:TP, t:t + 1], ACT.Sqrt), sem("k_norms"))
            for t in range(T):
                act.wait_ge(sem("q_sums"), t + 1)
                do(A(small[0:TP, 10 + t:11 + t], small[0:TP, 10 + t:11 + t], ACT.Sqrt), sem("q_norms"))
            root(6)
            turned("on")
            root(7)
            turned("m1")
            act.wait_ge(sem("shifted1"), 1)
            do(A(L2[0:TP, :, :], L0[0:TP, :, :], ACT.Exp), sem("exp1"))
            act.wait_ge(sem("in_b1E"), 16 * E1)

            def block_T():
                for i in range(2):
                    ins = A(xbT[:, 3 * i:3 * i + 3, :], PS[i][:, 0:384].rearrange("p (k n) -> p k n", k=3), ACT.Copy)
                ins.then_inc(sem("block_T_ready"), 1)

            act.wait_ge(sem("block_turned"), 1)
            block_T()
            act.wait_ge(sem("blocks_known"), 1)
            for e in range(E1):
                b0 = act.value_load(first_i[0:1, e:e + 1], min_val=e, max_val=MAXB - 1)
                b1_ = act.value_load(first_i[0:1, e + 1:e + 2], min_val=e + 1, max_val=MAXB)
                with act.Fori(b0, b1_) as b:
                    act.wait_ge(sem("block_h"), b + 1)
                    for f in range(F0C):
                        ins = A(hB[:, f, :], PS[2][:, f * BLK:(f + 1) * BLK], ACT.Silu, bias=b1E[:, e, f:f + 1])
                    ins.then_inc(sem("block_h_ready"), 1)
                    act.wait_ge(sem("block_turned"), b + 2)
                    block_T()
                    act.wait_ge(sem("block_out_emptied"), b + 2)
                    act.dma_start(scr_out1[bass.ds(b * BLK, BLK), :], oB).then_inc(sem("block_stored"), 16)

        @block.gpsimd
        def _(pool):
            do = Steps(pool, own_g)
            g = nc.gpsimd
            do(g.memset(ones, 1.0), sem("consts"))
            do(g.memset(ident, 0.0))
            do.settle()
            do(g.affine_select(out=ident, in_=ident, compare_op=ALU.not_equal, fill=1.0, base=0, pattern=[[-1, 128]], channel_multiplier=1), sem("consts"))
            do(g.memset(upto, 1.0))
            do.settle()
            do(g.affine_select(out=upto, in_=upto, compare_op=ALU.is_ge, fill=0.0, base=0, pattern=[[1, 128]], channel_multiplier=-1), sem("consts"))
            do(g.memset(rfn, 0.0), sem("pads"))
            do(g.memset(kvpad[0], 0.0))
            do(g.memset(kvpad[1], 0.0), sem("pads"))
            next_piece = [0]

            def split_pieces(*names):
                for name in names:
                    while next_piece[0] < len(pieces) and pieces[next_piece[0]][0] == name:
                        n = next_piece[0]
                        next_piece[0] += 1
                        _, a, (hi, lo), stage, place = pieces[n]
                        if n in piece_after:
                            filled(pool, *piece_after[n])
                        pool.wait_ge(sem(f"weight_in_{place[0]}{place[1]}"), 16 * len([1 for p in pieces[:n + 1] if p[4] == place]))
                        v = shaped(stage, a)
                        do(g.tensor_copy(hi, v))
                        do.settle()
                        do(g.tensor_tensor(lo, v, hi, ALU.subtract), sem("weights_split"))

            split_pieces("Wv", ("Wqk", 0), "Wp", *[("Wqk", p) for p in range(1, MH // 2)])
            pool.wait_ge(sem("in_bias"), 32)
            for t in range(T):
                all_emptied(pool, "proj", t, 1)
                do(g.tensor_tensor(R1[0:TP, t, :], R1[0:TP, t, :], bias_rows[0:TP, 0, :], ALU.add))
                do.settle()
                do(g.tensor_tensor(R1[0:TP, t, :], R1[0:TP, t, :], bias_rows[0:TP, 1, :], ALU.add), sem("bias_added"))
            pool.wait_ge(sem("in_edges"), 32)
            do(g.iota(iota_i, [[1, 500]], base=0, channel_multiplier=0), sem("iotas"))
            do(g.iota(iota_c_i, [[0, 1]], base=0, channel_multiplier=WIN), sem("iotas"))
            do(g.memset(upper, 1.0))
            do.settle()
            do(g.affine_select(out=upper, in_=upper, compare_op=ALU.is_ge, fill=0.0, base=-1, pattern=[[1, 32]], channel_multiplier=-1), sem("iotas"))
            do(g.memset(zero_bf, 0.0), sem("iota_set"))

            def sums(u):
                pool.wait_ge(sem("P_ready"), u + 1)
                if u >= 2:
                    agg_done(pool, u - 2)
                S = Sp[u % 2]
                pool.wait_ge(sem("P_high"), u + 1)
                do(g.tensor_tensor(Pm[u % 2][1][0:TP, :, :], U[0:TP, :, :], Pm[u % 2][0][0:TP, :, :], ALU.subtract), sem("P_low"))
                do(g.tensor_tensor(S[0:TP, :], U[0:TP, 0, :], U[0:TP, 1, :], ALU.add))
                for t in range(2, T):
                    do.settle()
                    do(g.tensor_tensor(S[0:TP, :], S[0:TP, :], U[0:TP, t, :], ALU.add), sem("P_sums") if t == T - 1 else None)

            split_pieces(("W1h", 0), ("W2h", 0))
            for u in range(H1 * NC):
                sums(u)
                h = u // NC
                if u % NC == 1 and h + 1 < H1:
                    split_pieces(("W1h", h + 1))
                if u % NC == 0 and h:
                    split_pieces(("W2h", h))
            for c in range(NC):
                sums(H1 * NC + c)
            all_emptied(pool, "agg2", T - 1, 1)
            do(g.memset(zero_row, 0.0), sem("zeros_set"))
            split_pieces("router")
            do(g.iota(e_i, [[0, T], [-1, E0]], base=E0, channel_multiplier=0), sem("iotas"))
            for t in range(T):
                pool.wait_ge(sem("y_rows"), t + 1)
                do(g.tensor_tensor(R1[0:TP, t, :], R1[0:TP, t, :], R2[0:TP, t, :], ALU.add), sem("y_added"))
            pool.wait_ge(sem("slots"), 1)
            pool.wait_ge(sem("slots_zeroed"), 16 * (SLOTS // 128))
            for t in range(T):
                g.indirect_dma_start(scr_in, bass.IndirectOffsetOnAxis(ap=slot_s[0:TP, t:t + 1], axis=0), R2[0:TP, t, :], None,
                                     bounds_check=SLOTS - 1, oob_is_err=False).then_inc(sem("scattered"), 16)
            for i in range(2 * T):
                do(g.tensor_copy(ct_tmp[0:TP, :], CTt[0:TP, i * N // 2:(i + 1) * N // 2]))
                do.settle()
                do(g.tensor_copy(CT2[i][0][0:TP, :], ct_tmp[0:TP, :]))
                do.settle()
                do(g.tensor_tensor(CT2[i][1][0:TP, :], ct_tmp[0:TP, :], CT2[i][0][0:TP, :], ALU.subtract), sem("counts_split"))
                do.settle()
            for e in range(E0):
                for i in range(2):
                    emptied(pool, "eo", e, i)
                pool.dma_start(scr_out[e * CAP:(e + 1) * CAP, :], oE[e % 2][0:CAP, :]).then_inc(sem(f"out_kept{e % 2}"), 16)
            pool.wait_ge(sem("out_kept0"), 16 * E0 // 2)
            pool.wait_ge(sem("out_kept1"), 16 * E0 // 2)
            filled(pool, "eo", E0 - 1, 1)
            for t in range(T):
                if t >= 2:
                    pool.wait_ge(sem("gathered_used"), t - 1)
                g.indirect_dma_start(gath[t % 2][0:TP, :], None, scr_out, bass.IndirectOffsetOnAxis(ap=slot_g[0:TP, t:t + 1], axis=0),
                                     bounds_check=SLOTS - 1, oob_is_err=False).then_inc(sem(f"gathered{t % 2}"), 16)
            split_pieces("gW", "wk", "wv", "wq", "wpr")
            all_emptied(pool, "mproj", T - 1, 1)
            do(g.iota(e1_i, [[0, T], [-1, E1]], base=E1, channel_multiplier=0), sem("iotas"))
            do(g.memset(zero1, 0.0), sem("zeros1_set"))
            do(g.memset(tick, 0.0))
            do.settle()
            split_pieces("wg")
            for e in range(2):
                pool.dma_start(w1E[e], kchunks(F1w[e])).then_inc(sem(f"in_fe{e}"), 16)
                pool.dma_start(w2E[e], kchunks(F2w[e])).then_inc(sem(f"in_fe{e}"), 16)
            pool.wait_ge(sem("slots1"), 1)
            pool.wait_ge(sem("blocks_zeroed"), 16 * (MAXB + 1 + MAXB - MINB))
            for t in range(T):
                g.indirect_dma_start(scr_in1, bass.IndirectOffsetOnAxis(ap=slot1[0:TP, t:t + 1], axis=0), R2[0:TP, t, :], None,
                                     bounds_check=MAXB * BLK - 1, oob_is_err=False).then_inc(sem("scattered1"), 16)
            for e in range(2, E1):
                done = pool.value_load(first_i[0:1, e - 1:e], min_val=e - 1, max_val=MAXB)
                pool.wait_ge(sem("block_out"), done)
                do(g.tensor_tensor(tick, tick, tick, ALU.add))
                do.settle()
                pool.dma_start(w1E[e % 2], kchunks(F1w[e])).then_inc(sem(f"in_fe{e % 2}"), 16)
                pool.dma_start(w2E[e % 2], kchunks(F2w[e])).then_inc(sem(f"in_fe{e % 2}"), 16)
            blocks = pool.value_load(first_i[0:1, E1:E1 + 1], min_val=E1, max_val=MAXB)
            pool.wait_ge(sem("block_stored"), blocks * 16 + 16)
            do(g.tensor_tensor(tick, tick, tick, ALU.add))
            do.settle()
            for t in range(T):
                if t >= 2:
                    pool.wait_ge(sem("out_rows"), t - 1)
                g.indirect_dma_start(gath1[t % 2][0:TP, :], None, scr_out1, bass.IndirectOffsetOnAxis(ap=slot1[0:TP, t:t + 1], axis=0),
                                     bounds_check=MAXB * BLK - 1, oob_is_err=False).then_inc(sem(f"in_gath{t % 2}"), 16)

        @block.vector
        def _(v):
            do = Steps(v, own_v)
            V = nc.vector

            def norm_rows(source, at, eps, rows_sem, rms=False, scale_row=None, ready=None, extra=None):
                for t in range(T):
                    if ready:
                        ready(t)
                    for i in range(2):
                        do(V.bn_stats(stat[0:TP, t, 6 * i:6 * i + 6], source[0:TP, t, i * HALF:(i + 1) * HALF]))
                    do.settle()
                    do(V.bn_aggr(mv[0:TP, t, :], stat[0:TP, t, :]))
                do.settle()
                if rms:
                    do(V.tensor_tensor(rstd[0:TP, :], mv[0:TP, :, 0], mv[0:TP, :, 0], ALU.mult))
                    do.settle()
                    do(V.tensor_tensor(rstd[0:TP, :], rstd[0:TP, :], mv[0:TP, :, 1], ALU.add))
                    do.settle()
                    do(V.tensor_scalar(rstd[0:TP, :], rstd[0:TP, :], eps, None, ALU.add), sem("variances"))
                else:
                    do(V.tensor_scalar(rstd[0:TP, :], mv[0:TP, :, 1], eps, None, ALU.add), sem("variances"))
                v.wait_ge(sem("roots"), at)
                do(V.reciprocal(rstd[0:TP, :], rstd[0:TP, :]))
                do.settle()
                for t in range(T):
                    if rms:
                        v.wait_ge(sem("y_added"), t + 1)
                        do(V.scalar_tensor_tensor(R2[0:TP, t, :], R2[0:TP, t, :], rstd[0:TP, t:t + 1], scale_row, ALU.mult, ALU.mult), rows_sem)
                    elif extra:
                        do(V.tensor_scalar(R2[0:TP, t, :], source[0:TP, t, :], mv[0:TP, t, 0:1], rstd[0:TP, t:t + 1], ALU.subtract, ALU.mult))
                        do.settle()
                        do(V.tensor_tensor(R2[0:TP, t, :], R2[0:TP, t, :], extra[0:TP, 0, :], ALU.mult))
                        do.settle()
                        do(V.tensor_tensor(R2[0:TP, t, :], R2[0:TP, t, :], extra[0:TP, 1, :], ALU.add), rows_sem)
                    else:
                        do(V.tensor_scalar(R2[0:TP, t, :], source[0:TP, t, :], mv[0:TP, t, 0:1], rstd[0:TP, t:t + 1], ALU.subtract, ALU.mult), rows_sem)

            def low(key, o, view, hi, scalar=None, op=None):
                v.wait_ge(sem("high_made"), SPLIT[key] + 1)
                b = view(bank(*key))
                if op is None:
                    do(V.tensor_tensor(o, b, hi, ALU.subtract), freed(*key))
                else:
                    do(V.scalar_tensor_tensor(o, b, scalar, hi, op, ALU.subtract), freed(*key))

            def turned_low(name):
                for t in range(T):
                    for i in range(2):
                        o, hi = (r[:, 3 * i:3 * i + 3, t * TP:(t + 1) * TP] for r in (RT[1], RT[0]))
                        low(("T", name, t, i), o, turned_bank, hi)

            norm_rows(R1, 1, 1e-5, sem("xn_rows"), ready=lambda t: v.wait_ge(sem(f"in_x{t}"), 16))
            turned_low("xn")
            v.wait_ge(sem("in_bv"), 16)
            filled(v, "T", "xn", T - 1, 1)
            for t in range(T):
                for i in range(2):
                    filled(v, "v", t, i)
                    c = slice(i * HALF, (i + 1) * HALF)
                    do(V.tensor_tensor(v_tmp[0:TP, :], bank("v", t, i)[0:TP, 0:HALF], bv_row[0:TP, c], ALU.add), freed("v", t, i))
                    do.settle()
                    do(V.tensor_copy(Vr[t][0][0:TP, c], v_tmp[0:TP, :]))
                    do.settle()
                    do(V.tensor_tensor(Vr[t][1][0:TP, c], v_tmp[0:TP, :], Vr[t][0][0:TP, c], ALU.subtract), sem("v_split"))
                    do.settle()
            low(("rfT",), rfp[1], lambda b: b.rearrange("p (s m) -> p s m", s=2), rfp[0])
            for p in range(MH // 2):
                for w, name in enumerate("qk"):
                    for c, (c0, cn) in enumerate(COLS):
                        q2 = (qT, kT)[w]
                        low((name, p, c), q2[1][:, c0:c0 + cn], lambda b: b[:, 0:cn], q2[0][:, c0:c0 + cn], bqk[:, w * 6 + p:w * 6 + p + 1], ALU.add)
                for s in range(2):
                    for m in range(2):
                        for c, (c0, cn) in enumerate(COLS):
                            low(("phiq", p, s, m, c), PQ[1][:, s, m, c0:c0 + cn], lambda b: b[:, 0:cn], PQ[0][:, s, m, c0:c0 + cn], 0.0, ALU.max)
                    for i in range(T // 2):
                        low(("phik", p, s, i), PK[1][0:TP, s, 2 * i:2 * i + 2, :], phik_bank, PK[0][0:TP, s, 2 * i:2 * i + 2, :], 0.0, ALU.max)
                for s in range(2):
                    if p + s == 0:
                        v.wait_ge(sem("pads"), 2)
                    low(("kv", p, s), kvpad[1][:, s, :, s * MD:(s + 1) * MD], kv_bank, kvpad[0][:, s, :, s * MD:(s + 1) * MD], KV_SCALE, ALU.mult)
                for c, (c0, cn) in enumerate(COLS):
                    low(("at", p, c), ATt[1][:, p, c0:c0 + cn], lambda b: b[:, 0:cn], ATt[0][:, p, c0:c0 + cn])
            for t in range(T):
                for i in range(2):
                    filled(v, "proj", t, i)
                    do(V.tensor_tensor(R1[0:TP, t, i * HALF:(i + 1) * HALF], R1[0:TP, t, i * HALF:(i + 1) * HALF], bank("proj", t, i)[0:TP, 0:HALF], ALU.add), freed("proj", t, i))

            v.wait_ge(sem("bias_added"), T)
            v.wait_ge(sem("in_edges"), 32)
            do(V.tensor_copy(nat, nat_i))
            do.settle()
            do(V.tensor_scalar(tdiv, nat[:, 0, :], float(TP), None, ALU.is_ge))
            for m in range(2, T):
                do.settle()
                do(V.scalar_tensor_tensor(tdiv, nat[:, 0, :], float(TP * m), tdiv, ALU.is_ge, ALU.add))
            do.settle()
            do(V.scalar_tensor_tensor(keys[:, 0, :], nat[:, 1, :], float(T), tdiv, ALU.mult, ALU.add))
            do(V.scalar_tensor_tensor(keys[:, 1, :], tdiv, -float(TP), nat[:, 0, :], ALU.mult, ALU.add))
            do(V.tensor_reduce(gmm[:, 0:1], nat[:, 1, :], AX, ALU.min))
            do(V.tensor_reduce(gmm[:, 1:2], nat[:, 1, :], AX, ALU.max), sem("edge_keys"))
            v.wait_ge(sem("iotas"), 3)
            do(V.tensor_copy(iota, iota_i))
            do(V.tensor_copy(iota16, iota_i))
            do(V.tensor_copy(iota_c[:, 0:1], iota_c_i))
            for a in range(2):
                filled(v, "edgeT", a)
                do(V.tensor_copy(KL[0:TP, a, :, :], bank("edgeT", a)[0:TP, 0:320].rearrange("p (q g) -> p q g", q=QG)), freed("edgeT", a))
            do.settle()
            do(V.tensor_scalar(iota_c[:, 1:2], iota_c[:, 0:1], float(WIN), None, ALU.add))
            filled(v, "groupB")
            do.settle()
            ps = bank("groupB")
            do(V.tensor_scalar(cutI, ps[0:NW, 0:NG], iota_c[0:NW, 1:2], None, ALU.is_lt))
            do.settle()
            do(V.scalar_tensor_tensor(cutI, ps[0:NW, NG:2 * NG], iota_c[0:NW, 0:1], cutI, ALU.is_ge, ALU.mult), freed("groupB"))
            do(V.tensor_scalar(cutJ, iota[0:NW, 0:NG], -1.0, float(NG - 1), ALU.mult, ALU.add))
            do.settle()
            do(V.tensor_tensor(cutJ, cutJ, cutI, ALU.mult))
            do(V.scalar_tensor_tensor(cutK, iota[0:NW, 0:NG], 1.0, cutI, ALU.add, ALU.mult))
            do.settle()
            do(V.tensor_reduce(tab[:, 3:4], cutJ, AX, ALU.max))
            do(V.tensor_reduce(tab[:, 4:5], cutK, AX, ALU.max))
            do.settle()
            do(V.tensor_scalar(tab[:, 0:1], tab[:, 3:4], -1.0, float(NG - 1), ALU.mult, ALU.add))
            do.settle()
            do(V.scalar_tensor_tensor(tab[:, 1:2], tab[:, 0:1], 1.0, tab[:, 4:5], ALU.add, ALU.max))
            do.settle()
            do(V.tensor_tensor(tab[:, 2:3], tab[:, 1:2], tab[:, 0:1], ALU.subtract), sem("window_cols"))
            filled(v, "tables")
            ps = bank("tables")
            do(V.tensor_copy(trow_i[:, 0:2 * NW], ps[0:1, 0:2 * NW]))
            do(V.tensor_scalar(trow[:, 0:NW], ps[0:1, 0:NW], -2.0, float(BIAS), ALU.mult, ALU.add))
            do.settle()
            do(V.scalar_tensor_tensor(trow_i[:, 2 * NW:3 * NW], ps[0:1, 2 * NW:3 * NW], 2.0, trow[:, 0:NW], ALU.mult, ALU.add), freed("tables"))
            do.settle()
            do(V.tensor_copy(tab[0:1, 5:6], tab[0:1, 4:5]), sem("window_table"))
            v.sem_inc(sem("onehots_ready"), BIAS)
            for w in range(NW):
                g0 = v.value_load(trow_i[0:1, w:w + 1], min_val=0, max_val=NG - 1)
                g1 = v.value_load(trow_i[0:1, NW + w:NW + w + 1], min_val=1, max_val=NG)
                base = v.value_load(trow_i[0:1, 2 * NW + w:2 * NW + w + 1], min_val=0, max_val=2 * NG * NW + BIAS)
                if w:
                    do(V.tensor_copy(tab[0:1, 5:6], tab[0:1, 4:5]))
                    do.settle()
                    do(V.tensor_scalar(KL[0:TP, 0, :, :], KL[0:TP, 0, :, :], -float(WIN * T), None, ALU.add))
                do.settle()
                with v.Fori(g0, g1) as g:
                    for half in range(2):
                        v.wait_ge(sem("onehots_used"), base + g * 2 + (half + 1))
                        for q in range(2 * half, 2 * half + 2):
                            V.tensor_scalar(oh_lo[q][0:TP, 0:TP], iota16[0:TP, 0:TP], KL[0:TP, 1, q, bass.ds(g, 1)], None, ALU.is_equal)
                            ins = V.tensor_scalar(oh_key[q][0:TP, 0:500], iota16[0:TP, 0:500], KL[0:TP, 0, q, bass.ds(g, 1)], None, ALU.is_equal)
                        ins.then_inc(sem("onehots_ready"), 1)
            v.wait_ge(sem("window_emptied"), NW)
            for t in range(T):
                do(V.tensor_tensor(CT[0:TP, t, t * TP:(t + 1) * TP], CT[0:TP, t, t * TP:(t + 1) * TP], ident[0:TP, 0:TP], ALU.add))
            do.settle()
            do(V.tensor_reduce(degp[0:TP, :], CT[0:TP, :, :].rearrange("p t n -> p n t"), AX, ALU.add), sem("deg_parts"))
            filled(v, "deg")
            do(V.tensor_copy(dinv[0:TP, :], bank("deg")[0:TP, 0:T]), sem("deg_copied"))
            v.wait_ge(sem("deg_root"), 1)
            do(V.reciprocal(dinv[0:TP, :], dinv[0:TP, :]), freed("deg"))

            v.wait_ge(sem("in_a1"), 32)
            for h in range(H1):
                v.wait_ge(sem(f"in_W1s{h % 2}"), 16 * (h // 2 + 1))
                for k in range(KD):
                    for a in range(2):
                        if k + a or h:
                            do.settle()
                        do(V.tensor_tensor_reduce(junk[:, 0:HID], W1s[h % 2][:, k, :], arow[:, a, h * HID:(h + 1) * HID], 1.0, 0.0,
                                                  ALU.mult, ALU.add, wa[:, k, 4 * a + h:4 * a + h + 1]), sem("W1_folded") if k == KD - 1 and a else None)
            do.settle()
            do(V.tensor_copy(wa2[0], wa))
            do.settle()
            do(V.tensor_tensor(wa2[1], wa, wa2[0], ALU.subtract), sem("fold_split"))
            filled(v, "coef1")
            do(V.tensor_copy(AS[0:TP, :, :], bank("coef1")[0:TP, 0:80].rearrange("p (t n) -> p t n", t=T)))
            do(V.tensor_scalar(AS2[0:TP, :, :], bank("coef1")[0:TP, 0:80].rearrange("p (t n) -> p t n", t=T), 0.2, None, ALU.mult), freed("coef1"))
            do.settle()

            def neighbour_max(acc, mask, cols):
                for t in range(T):
                    do(V.tensor_scalar(mask[0:TP, :], CT[0:TP, t, :], 0.0, -BIG, ALU.is_equal, ALU.mult))
                    do.settle()
                    for a, col in zip(acc, cols):
                        if t == 0:
                            do(V.tensor_scalar(a[0:TP, :], mask[0:TP, :], AS[0:TP, t, col:col + 1], None, ALU.add))
                        else:
                            do(V.scalar_tensor_tensor(a[0:TP, :], mask[0:TP, :], AS[0:TP, t, col:col + 1], a[0:TP, :], ALU.add, ALU.max))
                    do.settle()

            def coef_columns(h, key, dcol):
                for i in range(3):
                    filled(v, *key, i)
                    n = min(4, T - 4 * i)
                    do(V.tensor_reduce(Mx[0:TP, h, 4 * i:4 * i + n], bank(*key, i)[0:TP, 0:n * TP].rearrange("p (t n) -> p t n", t=n), AX, ALU.max), freed(*key, i))
                do.settle()
                do(V.tensor_tensor(Mx[0:TP, h, :], Mx[0:TP, h, :], AS[0:TP, :, dcol], ALU.add))
                do.settle()
                do(V.scalar_tensor_tensor(Mx[0:TP, h, :], Mx[0:TP, h, :], 0.2, Mx[0:TP, h, :], ALU.mult, ALU.max))
                do.settle()
                do(V.tensor_tensor(Ac[0:TP, h, :], AS[0:TP, :, dcol], Mx[0:TP, h, :], ALU.subtract))
                return do(V.tensor_tensor(Bc[0:TP, h, :], AS2[0:TP, :, dcol], Mx[0:TP, h, :], ALU.subtract))

            neighbour_max([maxacc[:, h, :] for h in range(H1)], maskt, range(H1))
            do(V.tensor_copy(small[0:TP, 0:1], AS[0:TP, 0, 0:1]), sem("max_rows"))
            for h in range(H1):
                coef_columns(h, ("max1", h), 4 + h)
            do.settle()
            do(V.tensor_copy(small[0:TP, 0:1], AS[0:TP, 0, 0:1]), sem("coef_cols"))

            def weights(u, col):
                ps = PS[6 + u % 2]
                v.wait_ge(sem("lower_lines"), (u + 1) * T)
                for t in range(T):
                    s = sem("exponents") if t == T - 1 else None
                    do(V.scalar_tensor_tensor(U[0:TP, t, :], ps[0:TP, 0:IC], AS[0:TP, t, col:col + 1], U[0:TP, t, :], ALU.add, ALU.max), s)
                do(V.tensor_copy(small[0:TP, 1:2], small[0:TP, 0:1]), sem("coef_used"))
                v.wait_ge(sem("exps"), u + 1)
                c = u % NC
                do(V.scalar_tensor_tensor(U[0:TP, :, :], U[0:TP, :, :], 1.0, CT[0:TP, :, c * IC:(c + 1) * IC], ALU.min, ALU.mult), sem("P_ready"))

            def elu(h, c, f):
                u = h * NC + c
                n = u * FC + f
                filled(v, "agg1", h, c, f)
                if n:
                    v.wait_ge(sem("elu_parts"), n)
                do(V.tensor_tensor(elu_z[:, :], bank("agg1", h, c, f)[:, 0:IC], rden[u % 2][:, :], ALU.mult), freed("agg1", h, c, f))
                do.settle()
                do(V.tensor_scalar(elu_m[:, :], elu_z[:, :], b1c[:, h * FC + f:h * FC + f + 1], 0.0, ALU.add, ALU.min), sem("elu_in"))
                v.wait_ge(sem("elu_parts"), n + 1)
                do(V.scalar_tensor_tensor(elu_z[:, :], elu_m[:, :], -1.0, elu_r[:, :], ALU.add, ALU.add))
                do.settle()
                do(V.tensor_copy(H1T[u % 2][0][:, f, :], elu_z[:, :]))
                do.settle()
                do(V.tensor_tensor(H1T[u % 2][1][:, f, :], elu_z[:, :], H1T[u % 2][0][:, f, :], ALU.subtract), sem("elu_done"))
                do.settle()

            def w2_rows(h, c):
                for t in range(c * TC, (c + 1) * TC):
                    for i in range(2):
                        filled(v, "w2", h, t, i)
                        o, ps = R2[0:TP, t, i * HALF:(i + 1) * HALF], bank("w2", h, t, i)[0:TP, 0:HALF]
                        if h == 0:
                            do(V.tensor_copy(o, ps), freed("w2", h, t, i))
                        else:
                            do(V.tensor_tensor(o, o, ps, ALU.add), freed("w2", h, t, i))

            v.wait_ge(sem("in_b1"), 16)
            weights(0, 0)
            for h in range(H1):
                for t in range(T):
                    low(("h1", h, t), Hh[1][0:TP, t, :], lambda b: b[0:TP, :], Hh[0][0:TP, t, :])
                for c in range(NC):
                    u = h * NC + c
                    if u + 1 < H1 * NC:
                        weights(u + 1, (u + 1) // NC)
                    filled(v, "den1", h, c)
                    do(V.tensor_scalar(rden[u % 2][:, :], bank("den1", h, c)[:, 0:IC], 1e-16, None, ALU.add), freed("den1", h, c))
                    do.settle()
                    do(V.reciprocal(rden[u % 2][:, :], rden[u % 2][:, :]))
                    do.settle()
                    for f in range(FC):
                        elu(h, c, f)
                    if c:
                        w2_rows(h, c - 1)
                w2_rows(h, NC - 1)

            v.wait_ge(sem("in_a2"), 32)
            for t in range(T):
                for a in range(2):
                    do.settle()
                    do(V.tensor_tensor_reduce(junk2[0:TP, :], R2[0:TP, t, :], a2row[0:TP, a, :], 1.0, 0.0, ALU.mult, ALU.add, AS[0:TP, t, 4 * a:4 * a + 1]))
            do.settle()
            do(V.tensor_scalar(AS2[0:TP, :, :], AS[0:TP, :, :], 0.2, None, ALU.mult))
            do.settle()
            for t in range(T):
                tmp = h2_tmp[t % 2][0:TP, :]
                do(V.tensor_copy(tmp, R2[0:TP, t, :]))
                do.settle()
                do(V.tensor_copy(H2[t][0][0:TP, :], tmp))
                do.settle()
                do(V.tensor_tensor(H2[t][1][0:TP, :], tmp, H2[t][0][0:TP, :], ALU.subtract), sem("h2_split"))
            do.settle()
            neighbour_max([max2a], mask2, [0])
            do(V.tensor_copy(small[0:TP, 0:1], AS[0:TP, 0, 0:1]), sem("max_rows"))
            coef_columns(0, ("max2",), 4)
            do.settle()
            do(V.tensor_copy(small[0:TP, 0:1], AS[0:TP, 0, 0:1]), sem("coef_cols"))
            v.wait_ge(sem("xm_back"), 16)
            weights(H1 * NC, 0)
            for c in range(NC):
                if c + 1 < NC:
                    weights(H1 * NC + c + 1, 0)
                filled(v, "den2", c)
                do(V.tensor_scalar(rd2[0:TP, :], bank("den2", c)[0:TP, 0:TC], 1e-16, None, ALU.add), freed("den2", c))
                do.settle()
                do(V.reciprocal(rd2[0:TP, :], rd2[0:TP, :]))
                do.settle()
                for t in range(TC):
                    for i in range(2):
                        tt = c * TC + t
                        filled(v, "agg2", tt, i)
                        o = R1[0:TP, tt, i * HALF:(i + 1) * HALF]
                        do(V.scalar_tensor_tensor(o, bank("agg2", tt, i)[0:TP, 0:HALF], rd2[0:TP, t:t + 1], o, ALU.mult, ALU.add), freed("agg2", tt, i))
                do.settle()

            norm_rows(R1, 2, 1e-5, sem("y_rows"))
            do.settle()
            v.wait_ge(sem("in_lnw"), 16)
            norm_rows(R2, 3, 1e-6, sem("normed_rows"), rms=True, scale_row=lnw_row[0:TP, :])
            turned_low("m0")
            filled(v, "logits0")
            lg = bank("logits0")[0:TP, 0:160].rearrange("p (t e) -> p t e", t=T)

            def wide(col, n):
                return col.unsqueeze(2).to_broadcast([TP, T, n])

            g0, g1_, g2, g3 = (a[0:TP] for a in (G0, G1, G2, G3))
            eb, es, gc = ebase[0:TP], esort[0:TP], gcol[0:TP]
            do(V.tensor_copy(g3, lg), freed("logits0"))
            do.settle()
            do(V.tensor_reduce(gc[:, 0, :], g3, AX, ALU.max))
            v.wait_ge(sem("iotas"), 4)
            do(V.tensor_copy(es, e_i[0:TP].rearrange("p (t e) -> p t e", t=T)))
            do.settle()
            do(V.tensor_tensor(g0, g3, wide(gc[:, 0, :], E0), ALU.subtract), sem("shifted0"))
            do(V.tensor_scalar(eb, es, -float(CAP), float(CAP * E0), ALU.mult, ALU.add))
            do(V.tensor_tensor(g1_, g3, wide(gc[:, 0, :], E0), ALU.is_equal))
            do.settle()
            do(V.tensor_tensor(g1_, g1_, es, ALU.mult))
            do.settle()
            do(V.tensor_reduce(gc[:, 1, :], g1_, AX, ALU.max))
            do.settle()
            do(V.tensor_tensor(g1_, es, wide(gc[:, 1, :], E0), ALU.is_equal), sem("onehot0"))
            v.wait_ge(sem("exp0"), 1)
            do(V.tensor_reduce(gc[:, 2, :], g2, AX, ALU.add))
            do.settle()
            do(V.reciprocal(gc[:, 3, :], gc[:, 2, :]))
            filled(v, "order0")
            ps = bank("order0")
            do(V.memset(g0[:, 0, :], 0.0))
            for t in range(1, T):
                do.settle()
                do(V.tensor_tensor(g0[:, t, :], g0[:, t - 1, :], ps[0:TP, 160 + (t - 1) * E0:160 + t * E0], ALU.add))
            do.settle()
            do(V.tensor_tensor(g3, g0, ps[0:TP, 0:160].rearrange("p (t e) -> p t e", t=T), ALU.add), freed("order0"))
            do.settle()
            do(V.tensor_tensor(g3, g3, g1_, ALU.mult))
            do(V.tensor_tensor(g2, eb, g1_, ALU.mult))
            do.settle()
            do(V.tensor_reduce(gc[:, 4, :], g3, AX, ALU.add))
            do(V.tensor_reduce(gc[:, 5, :], g2, AX, ALU.add))
            do.settle()
            do(V.tensor_scalar(gc[:, 6, :], gc[:, 4, :], float(CAP), None, ALU.is_le))
            do(V.scalar_tensor_tensor(gc[:, 7, :], gc[:, 4, :], -1.0, gc[:, 5, :], ALU.add, ALU.add))
            do.settle()
            do(V.tensor_scalar(gc[:, 8, :], gc[:, 6, :], -1.0, 1.0, ALU.mult, ALU.add))
            do(V.tensor_tensor(gc[:, 9, :], gc[:, 7, :], gc[:, 6, :], ALU.mult))
            do(V.tensor_tensor(gc[:, 10, :], gc[:, 6, :], gc[:, 3, :], ALU.mult))
            do.settle()
            do(V.scalar_tensor_tensor(gc[:, 7, :], gc[:, 8, :], float(4 * SLOTS), gc[:, 9, :], ALU.mult, ALU.add))
            do(V.tensor_tensor(gc[:, 11, :], gc[:, 8, :], gc[:, 3, :], ALU.mult))
            do.settle()
            do(V.tensor_copy(slot_g[0:TP, :], gc[:, 9, :]))
            do(V.tensor_copy(slot_s[0:TP, :], gc[:, 7, :]), sem("slots"))
            v.wait_ge(sem("scattered"), 16 * T)
            for t in range(T):
                do(V.scalar_tensor_tensor(R1[0:TP, t, :], R2[0:TP, t, :], gc[:, 11, t:t + 1], R1[0:TP, t, :], ALU.mult, ALU.add))
            for e in range(E0):
                if e >= 2:
                    v.wait_ge(sem(f"out_kept{e % 2}"), 16 * (e // 2))
                for i in range(2):
                    filled(v, "eo", e, i)
                    do(V.tensor_copy(oE[e % 2][0:CAP, i * HALF:(i + 1) * HALF], bank("eo", e, i)[0:CAP, 0:HALF]), freed("eo", e, i))
            do.settle()
            for t in range(T):
                v.wait_ge(sem(f"gathered{t % 2}"), 16 * (t // 2 + 1))
                do(V.scalar_tensor_tensor(R1[0:TP, t, :], gath[t % 2][0:TP, :], gc[:, 10, t:t + 1], R1[0:TP, t, :], ALU.mult, ALU.add), sem("gathered_used"))
            do.settle()
            do(V.tensor_copy(small[0:TP, 0:1], small[0:TP, 1:2]), sem("switch_done"))

            norm_rows(R1, 4, 1e-5, sem("x2_rows"))
            turned_low("x2")
            v.wait_ge(sem("in_gb"), 16)
            for t in range(T):
                do(V.tensor_tensor(R1[0:TP, t, :], R1[0:TP, t, :], grow[0:TP, :], ALU.add))
            for t in range(T):
                for i in range(2):
                    c = slice(i * HALF, (i + 1) * HALF)
                    low(("gcnh", t, i), gH[t][1][0:TP, c], lambda b: b[0:TP, 0:HALF], gH[t][0][0:TP, c], dinv[0:TP, t:t + 1], ALU.mult)
            do.settle()
            for t in range(T):
                for i in range(2):
                    filled(v, "gcn", t, i)
                    o = R1[0:TP, t, i * HALF:(i + 1) * HALF]
                    do(V.scalar_tensor_tensor(o, bank("gcn", t, i)[0:TP, 0:HALF], dinv[0:TP, t:t + 1], o, ALU.mult, ALU.add), freed("gcn", t, i))

            v.wait_ge(sem("in_ln"), 32)
            norm_rows(R2, 5, 1e-5, sem("hn_rows"), extra=grow2)
            turned_low("hn")
            for t in range(T):
                kk = kt_[0]
                for i in range(2):
                    filled(v, "mk", t, i)
                    do(V.tensor_copy(kk[0:TP, i * HALF:(i + 1) * HALF], bank("mk", t, i)[0:TP, 0:HALF]), freed("mk", t, i))
                do.settle()
                do(V.tensor_tensor_reduce(sq_[0:TP, :], kk[0:TP, :], kk[0:TP, :], 1.0, 0.0, ALU.mult, ALU.add, small[0:TP, t:t + 1]), sem("k_sums"))
                v.wait_ge(sem("k_norms"), t + 1)
                do(V.tensor_scalar(small[0:TP, t:t + 1], small[0:TP, t:t + 1], 1e-12, None, ALU.max))
                do.settle()
                do(V.reciprocal(small[0:TP, t:t + 1], small[0:TP, t:t + 1]))
                do.settle()
                for i in range(2):
                    filled(v, "mv", t, i)
                    o = prodsum if t == 0 else psum_row
                    do(V.scalar_tensor_tensor(o[0:TP, i * HALF:(i + 1) * HALF], kk[0:TP, i * HALF:(i + 1) * HALF], small[0:TP, t:t + 1],
                                              bank("mv", t, i)[0:TP, 0:HALF], ALU.mult, ALU.mult), freed("mv", t, i))
                do.settle()
                if t:
                    do(V.tensor_tensor(prodsum[0:TP, :], prodsum[0:TP, :], psum_row[0:TP, :], ALU.add), sem("kv_rows") if t == T - 1 else None)
                    do.settle()
            for i in range(2):
                filled(v, "kvsum", i)
                do(V.tensor_copy(kvb[0:TP, i * HALF:(i + 1) * HALF], bank("kvsum", i)[0:TP, 0:HALF]), freed("kvsum", i))
            do.settle()
            filled(v, "T", "hn", T - 1, 1)
            for t in range(T):
                qq = kt_[1]
                for i in range(2):
                    filled(v, "mq", t, i)
                    do(V.tensor_copy(qq[0:TP, i * HALF:(i + 1) * HALF], bank("mq", t, i)[0:TP, 0:HALF]), freed("mq", t, i))
                do.settle()
                do(V.tensor_tensor_reduce(sq_[0:TP, :], qq[0:TP, :], qq[0:TP, :], 1.0, 0.0, ALU.mult, ALU.add, small[0:TP, 10 + t:11 + t]), sem("q_sums"))
                v.wait_ge(sem("q_norms"), t + 1)
                do(V.tensor_scalar(small[0:TP, 10 + t:11 + t], small[0:TP, 10 + t:11 + t], 1e-12, None, ALU.max))
                do.settle()
                do(V.reciprocal(small[0:TP, 10 + t:11 + t], small[0:TP, 10 + t:11 + t]))
                do.settle()
                do(V.scalar_tensor_tensor(R2[0:TP, t, :], qq[0:TP, :], small[0:TP, 10 + t:11 + t], kvb[0:TP, :], ALU.mult, ALU.mult))
                do.settle()
            v.wait_ge(sem("in_ln"), 64)
            norm_rows(R2, 6, 1e-5, sem("on_rows"), extra=grow2)
            turned_low("on")
            for t in range(T):
                for i in range(2):
                    filled(v, "mproj", t, i)
                    o = R1[0:TP, t, i * HALF:(i + 1) * HALF]
                    do(V.tensor_tensor(o, o, bank("mproj", t, i)[0:TP, 0:HALF], ALU.add), freed("mproj", t, i))
            do.settle()

            norm_rows(R1, 7, 1e-5, sem("m1_rows"))
            turned_low("m1")
            filled(v, "logits1")
            l0, l1, l2, l3, e1_, lc = (a[0:TP] for a in (L0, L1, L2, L3, esort1, lcol))
            do(V.tensor_copy(l3, bank("logits1")[0:TP, 0:80].rearrange("p (t e) -> p t e", t=T)), freed("logits1"))
            do.settle()
            do(V.tensor_reduce(lc[:, 0, :], l3, AX, ALU.max))
            v.wait_ge(sem("iotas"), 5)
            do(V.tensor_copy(e1_, e1_i[0:TP].rearrange("p (t e) -> p t e", t=T)))
            do.settle()
            do(V.tensor_tensor(l0, l3, wide(lc[:, 0, :], E1), ALU.subtract), sem("shifted1"))
            do(V.tensor_tensor(l1, l3, wide(lc[:, 0, :], E1), ALU.is_equal))
            do.settle()
            do(V.tensor_tensor(l1, l1, e1_, ALU.mult))
            do.settle()
            do(V.tensor_reduce(lc[:, 1, :], l1, AX, ALU.max))
            do.settle()
            do(V.tensor_tensor(l1, e1_, wide(lc[:, 1, :], E1), ALU.is_equal), sem("onehot1"))
            v.wait_ge(sem("exp1"), 1)
            do(V.tensor_reduce(lc[:, 2, :], l2, AX, ALU.add))
            do.settle()
            do(V.reciprocal(lc[:, 3, :], lc[:, 2, :]))
            filled(v, "order1")
            ps = bank("order1")
            tot = ps[0:TP, 80:160].rearrange("p (t e) -> p t e", t=T)
            do(V.tensor_reduce(cnt1[0:TP, :], tot.rearrange("p t e -> p e t"), AX, ALU.add))
            do(V.memset(l0[:, 0, :], 0.0))
            for t in range(1, T):
                do.settle()
                do(V.tensor_tensor(l0[:, t, :], l0[:, t - 1, :], tot[:, t - 1, :], ALU.add))
            do.settle()
            do(V.tensor_tensor(l3, l0, ps[0:TP, 0:80].rearrange("p (t e) -> p t e", t=T), ALU.add), freed("order1"))
            do(V.tensor_scalar(nblk[0:TP, :], cnt1[0:TP, :], float(BLK), 1.0, ALU.is_gt, ALU.add))
            for m in range(2, N // BLK + 1):
                do.settle()
                do(V.scalar_tensor_tensor(nblk[0:TP, :], cnt1[0:TP, :], float(BLK * m), nblk[0:TP, :], ALU.is_gt, ALU.add))
            do(V.memset(first1[0:TP, 0:1], 0.0))
            for e in range(E1):
                do.settle()
                do(V.tensor_tensor(first1[0:TP, e + 1:e + 2], first1[0:TP, e:e + 1], nblk[0:TP, e:e + 1], ALU.add))
            do.settle()
            do(V.tensor_copy(first_i[0:TP, :], first1[0:TP, :]))
            do(V.tensor_scalar(l2, first1[0:TP, 0:E1].unsqueeze(1).to_broadcast([TP, T, E1]), float(BLK), -1.0, ALU.mult, ALU.add))
            do.settle()
            do(V.tensor_tensor(l3, l3, l2, ALU.add))
            do.settle()
            do(V.tensor_tensor(l3, l3, l1, ALU.mult))
            do.settle()
            do(V.tensor_reduce(lc[:, 4, :], l3, AX, ALU.add))
            do.settle()
            do(V.tensor_copy(slot1[0:TP, :], lc[:, 4, :]), sem("slots1"))
            v.wait_ge(sem("scattered1"), 16 * T)
            do(V.tensor_copy(small[0:TP, 0:1], small[0:TP, 1:2]), sem("blocks_known"))
            v.wait_ge(sem("in_b2E"), 16 * E1)
            v.sem_inc(sem("block_out_emptied"), 1)
            v.sem_inc(sem("block_stored"), 16)
            for e in range(E1):
                b0 = v.value_load(first_i[0:1, e:e + 1], min_val=e, max_val=MAXB - 1)
                b1_ = v.value_load(first_i[0:1, e + 1:e + 2], min_val=e + 1, max_val=MAXB)
                with v.Fori(b0, b1_) as b:
                    v.wait_ge(sem("block_out"), b + 1)
                    v.wait_ge(sem("block_stored"), b * 16 + 16)
                    for i in range(2):
                        ins = V.tensor_tensor(oB[:, i * HALF:(i + 1) * HALF], PS[4 + i][:, 0:HALF], b2row[:, e, i * HALF:(i + 1) * HALF], ALU.add)
                    ins.then_inc(sem("block_out_emptied"), 1)
            for t in range(T):
                v.wait_ge(sem(f"in_gath{t % 2}"), 16 * (t // 2 + 1))
                do(V.scalar_tensor_tensor(R1[0:TP, t, :], gath1[t % 2][0:TP, :], lc[:, 3, t:t + 1], R1[0:TP, t, :], ALU.mult, ALU.add), sem("out_rows"))


_INS = ["x", "src", "dst", "L0_gnn_W1", "L0_gnn_a1_src", "L0_gnn_a1_dst", "L0_gnn_b1", "L0_gnn_W2", "L0_gnn_a2_src",
        "L0_gnn_a2_dst", "L0_gnn_b2", "L0_mix_W_qkv", "L0_mix_b_qkv", "L0_mix_W_proj", "L0_mix_b_proj",
        "L0_mix_random_features", "L0_ffn_ln_w", "L0_ffn_w_router", "L0_ffn_wi", "L0_ffn_wo", "L1_gnn_W", "L1_gnn_b",
        "L1_mix_w_qkv", "L1_mix_w_proj", "L1_mix_ln_in_g", "L1_mix_ln_in_b", "L1_mix_ln_out_g", "L1_mix_ln_out_b",
        "L1_ffn_Wg", "L1_ffn_W1", "L1_ffn_b1", "L1_ffn_W2", "L1_ffn_b2"]


def kernel(**inputs):
    import numpy as _np
    import concourse.bacc as _bacc
    from concourse import mybir as _mybir
    from concourse.bass_utils import run_bass_kernel_spmd as _run

    nc = _bacc.Bacc("TRN2", target_bir_lowering=False, num_devices=1)
    arrays, args = {}, []
    for name in _INS:
        a = _np.ascontiguousarray(inputs[name])
        arrays[f"in_{name}_dram"] = a
        args.append(nc.dram_tensor(f"in_{name}_dram", a.shape, _mybir.dt.from_np(a.dtype), kind="ExternalInput").ap())
    args.append(nc.dram_tensor("out_0_dram", (1250, 768), _mybir.dt.float32, kind="ExternalOutput").ap())
    build(nc, *args)
    r = _run(nc, [arrays], core_ids=[0])
    return r.results[0]["out_0_dram"]
```

```python
from contextlib import ExitStack

import concourse.bass as bass
from concourse import mybir

F32 = mybir.dt.float32
F16 = mybir.dt.float16
I32 = mybir.dt.int32
ALU = mybir.AluOpType
ACT = mybir.ActivationFunctionType
AX = mybir.AxisListType.X


N = 1250
TP = 125
T = N // TP
D = 768
KD = D // 128
HALF = D // 2
NE = 40000
GE = 500
NG = NE // GE
QG = GE // TP
WIN = 50
NW = N // WIN
BIAS = 2 * NG
H1, HID = 4, 512
FC = HID // 128
IC = 250
NC = N // IC
HT = T // 2
TC = IC // TP
LEAD = 3
MH, MD, MM = 12, 64, 256
KV_SCALE = MD ** -0.5 * MD ** -0.5 / MM
COLS = ((0, 500), (500, 500), (1000, 250))
E0, F0, CAP = 16, 384, 64
E1, F1 = 8, 384
BLK = 128
MINB = -(-N // BLK)
MAXB = E1 + (N - E1) // BLK
F0C = F0 // 128
SLOTS = E0 * CAP
BANKS = 6
BIG = 1.0e30


def pe_groups():
    def transposed(name):
        return [("T", name, t, i) for t in range(T) for i in range(2)]

    def rows(name):
        return [(name, t, i) for t in range(T) for i in range(2)]

    g = transposed("xn")
    g += rows("v") + [("rfT",)]
    for p in range(MH // 2):
        g += [("q", p, c) for c in range(3)] + [("k", p, c) for c in range(3)]
        for s in range(2):
            g += [("phiq", p, s, m, c) for m in range(2) for c in range(3)]
            g += [("phik", p, s, i) for i in range(T // 2)]
        g += [("kv", p, s) for s in range(2)]
        g += [("at", p, c) for c in range(3)]
    g += rows("proj")
    g += [("edgeT", 0), ("edgeT", 1), ("groupB",), ("tables",)]
    g += [("deg",), ("coef1",)]
    g += [("max1", h, i) for h in range(H1) for i in range(3)]
    for h in range(H1):
        g += [("h1", h, t) for t in range(T)]
        for c in range(NC):
            g += [("den1", h, c)] + [("agg1", h, c, f) for f in range(FC)]
            if c:
                g += [("w2", h, (c - 1) * TC + t, i) for t in range(TC) for i in range(2)]
        g += [("w2", h, (NC - 1) * TC + t, i) for t in range(TC) for i in range(2)]
    g += [("max2", i) for i in range(3)]
    for c in range(NC):
        g += [("den2", c)] + [("agg2", c * TC + t, i) for t in range(TC) for i in range(2)]
    g += transposed("m0")
    g += [("logits0",), ("order0",)]
    for e in range(0, E0, 2):
        g += [("einT", e, i) for i in range(2)]
        for d in range(2):
            g += [("eh", e + d)] + [("eo", e + d, i) for i in range(2)]
    g += transposed("x2")
    g += rows("gcnh")
    g += transposed("hn")
    g += rows("gcn")
    for t in range(T):
        g += [("mk", t, i) for i in range(2)] + [("mv", t, i) for i in range(2)]
    g += [("kvsum", i) for i in range(2)]
    g += rows("mq")
    g += transposed("on") + rows("mproj")
    g += transposed("m1")
    g += [("logits1",), ("order1",)]
    return g


GROUPS = pe_groups()
AT = {key: n for n, key in enumerate(GROUPS)}
SPLIT = {key: n for n, key in enumerate(k for k in GROUPS if k[0] in ("T", "rfT", "q", "k", "phiq", "phik", "kv", "at", "h1", "gcnh"))}
assert len(AT) == len(GROUPS)


class Steps:

    def __init__(self, eng, own):
        self.eng, self.own, self.count, self.last = eng, own, {}, None

    def __call__(self, ins, signal=None):
        if isinstance(signal, tuple):
            sem, n = signal
        else:
            sem = self.own if signal is None else signal
            n = self.count.get(id(sem), 0) + 1
            self.count[id(sem)] = n
        ins.then_inc(sem, 1)
        self.last = (sem, n)
        return ins

    def settle(self):
        self.eng.wait_ge(*self.last)


def build(nc, x, src, dst, W1, a1_src, a1_dst, b1, W2, a2_src, a2_dst, b2, Wqkv, bqkv, Wp, bp, rf,
          ln_w, w_router, wi, wo, Wg1, bg1, w_qkv, w_proj, in_g, in_b, out_g, out_b, Wg, F1w, F1b, F2w, F2b, out):
    with ExitStack() as ctx:
        def sb(name, words, dt=F32):
            return ctx.enter_context(nc.sbuf_tensor(name, [128, words], dt))

        sems = {}

        def sem(name):
            if name not in sems:
                sems[name] = ctx.enter_context(nc.semaphore(name))
            return sems[name]

        CTt = sb("CTt", T * N)
        RTt = sb("RTt", KD * N)
        R1t = sb("R1t", T * D)
        R2t = sb("R2t", T * D)
        WK = sb("WK", 15720)
        MISC = sb("MISC", 2120)
        PS = [ctx.enter_context(nc.psum_tensor(f"bank{i}", [128, 512], F32)) for i in range(8)]

        def wk(at, n, pattern=None, parts=128, base=WK, **kw):
            v = base[0:parts, at:at + n]
            return v.rearrange(pattern, **kw) if pattern else v

        CT = CTt[:, :].rearrange("p (t n) -> p t n", t=T)

        def parts(view, pattern=None, **kw):
            h = view.bitcast(F16)
            n = view.shape[1]
            pair = (h[:, 0:n], h[:, n:2 * n])
            return tuple(a.rearrange(pattern, **kw) for a in pair) if pattern else pair

        def at2(pair, *index):
            return tuple(a[index] for a in pair)

        RT = parts(RTt[:, :], "p (k n) -> p k n", k=KD)
        R1 = R1t[:, :].rearrange("p (t d) -> p t d", t=T)
        R2 = R2t[:, :].rearrange("p (t d) -> p t d", t=T)

        used = [0]

        def misc(n, pattern=None, **kw):
            a = used[0]
            used[0] += n
            assert used[0] <= 2120, used
            v = MISC[:, a:a + n]
            return v.rearrange(pattern, **kw) if pattern else v

        ident = misc(128)
        ones = misc(128)
        upto = misc(128)
        late = MISC[:, used[0]:used[0] + 1024]
        kvpad = parts(misc(512), "p (s m d) -> p s m d", s=2, m=2)
        rfp = parts(misc(512), "p (s m) -> p s m", s=2)
        bqk = misc(12)
        b1c = misc(16)
        dinv = misc(10)
        stat = [misc(12) for _ in range(2)]
        mv = [misc(T * 2, "p (t n) -> p t n", t=T) for _ in range(2)]
        rstd = [misc(T) for _ in range(2)]
        AS = misc(80, "p (t n) -> p t n", t=T)
        AS2 = misc(80, "p (t n) -> p t n", t=T)
        Mx = misc(40, "p (h t) -> p h t", h=4)
        Ac = misc(40, "p (h t) -> p h t", h=4)
        Bc = misc(40, "p (h t) -> p h t", h=4)
        small = misc(60)
        rd2 = misc(2)

        filled_sem, own_v, own_a, own_g = sem("bank_filled"), sem("vector_step"), sem("scalar_step"), sem("pool_step")
        emptied_sem = [sem(f"bank_emptied{b}") for b in range(BANKS)]

        def bank(*key):
            return PS[AT[key] % BANKS]

        def filled(eng, *key):
            eng.wait_ge(filled_sem, AT[key] + 1)

        def emptied(eng, *key):
            eng.wait_ge(emptied_sem[AT[key] % BANKS], AT[key] // BANKS + 1)

        def all_emptied(eng, *key):
            for n in range(max(0, AT[key] - BANKS + 1), AT[key] + 1):
                emptied(eng, *GROUPS[n])

        def agg_done(eng, u):
            filled(eng, *(("agg1", u // NC, u % NC, FC - 1) if u < H1 * NC else ("agg2", (u - H1 * NC) * TC + TC - 1, 1)))

        def turned_bank(b):
            return b[:, 0:3 * TP].rearrange("p (k n) -> p k n", k=3)

        def phik_bank(b):
            return b[0:TP, :].rearrange("p (t m) -> p t m", t=2)

        def kv_bank(b):
            return b[:, 0:2 * MD].rearrange("p (m d) -> p m d", m=2)

        def freed(*key):
            return emptied_sem[AT[key] % BANKS], AT[key] // BANKS + 1

        zeros = CTt[:, 12110:12494]
        scr_xm = nc.dram_tensor("scr_xm", (N, D), F32).ap()
        scr_in = nc.dram_tensor("scr_in", (SLOTS, D), F32).ap()
        scr_in1 = nc.dram_tensor("scr_in1", ((MAXB + 1) * BLK, D), F32).ap()
        scr_out1 = nc.dram_tensor("scr_out1", (MAXB * BLK, D), F32).ap()
        scr_out = nc.dram_tensor("scr_out", (SLOTS, D), F32).ap()

        def node_rows(a):
            return a.rearrange("(t p) d -> p t d", p=TP)

        def kchunks(a):
            return a.rearrange("(k p) n -> p k n", p=128)

        def row(a):
            return a.rearrange("(a n) -> a n", a=1)

        qT, kT = parts(wk(0, 1250)), parts(wk(1250, 1250))
        rfn = wk(0, 512, "p (s m d) -> p s m d", s=2, m=2)
        PQ = parts(wk(2500, 5000), "p (s m n) -> p s m n", s=2, m=2)
        PK = parts(wk(7500, 5120), "p (s t m) -> p s t m", s=2, t=T)
        bv_row = wk(7500, 768)
        v_tmp = wk(8300, HALF)
        Wqk = [parts(wk(12620 + 768 * w, 768), "p (k n) -> p k n", k=KD) for w in range(2)]
        stages0 = [wk(14156 + 768 * i, 768) for i in range(2)]
        bias_rows = wk(0, 1536, "p (i d) -> p i d", i=2)
        ATt = parts(CTt[:, 0:7500], "p (k n) -> p k n", k=KD)
        Wv = parts(CTt[:, 7500:12108], "p (k n) -> p k n", k=KD)
        Vr = [parts(R2t[:, t * D:(t + 1) * D]) for t in range(T)]
        nat_i = WK[0:NG, 0:1000].bitcast(I32).rearrange("p (a e) -> p a e", a=2)
        nat = wk(1000, 1000, "p (a e) -> p a e", NG, a=2)
        keys = wk(2000, 1000, "p (a e) -> p a e", NG, a=2)
        tdiv = wk(3000, 500, None, NG)
        gmm = wk(3500, 2, None, NG)
        tab = wk(3510, 16, None, NW)
        iota_i = WK[:, 3600:4100].bitcast(I32)
        iota = wk(4100, 500)
        cutI = wk(4600, 80, None, NW)
        cutJ = wk(4700, 80, None, NW)
        cutK = wk(4800, 80, None, NW)
        trow_i = WK[0:1, 4900:4980].bitcast(I32)
        trow = WK[0:1, 5040:5066]
        iota_c_i = WK[:, 4980:4981].bitcast(I32)
        iota_c = wk(4984, 2)
        upper = wk(5000, 32, None, 32)
        KL = wk(5100, 640, "p (a q g) -> p a q g", a=2, q=QG)
        oh_lo = [WK[:, 5800 + 64 * i:5864 + 64 * i].bitcast(F16) for i in range(QG)]
        oh_key = [WK[:, 6100 + 250 * i:6350 + 250 * i].bitcast(F16) for i in range(QG)]
        zero_bf = WK[:, 7100:7350].bitcast(F16)
        iota16 = WK[:, 8700:8950].bitcast(F16)
        degp = wk(7400, 1250)
        arow = wk(0, 4096, "p (a n) -> p a n", a=2)
        W1s = [wk(4096 + 3072 * i, 3072, "p (k n) -> p k n", k=KD) for i in range(2)]
        junk = wk(10240, 768)
        wa = wk(11100, 48, "p (k n) -> p k n", k=KD)
        wa2 = parts(wk(11200, 48), "p (k n) -> p k n", k=KD)
        maxacc = wk(0, 5000, "p (h n) -> p h n", h=4)
        maskt = wk(5000, 1250)
        Hh = parts(wk(0, 5120), "p (t n) -> p t n", t=T)
        Pm = [parts(wk(5120 + 2500 * i, 2500), "p (t n) -> p t n", t=T) for i in range(2)]
        H1T = [parts(wk(10120 + 1000 * i, 1000), "p (f n) -> p f n", f=FC) for i in range(2)]
        U = wk(12120, 2500, "p (t n) -> p t n", t=T)
        rden = wk(14620, 250)
        Sp = [wk(14870 + 250 * i, 250) for i in range(2)]
        W1h = parts(R1t[:, 0:3072], "p (k n) -> p k n", k=KD)
        W2h = parts(R1t[:, 3072:6144], "p (k n) -> p k n", k=FC)
        elu_z = [R1t[:, 6144 + 500 * i:6394 + 500 * i] for i in range(2)]
        elu_m = [R1t[:, 6394 + 500 * i:6644 + 500 * i] for i in range(2)]
        stages1 = [R1t[:, 7160:7416], R1t[:, 7420:7676], wk(15400, 256)]
        PIECE = 256
        ab_rows = [late[:, 500 * i:500 * i + 500].rearrange("p (a n) -> p a n", a=2) for i in range(2)]
        h2_tmp = [wk(2304 + 768 * i, 768) for i in range(2)]
        H2 = [parts(R2t[:, t * D:(t + 1) * D]) for t in range(T)]
        a2row = wk(0, 1536, "p (a n) -> p a n", a=2)
        junk2 = wk(1536, 768)
        max2a, mask2 = wk(12120, 1250), wk(13370, 1250)
        lnw_row = wk(0, 768)
        router_in = wk(768, 96)
        router = parts(late[:, 0:96], "p (k e) -> p k e", k=KD)
        G0 = wk(900, 160, "p (t e) -> p t e", t=T)
        G1 = wk(1060, 160, "p (t e) -> p t e", t=T)
        G2 = wk(1220, 160, "p (t e) -> p t e", t=T)
        G3 = wk(1380, 160, "p (t e) -> p t e", t=T)
        ebase = wk(1540, 160, "p (t e) -> p t e", t=T)
        esort = wk(1700, 160, "p (t e) -> p t e", t=T)
        gcol = wk(1860, 120, "p (c t) -> p c t", c=12)
        e_i = WK[:, 1980:2140].bitcast(I32)
        slot_s = WK[:, 2140:2150].bitcast(I32)
        slot_g = WK[:, 2150:2160].bitcast(I32)
        ein = wk(3000, 768)
        einT = wk(3768, 768, "p (k n) -> p k n", k=KD)
        hE = [wk(4540 + 192 * i, 192, "p (f n) -> p f n", f=F0C) for i in range(2)]
        oE = [wk(4930 + 768 * i, 768) for i in range(2)]
        EW = [wk(6500 + 4608 * i, 4608) for i in range(2)]
        wiE = [w[:, 0:2304].rearrange("p (k n) -> p k n", k=KD) for w in EW]
        woE = [w[:, 2304:4608].rearrange("p (k n) -> p k n", k=F0C) for w in EW]
        gath = [wk(6500 + 768 * i, 768) for i in range(2)]
        gH = [parts(wk(D * t, D)) for t in range(T)]
        gW = parts(wk(7680, 4608), "p (k n) -> p k n", k=KD)
        grow2 = wk(12288, 1536, "p (a n) -> p a n", a=2)
        stages2 = [wk(13840 + 768 * i, 768) for i in range(2)]
        grow = late[:, 144:912]
        ct_tmp = late[:, 144:144 + N // 2]
        CT2 = [parts(CTt[:, i * N // 2:(i + 1) * N // 2]) for i in range(2 * T)]
        wqv = [gW, parts(R2t[:, 0:4608], "p (k n) -> p k n", k=KD)]
        wq2, wpr = (parts(CTt[:, 4608 * i:4608 * i + 4608], "p (k n) -> p k n", k=KD) for i in range(2))
        kt_ = [wk(768 * i, 768) for i in range(2)]
        sq_, psum_row, kvb, prodsum = (wk(768 * i, 768) for i in range(2, 6))
        FW = [CTt[:, 4608 * i:4608 * i + 4608] for i in range(2)]
        w1E = [w[:, 0:2304].rearrange("p (k n) -> p k n", k=KD) for w in FW]
        w2E = [w[:, 2304:4608].rearrange("p (k n) -> p k n", k=F0C) for w in FW]
        b2row = wk(0, 6144, "p (e d) -> p e d", e=E1)
        xb = wk(6144, 768)
        xbT = wk(6912, 768, "p (k n) -> p k n", k=KD)
        hB = wk(7680, 384, "p (f n) -> p f n", f=F0C)
        oB = wk(8064, 768)
        wgE_in = wk(8840, 48)
        wgE = parts(late[:, 96:144], "p (k e) -> p k e", k=KD)
        b1E = wk(8900, 24, "p (e f) -> p e f", e=E1)
        L0 = wk(9000, 80, "p (t e) -> p t e", t=T)
        L1 = wk(9080, 80, "p (t e) -> p t e", t=T)
        L2 = wk(9160, 80, "p (t e) -> p t e", t=T)
        L3 = wk(9240, 80, "p (t e) -> p t e", t=T)
        esort1 = wk(9320, 80, "p (t e) -> p t e", t=T)
        e1_i = WK[:, 9400:9480].bitcast(I32)
        lcol = wk(9480, 60, "p (c t) -> p c t", c=6)
        cnt1 = wk(9540, 8)
        nblk = wk(9550, 8)
        first1 = wk(9560, 9)
        first_i = WK[:, 9570:9579].bitcast(I32)
        slot1 = WK[:, 9580:9590].bitcast(I32)
        tick = wk(9592, 1)
        gath1 = [wk(10400 + 768 * i, 768) for i in range(2)]

        pieces = []
        piece_after = {}

        def weight(name, srcs, dests, stages, tag, after=None):
            for (a, d) in zip(srcs, dests):
                i = len([1 for p in pieces if p[4][0] == tag]) % len(stages)
                if after:
                    piece_after[len(pieces)] = after
                pieces.append((name, a, d, stages[i], (tag, i)))

        def last_piece(name):
            return max(n for n, p in enumerate(pieces) if p[0] == name)

        def by_k(w, n=KD):
            return [w[k * 128:(k + 1) * 128, :] for k in range(n)]

        def part_k(pair, n=KD):
            return [at2(pair, slice(None), k) for k in range(n)]

        weight("Wv", by_k(Wqkv[:, 2 * D:3 * D]), part_k(Wv), stages0, "a")
        for p in range(MH // 2):
            for w in range(2):
                weight(("Wqk", p), [kchunks(Wqkv[:, w * D + 128 * p:w * D + 128 * p + 128])], [Wqk[w]], stages0, "a", ("k", p - 1, 2) if p else None)
            if p == 0:
                weight("Wp", by_k(Wp), part_k(Wv), stages0, "a", ("v", T - 1, 1))
        for h in range(H1):
            pieces1 = [(k, slice(i, i + PIECE)) for k in range(KD) for i in range(0, HID, PIECE)]
            weight(("W1h", h), [W1[k * 128:(k + 1) * 128, h * HID + c.start:h * HID + c.stop] for k, c in pieces1],
                   [at2(W1h, slice(None), k, c) for k, c in pieces1], stages1, "b", ("h1", h - 1, T - 1) if h else None)
            pieces2 = [(f, slice(i, i + PIECE)) for f in range(FC) for i in range(0, D, PIECE)]
            weight(("W2h", h), [W2[(h * FC + f) * 128:(h * FC + f + 1) * 128, c] for f, c in pieces2],
                   [at2(W2h, slice(None), f, c) for f, c in pieces2], stages1, "b", ("w2", h - 1, T - 1, 1) if h else None)
        weight("router", [kchunks(w_router)], [router], [router_in], "c")
        weight("gW", by_k(Wg1), part_k(gW), stages2, "d")
        for name, c0, dest, read in (("wk", D, wqv[0], ("gcnh", T - 1, 1)), ("wv", 2 * D, wqv[1], ("T", "hn", T - 1, 1)), ("wq", 0, wq2, ("gcn", T - 1, 1))):
            weight(name, by_k(w_qkv[:, c0:c0 + D]), part_k(dest), stages2, "d", read)
        weight("wpr", by_k(w_proj), part_k(wpr), stages2, "d", ("gcn", T - 1, 1))
        weight("wg", [kchunks(Wg)], [wgE], [wgE_in], "e")

        def shaped(view, like):
            n = 1
            for x_ in like.shape[1:]:
                n *= x_
            v = view[:, 0:n]
            return v.rearrange("p (k n) -> p k n", n=like.shape[-1]) if len(like.shape) == 3 else v

        block = ctx.enter_context(nc.Block())

        @block.sync
        def _(sp):
            def load(o, i, s):
                sp.dma_start(o, i).then_inc(sem(s), 16)

            next_piece = [0]

            def load_pieces(*names):
                for name in names:
                    while next_piece[0] < len(pieces) and pieces[next_piece[0]][0] == name:
                        n = next_piece[0]
                        next_piece[0] += 1
                        _, a, _, stage, place = pieces[n]
                        before = [m for m in range(n) if pieces[m][4] == place]
                        if before:
                            sp.wait_ge(sem("weights_split"), before[-1] + 1)
                        load(shaped(stage, a), a, f"weight_in_{place[0]}{place[1]}")

            def after(*key):
                filled(sp, *key)

            for t in range(T):
                sp.dma_start(R1[0:TP, t, :], x[t * TP:(t + 1) * TP, :]).then_inc(sem(f"in_x{t}"), 16)
            load(bv_row, row(bqkv[2 * D:3 * D]).to_broadcast([128, D]), "in_bv")
            sp.wait_ge(sem("pads"), 1)
            for s in range(2):
                load(rfn[:, s, :, s * MD:(s + 1) * MD], rf.rearrange("(m p) d -> p m d", p=128), "in_rf")
            with nc.allow_non_contiguous_dma(reason="columns of a short vector"):
                load(bqk, bqkv[0:2 * D].rearrange("(k p) -> p k", p=128), "in_bqk")
                load(b1c, b1.rearrange("(k p) -> p k", p=128), "in_b1")
            load_pieces("Wv", ("Wqk", 0), "Wp", ("Wqk", 1))
            for a, rows_ in ((scr_in, SLOTS), (scr_in1, (MAXB + 1) * BLK), (scr_out1[MINB * BLK:MAXB * BLK, :], (MAXB - MINB) * BLK)):
                n = rows_ // 128 * 2
                sp.dma_start(a.rearrange("(p r) (h d) -> p (r h) d", p=128, h=2), zeros.unsqueeze(1).to_broadcast([128, n, HALF])).then_inc(sem("slots_zeroed"), 16)
            load_pieces(*[("Wqk", p) for p in range(2, MH // 2)])
            after("at", 5, 2)
            load(bias_rows[:, 0, :], row(bp).to_broadcast([128, D]), "in_bias")
            load(bias_rows[:, 1, :], row(b2).to_broadcast([128, D]), "in_bias")
            all_emptied(sp, "proj", T - 1, 1)
            sp.wait_ge(sem("bias_added"), T)
            sp.wait_ge(sem("slots_zeroed"), 48)
            load(nat_i[:, 0, :], src.rearrange("(g e) -> g e", g=NG), "in_edges")
            load(nat_i[:, 1, :], dst.rearrange("(g e) -> g e", g=NG), "in_edges")
            sp.dma_start(node_rows(scr_xm), R1[0:TP, :, :]).then_inc(sem("xm_kept"), 16)
            emptied(sp, "deg")
            load(arow[:, 0, :], row(a1_src.rearrange("h d -> (h d)")).to_broadcast([128, 2048]), "in_a1")
            load(arow[:, 1, :], row(a1_dst.rearrange("h d -> (h d)")).to_broadcast([128, 2048]), "in_a1")
            for h in range(H1):
                if h >= 2:
                    sp.wait_ge(sem("W1_folded"), h - 1)
                load(W1s[h % 2], kchunks(W1[:, h * HID:(h + 1) * HID]), f"in_W1s{h % 2}")
            sp.wait_ge(sem("xm_kept"), 16)
            for h in range(H1):
                load_pieces(("W1h", h), ("W2h", h))
            after("w2", H1 - 1, T - 1, 1)
            load(a2row[:, 0, :], a2_src.to_broadcast([128, D]), "in_a2")
            load(a2row[:, 1, :], a2_dst.to_broadcast([128, D]), "in_a2")
            all_emptied(sp, "w2", H1 - 1, T - 1, 1)
            load(R1[0:TP, :, :], node_rows(scr_xm), "xm_back")
            all_emptied(sp, "agg2", T - 1, 1)
            load(lnw_row, row(ln_w).to_broadcast([128, D]), "in_lnw")
            load_pieces("router")
            for e in range(E0):
                if e >= 2:
                    after("eo", e - 2, 1)
                if e and e % 2 == 0:
                    after("einT", e - 2, 1)
                    load(ein, scr_in[e * CAP:(e + 2) * CAP, :], "in_ein")
                load(wiE[e % 2], kchunks(wi[e]), f"in_we{e % 2}")
                load(woE[e % 2], kchunks(wo[e]), f"in_we{e % 2}")
                if e == 1:
                    sp.wait_ge(sem("scattered"), 16 * T)
                    load(ein, scr_in[0:2 * CAP, :], "in_ein")
            all_emptied(sp, "eo", E0 - 1, 1)
            sp.wait_ge(sem("moe0_read"), 1)
            load(grow2[:, 0, :], row(in_g).to_broadcast([128, D]), "in_ln")
            load(grow2[:, 1, :], row(in_b).to_broadcast([128, D]), "in_ln")
            load_pieces("gW")
            sp.wait_ge(sem("counts_split"), 2 * T)
            load(grow, row(bg1).to_broadcast([128, D]), "in_gb")
            load_pieces("wk", "wv")
            sp.wait_ge(sem("hn_rows"), T)
            load(grow2[:, 0, :], row(out_g).to_broadcast([128, D]), "in_ln")
            load(grow2[:, 1, :], row(out_b).to_broadcast([128, D]), "in_ln")
            load_pieces("wq", "wpr")
            all_emptied(sp, "mproj", T - 1, 1)
            load_pieces("wg")
            for e in range(E1):
                with nc.allow_non_contiguous_dma(reason="columns of a short vector"):
                    sp.dma_start(b1E[:, e, :], F1b[e].rearrange("(f p) -> p f", p=128)).then_inc(sem("in_b1E"), 16)
                load(b2row[:, e, :], F2b[e:e + 1, :].to_broadcast([128, D]), "in_b2E")
            sp.wait_ge(sem("scattered1"), 16 * T)
            load(xb, scr_in1[0:BLK, :], "in_xb")
            blocks = sp.value_load(first_i[0:1, E1:E1 + 1], min_val=E1, max_val=MAXB)
            with sp.Fori(1, blocks + 1) as b:
                sp.wait_ge(sem("block_turned"), b)
                sp.dma_start(xb, scr_in1[bass.ds(b * BLK, BLK), :]).then_inc(sem("in_xb"), 16)
            sp.wait_ge(sem("out_rows"), T)
            sp.dma_start(node_rows(out), R1[0:TP, :, :]).then_inc(sem("out_stored"), 16)
            sp.wait_ge(sem("out_stored"), 16)

        @block.tensor
        def _(pe):
            nth = [0]

            def group(*key):
                n = nth[0]
                assert GROUPS[n] == key, (GROUPS[n], key)
                nth[0] += 1
                if n >= BANKS:
                    pe.wait_ge(emptied_sem[n % BANKS], n // BANKS)
                return PS[n % BANKS]

            def mm(o, lhsT, rhs, first, last):
                return nc.tensor.matmul(o, lhsT, rhs, start=first, stop=last)

            def mm3(o, lhsT, rhs, first, last):
                nc.tensor.matmul(o, lhsT[0], rhs[0], start=first, stop=False)
                nc.tensor.matmul(o, lhsT[0], rhs[1], start=False, stop=False)
                return nc.tensor.matmul(o, lhsT[1], rhs[0], start=False, stop=last)

            def split(name):
                pe.wait_ge(sem("weights_split"), last_piece(name) + 1)

            def close(ins):
                ins.then_inc(filled_sem, 1)

            def transposed(name, rows_sem, rows_at=1):
                for t in range(T):
                    pe.wait_ge(rows_sem, rows_at * (t + 1))
                    for i in range(2):
                        ps = group("T", name, t, i)
                        for j in range(3):
                            k = 3 * i + j
                            ins = nc.tensor.transpose(ps[:, j * TP:(j + 1) * TP], R2[0:TP, t, k * 128:(k + 1) * 128], ident[0:TP, 0:TP])
                        close(ins)

            def rows(name, t, w, lhs=RT):
                for i in range(2):
                    ps = group(name, t, i)
                    for k in range(KD):
                        ins = mm3(ps[0:TP, 0:HALF], at2(lhs, slice(None), k, slice(t * TP, (t + 1) * TP)),
                                  at2(w, slice(None), k, slice(i * HALF, (i + 1) * HALF)), k == 0, k == KD - 1)
                    close(ins)

            pe.wait_ge(sem("consts"), 3)
            transposed("xn", sem("xn_rows"))
            all_emptied(pe, "T", "xn", T - 1, 1)
            split("Wv")
            for t in range(T):
                rows("v", t, Wv)
            pe.wait_ge(sem("in_rf"), 32)
            ps = group("rfT")
            for s in range(2):
                for m in range(2):
                    ins = nc.tensor.transpose(ps[:, (2 * s + m) * 128:(2 * s + m + 1) * 128], rfn[:, s, m, :], ident)
            close(ins)
            for p in range(MH // 2):
                split(("Wqk", p))
                for w, name in enumerate("qk"):
                    for c, (c0, cn) in enumerate(COLS):
                        ps = group(name, p, c)
                        for k in range(KD):
                            ins = mm3(ps[:, 0:cn], at2(Wqk[w], slice(None), k), at2(RT, slice(None), k, slice(c0, c0 + cn)), k == 0, k == KD - 1)
                        close(ins)
                all_emptied(pe, "k", p, 2)
                for s in range(2):
                    for m in range(2):
                        for c, (c0, cn) in enumerate(COLS):
                            ps = group("phiq", p, s, m, c)
                            close(mm3(ps[:, 0:cn], at2(rfp, slice(None), s, slice(m * 128, (m + 1) * 128)), at2(qT, slice(None), slice(c0, c0 + cn)), True, True))
                    for i in range(T // 2):
                        ps = group("phik", p, s, i)
                        for j in range(2):
                            t = 2 * i + j
                            ins = mm3(ps[0:TP, j * MM:(j + 1) * MM], at2(kT, slice(None), slice(t * TP, (t + 1) * TP)), at2(rfp, slice(None), s), True, True)
                        close(ins)
                for s in range(2):
                    all_emptied(pe, "phik", p, s, T // 2 - 1)
                    if p == 0 and s == 0:
                        pe.wait_ge(sem("v_split"), 2 * T)
                    ps = group("kv", p, s)
                    for m in range(2):
                        for t in range(T):
                            ins = mm3(ps[:, m * MD:(m + 1) * MD], at2(PK, slice(0, TP), s, t, slice(m * 128, (m + 1) * 128)),
                                      at2(Vr[t], slice(0, TP), slice((2 * p + s) * MD, (2 * p + s + 1) * MD)), t == 0, t == T - 1)
                    close(ins)
                all_emptied(pe, "kv", p, 1)
                for s in range(2):
                    all_emptied(pe, "phiq", p, s, 1, 2)
                for c, (c0, cn) in enumerate(COLS):
                    ps = group("at", p, c)
                    for s in range(2):
                        for m in range(2):
                            ins = mm3(ps[:, 0:cn], at2(kvpad, slice(None), s, m), at2(PQ, slice(None), s, m, slice(c0, c0 + cn)), s + m == 0, s + m == 2)
                    close(ins)
            all_emptied(pe, "at", 5, 2)
            split("Wp")
            for t in range(T):
                rows("proj", t, Wv, ATt)

            pe.wait_ge(sem("edge_keys"), 1)
            for a in range(2):
                ps = group("edgeT", a)
                for q in range(QG):
                    ins = nc.tensor.transpose(ps[0:TP, q * NG:(q + 1) * NG], keys[:, a, q * TP:(q + 1) * TP], ident[0:NG, 0:NG])
                close(ins)
            ps = group("groupB")
            for a in range(2):
                ins = mm(ps[0:NW, a * NG:(a + 1) * NG], gmm[:, a:a + 1].to_broadcast([NG, NW]), ident[0:NG, 0:NG], True, True)
            close(ins)
            pe.wait_ge(sem("window_cols"), 1)
            ps = group("tables")
            for a in range(2):
                mm(ps[0:1, a * NW:(a + 1) * NW], tab[:, a:a + 1], ident[0:NW, 0:NW], True, True)
            close(mm(ps[0:1, 2 * NW:3 * NW], tab[:, 2:3], upper[0:NW, 0:NW], True, True))
            pe.wait_ge(sem("window_table"), 1)
            pe.wait_ge(sem("iota_set"), 1)
            pe.sem_inc(sem("onehots_used"), BIAS + 2)
            for w in range(NW):
                ps = PS[6 + w % 2]
                if w >= 2:
                    pe.wait_ge(sem("window_emptied"), w - 1)
                g0 = pe.value_load(trow_i[0:1, w:w + 1], min_val=0, max_val=NG - 1)
                g1 = pe.value_load(trow_i[0:1, NW + w:NW + w + 1], min_val=1, max_val=NG)
                base = pe.value_load(trow_i[0:1, 2 * NW + w:2 * NW + w + 1], min_val=0, max_val=2 * NG * NW + BIAS)
                nc.tensor.matmul(ps[0:TP, 0:500], zero_bf[0:TP, 0:TP], zero_bf[0:TP, 0:500], start=True, stop=False)
                with pe.Fori(g0, g1) as g:
                    for half in range(2):
                        pe.wait_ge(sem("onehots_ready"), base + g * 2 + (half + 1))
                        for q in range(2 * half, 2 * half + 2):
                            ins = nc.tensor.matmul(ps[0:TP, 0:500], oh_lo[q][0:TP, 0:TP], oh_key[q][0:TP, 0:500], start=False, stop=False)
                        ins.then_inc(sem("onehots_used"), 1)
                nc.tensor.matmul(ps[0:TP, 0:500], zero_bf[0:TP, 0:TP], zero_bf[0:TP, 0:500], start=False, stop=True).then_inc(sem("window_filled"), 1)
            pe.wait_ge(sem("deg_parts"), 1)
            ps = group("deg")
            for t in range(T):
                ins = mm(ps[0:TP, t:t + 1], degp[0:TP, t * TP:(t + 1) * TP], ones[0:TP, 0:1], True, True)
            close(ins)

            pe.wait_ge(sem("fold_split"), 1)
            ps = group("coef1")
            for t in range(T):
                for k in range(KD):
                    ins = mm3(ps[0:TP, t * 8:t * 8 + 8], at2(RT, slice(None), k, slice(t * TP, (t + 1) * TP)), at2(wa2, slice(None), k), k == 0, k == KD - 1)
            close(ins)

            def max_tiles(i, acc, *key):
                ps = group(*key)
                for j, t in enumerate(range(4 * i, min(4 * i + 4, T))):
                    ins = nc.tensor.transpose(ps[0:TP, j * TP:(j + 1) * TP], acc[0:TP, t * TP:(t + 1) * TP], ident[0:TP, 0:TP])
                close(ins)

            pe.wait_ge(sem("max_rows"), 1)
            for h in range(H1):
                for i in range(3):
                    max_tiles(i, maxacc[:, h, :], "max1", h, i)

            def coef_rows(u, h, c):
                if u >= 2:
                    pe.wait_ge(sem("coef_copied"), u - 1)
                ps = PS[6 + u % 2]
                for a, col in enumerate((Ac, Bc)):
                    for t in range(TC):
                        tt = c * TC + t
                        ins = mm(ps[0:TP, (a * TC + t) * TP:(a * TC + t + 1) * TP], col[0:TP, h, tt:tt + 1].to_broadcast([TP, TP]),
                                 ident[0:TP, 0:TP], True, True)
                ins.then_inc(sem("coef_rows"), 1)

            pe.wait_ge(sem("coef_cols"), 1)
            coef_rows(0, 0, 0)
            coef_rows(1, 0, 1)
            for h in range(H1):
                split(("W1h", h))
                for t in range(T):
                    ps = group("h1", h, t)
                    for k in range(KD):
                        ins = mm3(ps[0:TP, :], at2(RT, slice(None), k, slice(t * TP, (t + 1) * TP)), at2(W1h, slice(None), k), k == 0, k == KD - 1)
                    close(ins)
                all_emptied(pe, "h1", h, T - 1)

                def w2(c):
                    split(("W2h", h))
                    all_emptied(pe, "agg1", h, c, FC - 1)
                    pe.wait_ge(sem("elu_done"), FC * (h * NC + c + 1))
                    for t in range(TC):
                        for i in range(2):
                            ps = group("w2", h, c * TC + t, i)
                            for f in range(FC):
                                ins = mm3(ps[0:TP, 0:HALF], at2(H1T[(h * NC + c) % 2], slice(None), f, slice(t * TP, (t + 1) * TP)),
                                          at2(W2h, slice(None), f, slice(i * HALF, (i + 1) * HALF)), f == 0, f == FC - 1)
                            close(ins)

                for c in range(NC):
                    u = h * NC + c
                    if u + 2 < H1 * NC:
                        coef_rows(u + 2, (u + 2) // NC, (u + 2) % NC)
                    pe.wait_ge(sem("P_sums"), 2 * u + 2)
                    ps = group("den1", h, c)
                    close(mm(ps[:, 0:IC], ones[0:TP, :], Sp[u % 2][0:TP, :], True, True))
                    pe.wait_ge(sem("P_high"), 2 * u + 2)
                    pe.wait_ge(sem("P_low"), 2 * u + 2)
                    for f in range(FC):
                        ps = group("agg1", h, c, f)
                        for j in range(T):
                            ins = mm3(ps[:, 0:IC], at2(Hh, slice(0, TP), j, slice(f * 128, (f + 1) * 128)), at2(Pm[u % 2], slice(0, TP), j), j == 0, j == T - 1)
                        close(ins)
                    if c:
                        w2(c - 1)
                w2(NC - 1)

            pe.wait_ge(sem("max_rows"), 2)
            for i in range(3):
                max_tiles(i, max2a, "max2", i)
            pe.wait_ge(sem("coef_cols"), 2)
            coef_rows(H1 * NC, 0, 0)
            coef_rows(H1 * NC + 1, 0, 1)
            for c in range(NC):
                u = H1 * NC + c
                if c + 2 < NC:
                    coef_rows(u + 2, 0, c + 2)
                pe.wait_ge(sem("P_sums"), 2 * u + 2)
                ps = group("den2", c)
                for t in range(TC):
                    ins = mm(ps[0:TP, t:t + 1], Sp[u % 2][0:TP, t * TP:(t + 1) * TP], ones[0:TP, 0:1], True, True)
                close(ins)
                pe.wait_ge(sem("P_high"), 2 * u + 2)
                pe.wait_ge(sem("P_low"), 2 * u + 2)
                pe.wait_ge(sem("h2_split"), T)
                for t in range(TC):
                    for i in range(2):
                        ps = group("agg2", c * TC + t, i)
                        for j in range(T):
                            ins = mm3(ps[0:TP, 0:HALF], at2(Pm[u % 2], slice(0, TP), j, slice(t * TP, (t + 1) * TP)),
                                      at2(H2[j], slice(0, TP), slice(i * HALF, (i + 1) * HALF)), j == 0, j == T - 1)
                        close(ins)

            transposed("m0", sem("normed_rows"))
            all_emptied(pe, "T", "m0", T - 1, 1)
            split("router")
            ps = group("logits0")
            for t in range(T):
                for k in range(KD):
                    ins = mm3(ps[0:TP, t * E0:(t + 1) * E0], at2(RT, slice(None), k, slice(t * TP, (t + 1) * TP)), at2(router, slice(None), k), k == 0, k == KD - 1)
            close(ins)
            pe.wait_ge(sem("onehot0"), 1)
            ps = group("order0")
            oh = G1[0:TP, :, :].rearrange("p t e -> p (t e)")
            mm(ps[0:TP, 0:160], upto[0:TP, 0:TP], oh, True, True)
            close(mm(ps[0:TP, 160:320], ones[0:TP, 0:TP], oh, True, True))
            for e in range(0, E0, 2):
                pe.wait_ge(sem("in_ein"), 16 * (e // 2 + 1))
                for i in range(2):
                    ps = group("einT", e, i)
                    for j in range(3):
                        k = 3 * i + j
                        ins = nc.tensor.transpose(ps[:, j * 128:(j + 1) * 128], ein[:, k * 128:(k + 1) * 128], ident[:, :])
                    close(ins)
                all_emptied(pe, "einT", e, 1)
                for d in range(2):
                    pe.wait_ge(sem(f"in_we{d}"), 32 * (e // 2 + 1))
                    ps = group("eh", e + d)
                    for f in range(F0C):
                        for k in range(KD):
                            ins = mm(ps[:, f * CAP:(f + 1) * CAP], wiE[d][:, k, f * 128:(f + 1) * 128], einT[:, k, d * CAP:(d + 1) * CAP], k == 0, k == KD - 1)
                    close(ins)
                    emptied(pe, "eh", e + d)
                    for i in range(2):
                        ps = group("eo", e + d, i)
                        for f in range(F0C):
                            ins = mm(ps[0:CAP, 0:HALF], hE[d][:, f, :], woE[d][:, f, i * HALF:(i + 1) * HALF], f == 0, f == F0C - 1)
                        close(ins)

            transposed("x2", sem("x2_rows"))
            all_emptied(pe, "T", "x2", T - 1, 1)
            split("gW")
            for t in range(T):
                rows("gcnh", t, gW)
            all_emptied(pe, "gcnh", T - 1, 1)
            transposed("hn", sem("hn_rows"))
            pe.wait_ge(sem("counts_split"), 2 * T)
            for t in range(T):
                for i in range(2):
                    ps = group("gcn", t, i)
                    for j in range(T):
                        ins = mm3(ps[0:TP, 0:HALF], at2(CT2[2 * j + t // (T // 2)], slice(0, TP), slice(t % (T // 2) * TP, (t % (T // 2) + 1) * TP)),
                                  at2(gH[j], slice(0, TP), slice(i * HALF, (i + 1) * HALF)), j == 0, j == T - 1)
                    close(ins)

            split("wv")
            for t in range(T):
                rows("mk", t, wqv[0])
                rows("mv", t, wqv[1])
            pe.wait_ge(sem("kv_rows"), 1)
            for i in range(2):
                ps = group("kvsum", i)
                close(mm(ps[0:TP, 0:HALF], ones[0:TP, 0:TP], prodsum[0:TP, i * HALF:(i + 1) * HALF], True, True))
            split("wq")
            for t in range(T):
                rows("mq", t, wq2)
            transposed("on", sem("on_rows"))
            all_emptied(pe, "T", "on", T - 1, 1)
            split("wpr")
            for t in range(T):
                rows("mproj", t, wpr)

            transposed("m1", sem("m1_rows"))
            all_emptied(pe, "T", "m1", T - 1, 1)
            split("wg")
            ps = group("logits1")
            for t in range(T):
                for k in range(KD):
                    ins = mm3(ps[0:TP, t * E1:(t + 1) * E1], at2(RT, slice(None), k, slice(t * TP, (t + 1) * TP)), at2(wgE, slice(None), k), k == 0, k == KD - 1)
            close(ins)
            pe.wait_ge(sem("onehot1"), 1)
            ps = group("order1")
            oh = L1[0:TP, :, :].rearrange("p t e -> p (t e)")
            mm(ps[0:TP, 0:80], upto[0:TP, 0:TP], oh, True, True)
            close(mm(ps[0:TP, 80:160], ones[0:TP, 0:TP], oh, True, True))
            emptied(pe, "order1")

            def turn_block():
                for i in range(2):
                    for j in range(3):
                        k = 3 * i + j
                        ins = nc.tensor.transpose(PS[i][:, j * BLK:(j + 1) * BLK], xb[:, k * 128:(k + 1) * 128], ident)
                ins.then_inc(sem("block_turned"), 1)

            pe.wait_ge(sem("in_xb"), 16)
            turn_block()
            pe.wait_ge(sem("blocks_known"), 1)
            for e in range(E1):
                b0 = pe.value_load(first_i[0:1, e:e + 1], min_val=e, max_val=MAXB - 1)
                b1_ = pe.value_load(first_i[0:1, e + 1:e + 2], min_val=e + 1, max_val=MAXB)
                pe.wait_ge(sem(f"in_fe{e % 2}"), 32 * (e // 2 + 1))
                with pe.Fori(b0, b1_) as b:
                    pe.wait_ge(sem("block_T_ready"), b + 1)
                    for f in range(F0C):
                        for k in range(KD):
                            ins = mm(PS[2][:, f * BLK:(f + 1) * BLK], w1E[e % 2][:, k, f * 128:(f + 1) * 128], xbT[:, k, :], k == 0, k == KD - 1)
                    ins.then_inc(sem("block_h"), 1)
                    pe.wait_ge(sem("in_xb"), b * 16 + 32)
                    turn_block()
                    pe.wait_ge(sem("block_h_ready"), b + 1)
                    pe.wait_ge(sem("block_out_emptied"), b + 1)
                    for i in range(2):
                        for f in range(F0C):
                            ins = mm(PS[4 + i][:, 0:HALF], hB[:, f, :], w2E[e % 2][:, f, i * HALF:(i + 1) * HALF], f == 0, f == F0C - 1)
                    ins.then_inc(sem("block_out"), 1)
            assert nth[0] == len(GROUPS)

        @block.scalar
        def _(act):
            do = Steps(act, own_a)
            A = nc.scalar.activation

            def high(key, o, view, func=ACT.Copy, **kw):
                filled(act, *key)
                assert SPLIT[key] == do.count.get(id(sem("high_made")), 0), key
                do(A(o, view(bank(*key)), func, **kw), sem("high_made"))

            def turned(name):
                for t in range(T):
                    for i in range(2):
                        high(("T", name, t, i), RT[0][:, 3 * i:3 * i + 3, t * TP:(t + 1) * TP], turned_bank)

            roots_done = []

            def root(x_, t):
                roots_done.append((x_, t))
                act.wait_ge(sem("variances"), len(roots_done))
                do(A(rstd[x_][0:TP, t:t + 1], rstd[x_][0:TP, t:t + 1], ACT.Sqrt), sem("roots"))

            for t in range(T):
                root(0, t)
            turned("xn")
            high(("rfT",), rfp[0], lambda b: b.rearrange("p (s m) -> p s m", s=2))
            act.wait_ge(sem("in_bqk"), 16)
            for p in range(MH // 2):
                for w, name in enumerate("qk"):
                    for c, (c0, cn) in enumerate(COLS):
                        high((name, p, c), (qT, kT)[w][0][:, c0:c0 + cn], lambda b: b[:, 0:cn], ACT.Identity, bias=bqk[:, w * 6 + p:w * 6 + p + 1])
                for s in range(2):
                    for m in range(2):
                        for c, (c0, cn) in enumerate(COLS):
                            high(("phiq", p, s, m, c), PQ[0][:, s, m, c0:c0 + cn], lambda b: b[:, 0:cn], ACT.Relu)
                    for i in range(T // 2):
                        high(("phik", p, s, i), PK[0][0:TP, s, 2 * i:2 * i + 2, :], phik_bank, ACT.Relu)
                for s in range(2):
                    if p + s == 0:
                        act.wait_ge(sem("pads"), 2)
                    high(("kv", p, s), kvpad[0][:, s, :, s * MD:(s + 1) * MD], kv_bank, scale=KV_SCALE)
                for c, (c0, cn) in enumerate(COLS):
                    high(("at", p, c), ATt[0][:, p, c0:c0 + cn], lambda b: b[:, 0:cn])
            all_emptied(act, "proj", T - 1, 1)
            for w in range(NW):
                act.wait_ge(sem("window_filled"), w + 1)
                do(A(CT[0:TP, :, w * WIN:(w + 1) * WIN], PS[6 + w % 2][0:TP, 0:500].rearrange("p (i t) -> p t i", t=T), ACT.Copy), sem("window_emptied"))
            act.wait_ge(sem("deg_copied"), 1)
            do(A(dinv[0:TP, :], dinv[0:TP, :], ACT.Sqrt), sem("deg_root"))

            def high_part(q):
                u, t0 = q // 2, q % 2 * HT
                act.wait_ge(sem("P_ready"), q + 1)
                if u >= 2:
                    agg_done(act, u - 2)
                do(A(Pm[u % 2][0][0:TP, t0:t0 + HT, :], U[0:TP, t0:t0 + HT, :], ACT.Copy), sem("P_high"))

            def lines(q):
                u, h0 = q // 2, q % 2 * HT
                col = u // NC if u < H1 * NC else 0
                if q % 2 == 0:
                    act.wait_ge(sem("coef_rows"), u + 1)
                    if u >= 2:
                        act.wait_ge(sem("exponents"), 2 * (u - 1))
                    do(A(ab_rows[u % 2][0:TP, :, :], PS[6 + u % 2][0:TP, 0:2 * IC].rearrange("p (a n) -> p a n", a=2), ACT.Copy), sem("coef_copied"))
                    do.settle()
                if q >= 2:
                    act.wait_ge(sem("P_low"), q - 1)
                    act.wait_ge(sem("P_sums"), q - 1)
                for t in range(h0, h0 + HT):
                    do(A(U[0:TP, t, :], ab_rows[u % 2][0:TP, 1, :], ACT.Identity, bias=AS2[0:TP, t, col:col + 1]), sem("lower_lines"))

            def exponential(q):
                h0 = q % 2 * HT
                act.wait_ge(sem("exponents"), q + 1)
                do(A(U[0:TP, h0:h0 + HT, :], U[0:TP, h0:h0 + HT, :], ACT.Exp), sem("exps"))

            act.wait_ge(sem("coef_cols"), 1)
            for q in range(LEAD):
                if q:
                    high_part(q - 1)
                lines(q)
                exponential(q)
            n_q = 2 * H1 * NC
            for h in range(H1):
                for t in range(T):
                    high(("h1", h, t), Hh[0][0:TP, t, :], lambda b: b[0:TP, :])
                for c in range(NC):
                    u = h * NC + c
                    for f in range(FC):
                        q = 2 * u + LEAD + f // 2
                        if f % 2 == 0 and q - 1 < n_q:
                            high_part(q - 1)
                        if f % 2 == 0 and q < n_q:
                            lines(q)
                        if f % 2 and q < n_q:
                            exponential(q)
                        n = u * FC + f
                        act.wait_ge(sem("elu_in"), n + 1)
                        do(A(elu_m[n % 2][:, :], elu_m[n % 2][:, :], ACT.Exp))
                        do(A(elu_z[n % 2][:, :], elu_z[n % 2][:, :], ACT.Relu, bias=b1c[:, h * FC + f:h * FC + f + 1]), sem("elu_parts"))
            act.wait_ge(sem("coef_cols"), 2)
            for q in range(n_q, n_q + 2 * NC + 1):
                if q > n_q:
                    high_part(q - 1)
                if q < n_q + 2 * NC:
                    lines(q)
                    exponential(q)
            for t in range(T):
                root(0, t)
            for t in range(T):
                root(1, t)
            turned("m0")
            act.wait_ge(sem("shifted0"), 1)
            do(A(G2[0:TP, :, :], G0[0:TP, :, :], ACT.Exp), sem("exp0"))
            for e in range(0, E0, 2):
                for i in range(2):
                    filled(act, "einT", e, i)
                    do(A(einT[:, 3 * i:3 * i + 3, :], bank("einT", e, i)[:, 0:384].rearrange("p (k n) -> p k n", k=3), ACT.Copy), freed("einT", e, i))
                for d in range(2):
                    filled(act, "eh", e + d)
                    do(A(hE[d], bank("eh", e + d)[:, 0:192].rearrange("p (k n) -> p k n", k=3), ACT.Relu), freed("eh", e + d))
            for t in range(T):
                root(0, t)
                if t:
                    root(1, t - 1)
            root(1, T - 1)
            turned("x2")
            for t in range(T):
                for i in range(2):
                    high(("gcnh", t, i), gH[t][0][0:TP, i * HALF:(i + 1) * HALF], lambda b: b[0:TP, 0:HALF], scale=dinv[0:TP, t:t + 1])
            turned("hn")
            for t in range(T):
                act.wait_ge(sem("k_sums"), t + 1)
                do(A(small[0:TP, t:t + 1], small[0:TP, t:t + 1], ACT.Sqrt), sem("k_norms"))
            for t in range(T):
                act.wait_ge(sem("q_sums"), t + 1)
                do(A(small[0:TP, 10 + t:11 + t], small[0:TP, 10 + t:11 + t], ACT.Sqrt), sem("q_norms"))
                root(0, t)
            turned("on")
            for t in range(T):
                root(0, t)
            turned("m1")
            act.wait_ge(sem("shifted1"), 1)
            do(A(L2[0:TP, :, :], L0[0:TP, :, :], ACT.Exp), sem("exp1"))
            act.wait_ge(sem("in_b1E"), 16 * E1)

            def block_T():
                for i in range(2):
                    ins = A(xbT[:, 3 * i:3 * i + 3, :], PS[i][:, 0:384].rearrange("p (k n) -> p k n", k=3), ACT.Copy)
                ins.then_inc(sem("block_T_ready"), 1)

            act.wait_ge(sem("block_turned"), 1)
            block_T()
            act.wait_ge(sem("blocks_known"), 1)
            for e in range(E1):
                b0 = act.value_load(first_i[0:1, e:e + 1], min_val=e, max_val=MAXB - 1)
                b1_ = act.value_load(first_i[0:1, e + 1:e + 2], min_val=e + 1, max_val=MAXB)
                with act.Fori(b0, b1_) as b:
                    act.wait_ge(sem("block_h"), b + 1)
                    for f in range(F0C):
                        ins = A(hB[:, f, :], PS[2][:, f * BLK:(f + 1) * BLK], ACT.Silu, bias=b1E[:, e, f:f + 1])
                    ins.then_inc(sem("block_h_ready"), 1)
                    act.wait_ge(sem("block_turned"), b + 2)
                    block_T()
                    act.wait_ge(sem("block_out_emptied"), b + 2)
                    act.dma_start(scr_out1[bass.ds(b * BLK, BLK), :], oB).then_inc(sem("block_stored"), 16)

        @block.gpsimd
        def _(pool):
            do = Steps(pool, own_g)
            g = nc.gpsimd
            do(g.memset(ones, 1.0), sem("consts"))
            do(g.memset(ident, 0.0))
            do.settle()
            do(g.affine_select(out=ident, in_=ident, compare_op=ALU.not_equal, fill=1.0, base=0, pattern=[[-1, 128]], channel_multiplier=1), sem("consts"))
            do(g.memset(upto, 1.0))
            do.settle()
            do(g.affine_select(out=upto, in_=upto, compare_op=ALU.is_ge, fill=0.0, base=0, pattern=[[1, 128]], channel_multiplier=-1), sem("consts"))
            do(g.memset(zeros, 0.0))
            do(g.memset(rfn, 0.0), sem("pads"))
            do(g.memset(kvpad[0], 0.0))
            do(g.memset(kvpad[1], 0.0), sem("pads"))
            next_piece = [0]

            def split_pieces(*names, most=len(pieces)):
                end = next_piece[0] + most
                for name in names:
                    while next_piece[0] < min(end, len(pieces)) and pieces[next_piece[0]][0] == name:
                        n = next_piece[0]
                        next_piece[0] += 1
                        _, a, (hi, lo), stage, place = pieces[n]
                        if n in piece_after:
                            filled(pool, *piece_after[n])
                        pool.wait_ge(sem(f"weight_in_{place[0]}{place[1]}"), 16 * len([1 for p in pieces[:n + 1] if p[4] == place]))
                        v = shaped(stage, a)
                        do(g.tensor_copy(hi, v))
                        do.settle()
                        do(g.tensor_tensor(lo, v, hi, ALU.subtract), sem("weights_split"))

            split_pieces("Wv", ("Wqk", 0), "Wp", *[("Wqk", p) for p in range(1, MH // 2)])
            pool.wait_ge(sem("in_bias"), 32)
            for t in range(T):
                all_emptied(pool, "proj", t, 1)
                do(g.tensor_tensor(R1[0:TP, t, :], R1[0:TP, t, :], bias_rows[0:TP, 0, :], ALU.add))
                do.settle()
                do(g.tensor_tensor(R1[0:TP, t, :], R1[0:TP, t, :], bias_rows[0:TP, 1, :], ALU.add), sem("bias_added"))
            pool.wait_ge(sem("in_edges"), 32)
            do(g.iota(iota_i, [[1, 500]], base=0, channel_multiplier=0), sem("iotas"))
            do(g.iota(iota_c_i, [[0, 1]], base=0, channel_multiplier=WIN), sem("iotas"))
            do(g.memset(upper, 1.0))
            do.settle()
            do(g.affine_select(out=upper, in_=upper, compare_op=ALU.is_ge, fill=0.0, base=-1, pattern=[[1, 32]], channel_multiplier=-1), sem("iotas"))
            do(g.memset(zero_bf, 0.0), sem("iota_set"))

            def sums(q):
                u, t0 = q // 2, q % 2 * HT
                if u >= 2 and q % 2 == 0:
                    agg_done(pool, u - 2)
                S = Sp[u % 2][0:TP, :]
                pool.wait_ge(sem("P_ready"), q + 1)
                for t in range(t0, t0 + HT):
                    if t == 0:
                        continue
                    if t > 1:
                        do.settle()
                    do(g.tensor_tensor(S, U[0:TP, 0, :] if t == 1 else S, U[0:TP, t, :], ALU.add), sem("P_sums") if t == t0 + HT - 1 else None)
                pool.wait_ge(sem("P_high"), q + 1)
                part = slice(t0, t0 + HT)
                do(g.tensor_tensor(Pm[u % 2][1][0:TP, part, :], U[0:TP, part, :], Pm[u % 2][0][0:TP, part, :], ALU.subtract), sem("P_low"))

            split_pieces(("W1h", 0), ("W2h", 0))
            for u in range(H1 * NC):
                sums(2 * u)
                sums(2 * u + 1)
                h = u // NC
                if u % NC == 0 and h:
                    split_pieces(("W2h", h))
                elif h + 1 < H1:
                    split_pieces(("W1h", h + 1), most=3)
            for t in range(T):
                pool.wait_ge(sem("h2_ready"), t + 1)
                tmp = h2_tmp[t % 2][0:TP, :]
                do(g.tensor_copy(tmp, R2[0:TP, t, :]))
                do.settle()
                do(g.tensor_copy(H2[t][0][0:TP, :], tmp))
                do.settle()
                do(g.tensor_tensor(H2[t][1][0:TP, :], tmp, H2[t][0][0:TP, :], ALU.subtract), sem("h2_split"))
            for q in range(2 * H1 * NC, 2 * (H1 * NC + NC)):
                sums(q)
            for t in range(T):
                pool.wait_ge(sem("y_rows"), t + 1)
                do(g.tensor_tensor(R1[0:TP, t, :], R1[0:TP, t, :], R2[0:TP, t, :], ALU.add), sem("y_added"))
            all_emptied(pool, "agg2", T - 1, 1)
            split_pieces("router")
            do(g.iota(e_i, [[0, T], [-1, E0]], base=E0, channel_multiplier=0), sem("iotas"))
            pool.wait_ge(sem("slots"), 1)
            pool.wait_ge(sem("slots_zeroed"), 48)
            for t in range(T):
                g.indirect_dma_start(scr_in, bass.IndirectOffsetOnAxis(ap=slot_s[0:TP, t:t + 1], axis=0), R2[0:TP, t, :], None,
                                     bounds_check=SLOTS - 1, oob_is_err=False).then_inc(sem("scattered"), 16)
            for i in range(2 * T):
                do(g.tensor_copy(ct_tmp[0:TP, :], CTt[0:TP, i * N // 2:(i + 1) * N // 2]))
                do.settle()
                do(g.tensor_copy(CT2[i][0][0:TP, :], ct_tmp[0:TP, :]))
                do.settle()
                do(g.tensor_tensor(CT2[i][1][0:TP, :], ct_tmp[0:TP, :], CT2[i][0][0:TP, :], ALU.subtract), sem("counts_split"))
                do.settle()
            for e in range(E0):
                for i in range(2):
                    emptied(pool, "eo", e, i)
                pool.dma_start(scr_out[e * CAP:(e + 1) * CAP, :], oE[e % 2][0:CAP, :]).then_inc(sem(f"out_kept{e % 2}"), 16)
            pool.wait_ge(sem("out_kept0"), 16 * E0 // 2)
            pool.wait_ge(sem("out_kept1"), 16 * E0 // 2)
            filled(pool, "eo", E0 - 1, 1)
            for t in range(T):
                if t >= 2:
                    pool.wait_ge(sem("gathered_used"), t - 1)
                g.indirect_dma_start(gath[t % 2][0:TP, :], None, scr_out, bass.IndirectOffsetOnAxis(ap=slot_g[0:TP, t:t + 1], axis=0),
                                     bounds_check=SLOTS - 1, oob_is_err=False).then_inc(sem(f"gathered{t % 2}"), 16)
            split_pieces("gW", "wk", "wv", "wq", "wpr")
            all_emptied(pool, "mproj", T - 1, 1)
            do(g.iota(e1_i, [[0, T], [-1, E1]], base=E1, channel_multiplier=0), sem("iotas"))
            do(g.memset(tick, 0.0))
            do.settle()
            split_pieces("wg")
            for e in range(2):
                pool.dma_start(w1E[e], kchunks(F1w[e])).then_inc(sem(f"in_fe{e}"), 16)
                pool.dma_start(w2E[e], kchunks(F2w[e])).then_inc(sem(f"in_fe{e}"), 16)
            pool.wait_ge(sem("slots1"), 1)
            for t in range(T):
                g.indirect_dma_start(scr_in1, bass.IndirectOffsetOnAxis(ap=slot1[0:TP, t:t + 1], axis=0), R2[0:TP, t, :], None,
                                     bounds_check=MAXB * BLK - 1, oob_is_err=False).then_inc(sem("scattered1"), 16)
            for e in range(2, E1):
                done = pool.value_load(first_i[0:1, e - 1:e], min_val=e - 1, max_val=MAXB)
                pool.wait_ge(sem("block_out"), done)
                do(g.tensor_tensor(tick, tick, tick, ALU.add))
                do.settle()
                pool.dma_start(w1E[e % 2], kchunks(F1w[e])).then_inc(sem(f"in_fe{e % 2}"), 16)
                pool.dma_start(w2E[e % 2], kchunks(F2w[e])).then_inc(sem(f"in_fe{e % 2}"), 16)
            blocks = pool.value_load(first_i[0:1, E1:E1 + 1], min_val=E1, max_val=MAXB)
            pool.wait_ge(sem("block_stored"), blocks * 16 + 16)
            do(g.tensor_tensor(tick, tick, tick, ALU.add))
            do.settle()
            for t in range(T):
                if t >= 2:
                    pool.wait_ge(sem("out_rows"), t - 1)
                g.indirect_dma_start(gath1[t % 2][0:TP, :], None, scr_out1, bass.IndirectOffsetOnAxis(ap=slot1[0:TP, t:t + 1], axis=0),
                                     bounds_check=MAXB * BLK - 1, oob_is_err=False).then_inc(sem(f"in_gath{t % 2}"), 16)

        @block.vector
        def _(v):
            do = Steps(v, own_v)
            V = nc.vector

            roots_asked = []
            root_of = {}

            def stats(x_, t, source, eps, rms=False):
                for i in range(2):
                    do(V.bn_stats(stat[x_][0:TP, 6 * i:6 * i + 6], source[0:TP, t, i * HALF:(i + 1) * HALF]))
                do.settle()
                do(V.bn_aggr(mv[x_][0:TP, t, :], stat[x_][0:TP, :]))
                do.settle()
                r = rstd[x_][0:TP, t:t + 1]
                roots_asked.append((x_, t))
                root_of[x_, t] = len(roots_asked)
                if rms:
                    do(V.scalar_tensor_tensor(r, mv[x_][0:TP, t, 0:1], mv[x_][0:TP, t, 0:1], mv[x_][0:TP, t, 1:2], ALU.mult, ALU.add))
                    do.settle()
                    do(V.tensor_scalar(r, r, eps, None, ALU.add), sem("variances"))
                else:
                    do(V.tensor_scalar(r, mv[x_][0:TP, t, 1:2], eps, None, ALU.add), sem("variances"))

            def scaled(x_, t, source, signal, rows=None, rms_row=None):
                r = rstd[x_][0:TP, t:t + 1]
                v.wait_ge(sem("roots"), root_of[x_, t])
                do(V.reciprocal(r, r))
                do.settle()
                o = R2[0:TP, t, :]
                if rms_row is not None:
                    do(V.scalar_tensor_tensor(o, source[0:TP, t, :], r, rms_row, ALU.mult, ALU.mult), signal)
                    return
                do(V.tensor_scalar(o, source[0:TP, t, :], mv[x_][0:TP, t, 0:1], r, ALU.subtract, ALU.mult), signal if rows is None else None)
                if rows is not None:
                    do.settle()
                    do(V.tensor_tensor(o, o, rows[0:TP, 0, :], ALU.mult))
                    do.settle()
                    do(V.tensor_tensor(o, o, rows[0:TP, 1, :], ALU.add), signal)

            def low(key, o, view, hi, scalar=None, op=None):
                v.wait_ge(sem("high_made"), SPLIT[key] + 1)
                b = view(bank(*key))
                if op is None:
                    do(V.tensor_tensor(o, b, hi, ALU.subtract), freed(*key))
                else:
                    do(V.scalar_tensor_tensor(o, b, scalar, hi, op, ALU.subtract), freed(*key))

            def turned_low(name):
                for t in range(T):
                    for i in range(2):
                        o, hi = (r[:, 3 * i:3 * i + 3, t * TP:(t + 1) * TP] for r in (RT[1], RT[0]))
                        low(("T", name, t, i), o, turned_bank, hi)

            for t in range(T):
                v.wait_ge(sem(f"in_x{t}"), 16)
                stats(0, t, R1, 1e-5)
                if t:
                    scaled(0, t - 1, R1, sem("xn_rows"))
            scaled(0, T - 1, R1, sem("xn_rows"))
            turned_low("xn")
            v.wait_ge(sem("in_bv"), 16)
            filled(v, "T", "xn", T - 1, 1)
            for t in range(T):
                for i in range(2):
                    filled(v, "v", t, i)
                    c = slice(i * HALF, (i + 1) * HALF)
                    do(V.tensor_tensor(v_tmp[0:TP, :], bank("v", t, i)[0:TP, 0:HALF], bv_row[0:TP, c], ALU.add), freed("v", t, i))
                    do.settle()
                    do(V.tensor_copy(Vr[t][0][0:TP, c], v_tmp[0:TP, :]))
                    do.settle()
                    do(V.tensor_tensor(Vr[t][1][0:TP, c], v_tmp[0:TP, :], Vr[t][0][0:TP, c], ALU.subtract), sem("v_split"))
                    do.settle()
            low(("rfT",), rfp[1], lambda b: b.rearrange("p (s m) -> p s m", s=2), rfp[0])
            for p in range(MH // 2):
                for w, name in enumerate("qk"):
                    for c, (c0, cn) in enumerate(COLS):
                        q2 = (qT, kT)[w]
                        low((name, p, c), q2[1][:, c0:c0 + cn], lambda b: b[:, 0:cn], q2[0][:, c0:c0 + cn], bqk[:, w * 6 + p:w * 6 + p + 1], ALU.add)
                for s in range(2):
                    for m in range(2):
                        for c, (c0, cn) in enumerate(COLS):
                            low(("phiq", p, s, m, c), PQ[1][:, s, m, c0:c0 + cn], lambda b: b[:, 0:cn], PQ[0][:, s, m, c0:c0 + cn], 0.0, ALU.max)
                    for i in range(T // 2):
                        low(("phik", p, s, i), PK[1][0:TP, s, 2 * i:2 * i + 2, :], phik_bank, PK[0][0:TP, s, 2 * i:2 * i + 2, :], 0.0, ALU.max)
                for s in range(2):
                    if p + s == 0:
                        v.wait_ge(sem("pads"), 2)
                    low(("kv", p, s), kvpad[1][:, s, :, s * MD:(s + 1) * MD], kv_bank, kvpad[0][:, s, :, s * MD:(s + 1) * MD], KV_SCALE, ALU.mult)
                for c, (c0, cn) in enumerate(COLS):
                    low(("at", p, c), ATt[1][:, p, c0:c0 + cn], lambda b: b[:, 0:cn], ATt[0][:, p, c0:c0 + cn])
            for t in range(T):
                for i in range(2):
                    filled(v, "proj", t, i)
                    do(V.tensor_tensor(R1[0:TP, t, i * HALF:(i + 1) * HALF], R1[0:TP, t, i * HALF:(i + 1) * HALF], bank("proj", t, i)[0:TP, 0:HALF], ALU.add), freed("proj", t, i))

            v.wait_ge(sem("bias_added"), T)
            v.wait_ge(sem("in_edges"), 32)
            do(V.tensor_copy(nat, nat_i))
            do.settle()
            do(V.tensor_scalar(tdiv, nat[:, 0, :], float(TP), None, ALU.is_ge))
            for m in range(2, T):
                do.settle()
                do(V.scalar_tensor_tensor(tdiv, nat[:, 0, :], float(TP * m), tdiv, ALU.is_ge, ALU.add))
            do.settle()
            do(V.scalar_tensor_tensor(keys[:, 0, :], nat[:, 1, :], float(T), tdiv, ALU.mult, ALU.add))
            do(V.scalar_tensor_tensor(keys[:, 1, :], tdiv, -float(TP), nat[:, 0, :], ALU.mult, ALU.add))
            do(V.tensor_reduce(gmm[:, 0:1], nat[:, 1, :], AX, ALU.min))
            do(V.tensor_reduce(gmm[:, 1:2], nat[:, 1, :], AX, ALU.max), sem("edge_keys"))
            v.wait_ge(sem("iotas"), 3)
            do(V.tensor_copy(iota, iota_i))
            do(V.tensor_copy(iota16, iota_i))
            do(V.tensor_copy(iota_c[:, 0:1], iota_c_i))
            for a in range(2):
                filled(v, "edgeT", a)
                do(V.tensor_copy(KL[0:TP, a, :, :], bank("edgeT", a)[0:TP, 0:320].rearrange("p (q g) -> p q g", q=QG)), freed("edgeT", a))
            do.settle()
            do(V.tensor_scalar(iota_c[:, 1:2], iota_c[:, 0:1], float(WIN), None, ALU.add))
            filled(v, "groupB")
            do.settle()
            ps = bank("groupB")
            do(V.tensor_scalar(cutI, ps[0:NW, 0:NG], iota_c[0:NW, 1:2], None, ALU.is_lt))
            do.settle()
            do(V.scalar_tensor_tensor(cutI, ps[0:NW, NG:2 * NG], iota_c[0:NW, 0:1], cutI, ALU.is_ge, ALU.mult), freed("groupB"))
            do(V.tensor_scalar(cutJ, iota[0:NW, 0:NG], -1.0, float(NG - 1), ALU.mult, ALU.add))
            do.settle()
            do(V.tensor_tensor(cutJ, cutJ, cutI, ALU.mult))
            do(V.scalar_tensor_tensor(cutK, iota[0:NW, 0:NG], 1.0, cutI, ALU.add, ALU.mult))
            do.settle()
            do(V.tensor_reduce(tab[:, 3:4], cutJ, AX, ALU.max))
            do(V.tensor_reduce(tab[:, 4:5], cutK, AX, ALU.max))
            do.settle()
            do(V.tensor_scalar(tab[:, 0:1], tab[:, 3:4], -1.0, float(NG - 1), ALU.mult, ALU.add))
            do.settle()
            do(V.scalar_tensor_tensor(tab[:, 1:2], tab[:, 0:1], 1.0, tab[:, 4:5], ALU.add, ALU.max))
            do.settle()
            do(V.tensor_tensor(tab[:, 2:3], tab[:, 1:2], tab[:, 0:1], ALU.subtract), sem("window_cols"))
            filled(v, "tables")
            ps = bank("tables")
            do(V.tensor_copy(trow_i[:, 0:2 * NW], ps[0:1, 0:2 * NW]))
            do(V.tensor_scalar(trow[:, 0:NW], ps[0:1, 0:NW], -2.0, float(BIAS), ALU.mult, ALU.add))
            do.settle()
            do(V.scalar_tensor_tensor(trow_i[:, 2 * NW:3 * NW], ps[0:1, 2 * NW:3 * NW], 2.0, trow[:, 0:NW], ALU.mult, ALU.add), freed("tables"))
            do.settle()
            do(V.tensor_copy(tab[0:1, 5:6], tab[0:1, 4:5]), sem("window_table"))
            v.sem_inc(sem("onehots_ready"), BIAS)
            for w in range(NW):
                g0 = v.value_load(trow_i[0:1, w:w + 1], min_val=0, max_val=NG - 1)
                g1 = v.value_load(trow_i[0:1, NW + w:NW + w + 1], min_val=1, max_val=NG)
                base = v.value_load(trow_i[0:1, 2 * NW + w:2 * NW + w + 1], min_val=0, max_val=2 * NG * NW + BIAS)
                if w:
                    do(V.tensor_copy(tab[0:1, 5:6], tab[0:1, 4:5]))
                    do.settle()
                    do(V.tensor_scalar(KL[0:TP, 0, :, :], KL[0:TP, 0, :, :], -float(WIN * T), None, ALU.add))
                do.settle()
                with v.Fori(g0, g1) as g:
                    for half in range(2):
                        v.wait_ge(sem("onehots_used"), base + g * 2 + (half + 1))
                        for q in range(2 * half, 2 * half + 2):
                            V.tensor_scalar(oh_lo[q][0:TP, 0:TP], iota16[0:TP, 0:TP], KL[0:TP, 1, q, bass.ds(g, 1)], None, ALU.is_equal)
                            ins = V.tensor_scalar(oh_key[q][0:TP, 0:500], iota16[0:TP, 0:500], KL[0:TP, 0, q, bass.ds(g, 1)], None, ALU.is_equal)
                        ins.then_inc(sem("onehots_ready"), 1)
            v.wait_ge(sem("window_emptied"), NW)
            for t in range(T):
                do(V.tensor_tensor(CT[0:TP, t, t * TP:(t + 1) * TP], CT[0:TP, t, t * TP:(t + 1) * TP], ident[0:TP, 0:TP], ALU.add))
            do.settle()
            do(V.tensor_reduce(degp[0:TP, :], CT[0:TP, :, :].rearrange("p t n -> p n t"), AX, ALU.add), sem("deg_parts"))
            filled(v, "deg")
            do(V.tensor_copy(dinv[0:TP, :], bank("deg")[0:TP, 0:T]), sem("deg_copied"))
            v.wait_ge(sem("deg_root"), 1)
            do(V.reciprocal(dinv[0:TP, :], dinv[0:TP, :]), freed("deg"))

            v.wait_ge(sem("in_a1"), 32)
            for h in range(H1):
                v.wait_ge(sem(f"in_W1s{h % 2}"), 16 * (h // 2 + 1))
                for k in range(KD):
                    for a in range(2):
                        if k + a or h:
                            do.settle()
                        do(V.tensor_tensor_reduce(junk[:, 0:HID], W1s[h % 2][:, k, :], arow[:, a, h * HID:(h + 1) * HID], 1.0, 0.0,
                                                  ALU.mult, ALU.add, wa[:, k, 4 * a + h:4 * a + h + 1]), sem("W1_folded") if k == KD - 1 and a else None)
            do.settle()
            do(V.tensor_copy(wa2[0], wa))
            do.settle()
            do(V.tensor_tensor(wa2[1], wa, wa2[0], ALU.subtract), sem("fold_split"))
            filled(v, "coef1")
            do(V.tensor_copy(AS[0:TP, :, :], bank("coef1")[0:TP, 0:80].rearrange("p (t n) -> p t n", t=T)))
            do(V.tensor_scalar(AS2[0:TP, :, :], bank("coef1")[0:TP, 0:80].rearrange("p (t n) -> p t n", t=T), 0.2, None, ALU.mult), freed("coef1"))
            do.settle()

            def neighbour_max(acc, mask, cols):
                for t in range(T):
                    do(V.tensor_scalar(mask[0:TP, :], CT[0:TP, t, :], 0.0, -BIG, ALU.is_equal, ALU.mult))
                    do.settle()
                    for a, col in zip(acc, cols):
                        if t == 0:
                            do(V.tensor_scalar(a[0:TP, :], mask[0:TP, :], AS[0:TP, t, col:col + 1], None, ALU.add))
                        else:
                            do(V.scalar_tensor_tensor(a[0:TP, :], mask[0:TP, :], AS[0:TP, t, col:col + 1], a[0:TP, :], ALU.add, ALU.max))
                    do.settle()

            def coef_columns(h, key, dcol):
                for i in range(3):
                    filled(v, *key, i)
                    n = min(4, T - 4 * i)
                    do(V.tensor_reduce(Mx[0:TP, h, 4 * i:4 * i + n], bank(*key, i)[0:TP, 0:n * TP].rearrange("p (t n) -> p t n", t=n), AX, ALU.max), freed(*key, i))
                do.settle()
                do(V.tensor_tensor(Mx[0:TP, h, :], Mx[0:TP, h, :], AS[0:TP, :, dcol], ALU.add))
                do.settle()
                do(V.scalar_tensor_tensor(Mx[0:TP, h, :], Mx[0:TP, h, :], 0.2, Mx[0:TP, h, :], ALU.mult, ALU.max))
                do.settle()
                do(V.tensor_tensor(Ac[0:TP, h, :], AS[0:TP, :, dcol], Mx[0:TP, h, :], ALU.subtract))
                return do(V.tensor_tensor(Bc[0:TP, h, :], AS2[0:TP, :, dcol], Mx[0:TP, h, :], ALU.subtract))

            neighbour_max([maxacc[:, h, :] for h in range(H1)], maskt, range(H1))
            do(V.tensor_copy(small[0:TP, 0:1], AS[0:TP, 0, 0:1]), sem("max_rows"))
            for h in range(H1):
                coef_columns(h, ("max1", h), 4 + h)
            do.settle()
            do(V.tensor_copy(small[0:TP, 0:1], AS[0:TP, 0, 0:1]), sem("coef_cols"))

            def exponents(q):
                u, h0 = q // 2, q % 2 * HT
                col = u // NC if u < H1 * NC else 0
                v.wait_ge(sem("lower_lines"), (q + 1) * HT)
                for t in range(h0, h0 + HT):
                    do(V.scalar_tensor_tensor(U[0:TP, t, :], ab_rows[u % 2][0:TP, 0, :], AS[0:TP, t, col:col + 1], U[0:TP, t, :], ALU.add, ALU.max),
                       sem("exponents") if t == h0 + HT - 1 else None)

            def counted(q):
                h0, c = q % 2 * HT, q // 2 % NC
                v.wait_ge(sem("exps"), q + 1)
                do(V.scalar_tensor_tensor(U[0:TP, h0:h0 + HT, :], U[0:TP, h0:h0 + HT, :], 1.0, CT[0:TP, h0:h0 + HT, c * IC:(c + 1) * IC],
                                          ALU.min, ALU.mult), sem("P_ready"))

            def elu_in(h, c, f):
                u = h * NC + c
                n = u * FC + f
                if n >= 2:
                    v.wait_ge(sem("elu_done"), n - 1)
                filled(v, "agg1", h, c, f)
                do(V.tensor_tensor(elu_z[n % 2][:, :], bank("agg1", h, c, f)[:, 0:IC], rden[:, :], ALU.mult), freed("agg1", h, c, f))
                do.settle()
                do(V.tensor_scalar(elu_m[n % 2][:, :], elu_z[n % 2][:, :], b1c[:, h * FC + f:h * FC + f + 1], 0.0, ALU.add, ALU.min), sem("elu_in"))

            def elu_out(h, c, f):
                u = h * NC + c
                n = u * FC + f
                z = elu_z[n % 2][:, :]
                v.wait_ge(sem("elu_parts"), n + 1)
                do(V.scalar_tensor_tensor(z, elu_m[n % 2][:, :], -1.0, z, ALU.add, ALU.add))
                do.settle()
                do(V.tensor_copy(H1T[u % 2][0][:, f, :], z))
                do.settle()
                do(V.tensor_tensor(H1T[u % 2][1][:, f, :], z, H1T[u % 2][0][:, f, :], ALU.subtract), sem("elu_done"))

            def w2_rows(h, c):
                for t in range(c * TC, (c + 1) * TC):
                    for i in range(2):
                        filled(v, "w2", h, t, i)
                        o, ps = R2[0:TP, t, i * HALF:(i + 1) * HALF], bank("w2", h, t, i)[0:TP, 0:HALF]
                        if h == 0:
                            do(V.tensor_copy(o, ps), freed("w2", h, t, i))
                        else:
                            do(V.tensor_tensor(o, o, ps, ALU.add), freed("w2", h, t, i))

            v.wait_ge(sem("in_b1"), 16)
            for q in range(LEAD):
                exponents(q)
                counted(q)
            for h in range(H1):
                for t in range(T):
                    low(("h1", h, t), Hh[1][0:TP, t, :], lambda b: b[0:TP, :], Hh[0][0:TP, t, :])
                for c in range(NC):
                    u = h * NC + c
                    filled(v, "den1", h, c)
                    do(V.tensor_scalar(rden[:, :], bank("den1", h, c)[:, 0:IC], 1e-16, None, ALU.add), freed("den1", h, c))
                    do.settle()
                    do(V.reciprocal(rden[:, :], rden[:, :]))
                    do.settle()
                    for f in range(FC):
                        elu_in(h, c, f)
                        q = 2 * u + LEAD + f // 2
                        if q < 2 * H1 * NC:
                            (counted if f % 2 else exponents)(q)
                        if f:
                            elu_out(h, c, f - 1)
                    elu_out(h, c, FC - 1)
                    if c:
                        w2_rows(h, c - 1)
                w2_rows(h, NC - 1)

            v.wait_ge(sem("in_a2"), 32)
            for t in range(T):
                for a in range(2):
                    do.settle()
                    do(V.tensor_tensor_reduce(junk2[0:TP, :], R2[0:TP, t, :], a2row[0:TP, a, :], 1.0, 0.0, ALU.mult, ALU.add, AS[0:TP, t, 4 * a:4 * a + 1]),
                       sem("h2_ready") if a else None)
            do.settle()
            do(V.tensor_scalar(AS2[0:TP, :, :], AS[0:TP, :, :], 0.2, None, ALU.mult))
            do.settle()
            neighbour_max([max2a], mask2, [0])
            do(V.tensor_copy(small[0:TP, 0:1], AS[0:TP, 0, 0:1]), sem("max_rows"))
            coef_columns(0, ("max2",), 4)
            do.settle()
            do(V.tensor_copy(small[0:TP, 0:1], AS[0:TP, 0, 0:1]), sem("coef_cols"))
            v.wait_ge(sem("xm_back"), 16)
            q0 = 2 * H1 * NC
            for q in range(LEAD):
                exponents(q0 + q)
                counted(q0 + q)
            for c in range(NC):
                filled(v, "den2", c)
                do(V.tensor_scalar(rd2[0:TP, :], bank("den2", c)[0:TP, 0:TC], 1e-16, None, ALU.add), freed("den2", c))
                do.settle()
                do(V.reciprocal(rd2[0:TP, :], rd2[0:TP, :]))
                do.settle()
                for t in range(TC):
                    for i in range(2):
                        tt = c * TC + t
                        q = 2 * c + LEAD + t
                        if q < 2 * NC:
                            (counted if i else exponents)(q0 + q)
                        filled(v, "agg2", tt, i)
                        o = R1[0:TP, tt, i * HALF:(i + 1) * HALF]
                        do(V.scalar_tensor_tensor(o, bank("agg2", tt, i)[0:TP, 0:HALF], rd2[0:TP, t:t + 1], o, ALU.mult, ALU.add), freed("agg2", tt, i))
                    do.settle()
                    stats(0, tt, R1, 1e-5)

            v.wait_ge(sem("in_lnw"), 16)
            for t in range(T):
                scaled(0, t, R1, sem("y_rows"))
                do.settle()
                stats(1, t, R2, 1e-6, rms=True)
                if t:
                    v.wait_ge(sem("y_added"), t)
                    scaled(1, t - 1, R2, sem("normed_rows"), rms_row=lnw_row[0:TP, :])
            v.wait_ge(sem("y_added"), T)
            scaled(1, T - 1, R2, sem("normed_rows"), rms_row=lnw_row[0:TP, :])
            turned_low("m0")
            filled(v, "logits0")
            lg = bank("logits0")[0:TP, 0:160].rearrange("p (t e) -> p t e", t=T)

            def wide(col, n):
                return col.unsqueeze(2).to_broadcast([TP, T, n])

            g0, g1_, g2, g3 = (a[0:TP] for a in (G0, G1, G2, G3))
            eb, es, gc = ebase[0:TP], esort[0:TP], gcol[0:TP]
            do(V.tensor_copy(g3, lg), freed("logits0"))
            do.settle()
            do(V.tensor_reduce(gc[:, 0, :], g3, AX, ALU.max))
            v.wait_ge(sem("iotas"), 4)
            do(V.tensor_copy(es, e_i[0:TP].rearrange("p (t e) -> p t e", t=T)))
            do.settle()
            do(V.tensor_tensor(g0, g3, wide(gc[:, 0, :], E0), ALU.subtract), sem("shifted0"))
            do(V.tensor_scalar(eb, es, -float(CAP), float(CAP * E0), ALU.mult, ALU.add))
            do(V.tensor_tensor(g1_, g3, wide(gc[:, 0, :], E0), ALU.is_equal))
            do.settle()
            do(V.tensor_tensor(g1_, g1_, es, ALU.mult))
            do.settle()
            do(V.tensor_reduce(gc[:, 1, :], g1_, AX, ALU.max))
            do.settle()
            do(V.tensor_tensor(g1_, es, wide(gc[:, 1, :], E0), ALU.is_equal), sem("onehot0"))
            v.wait_ge(sem("exp0"), 1)
            do(V.tensor_reduce(gc[:, 2, :], g2, AX, ALU.add))
            do.settle()
            do(V.reciprocal(gc[:, 3, :], gc[:, 2, :]))
            filled(v, "order0")
            ps = bank("order0")
            do(V.memset(g0[:, 0, :], 0.0))
            for t in range(1, T):
                do.settle()
                do(V.tensor_tensor(g0[:, t, :], g0[:, t - 1, :], ps[0:TP, 160 + (t - 1) * E0:160 + t * E0], ALU.add))
            do.settle()
            do(V.tensor_tensor(g3, g0, ps[0:TP, 0:160].rearrange("p (t e) -> p t e", t=T), ALU.add), freed("order0"))
            do.settle()
            do(V.tensor_tensor(g3, g3, g1_, ALU.mult))
            do(V.tensor_tensor(g2, eb, g1_, ALU.mult))
            do.settle()
            do(V.tensor_reduce(gc[:, 4, :], g3, AX, ALU.add))
            do(V.tensor_reduce(gc[:, 5, :], g2, AX, ALU.add))
            do.settle()
            do(V.tensor_scalar(gc[:, 6, :], gc[:, 4, :], float(CAP), None, ALU.is_le))
            do(V.scalar_tensor_tensor(gc[:, 7, :], gc[:, 4, :], -1.0, gc[:, 5, :], ALU.add, ALU.add))
            do.settle()
            do(V.tensor_scalar(gc[:, 8, :], gc[:, 6, :], -1.0, 1.0, ALU.mult, ALU.add))
            do(V.tensor_tensor(gc[:, 9, :], gc[:, 7, :], gc[:, 6, :], ALU.mult))
            do(V.tensor_tensor(gc[:, 10, :], gc[:, 6, :], gc[:, 3, :], ALU.mult))
            do.settle()
            do(V.scalar_tensor_tensor(gc[:, 7, :], gc[:, 8, :], float(4 * SLOTS), gc[:, 9, :], ALU.mult, ALU.add))
            do(V.tensor_tensor(gc[:, 11, :], gc[:, 8, :], gc[:, 3, :], ALU.mult))
            do.settle()
            do(V.tensor_copy(slot_g[0:TP, :], gc[:, 9, :]))
            do(V.tensor_copy(slot_s[0:TP, :], gc[:, 7, :]), sem("slots"))
            v.wait_ge(sem("scattered"), 16 * T)
            for t in range(T):
                do(V.scalar_tensor_tensor(R1[0:TP, t, :], R2[0:TP, t, :], gc[:, 11, t:t + 1], R1[0:TP, t, :], ALU.mult, ALU.add))
            for e in range(E0):
                if e >= 2:
                    v.wait_ge(sem(f"out_kept{e % 2}"), 16 * (e // 2))
                for i in range(2):
                    filled(v, "eo", e, i)
                    do(V.tensor_copy(oE[e % 2][0:CAP, i * HALF:(i + 1) * HALF], bank("eo", e, i)[0:CAP, 0:HALF]), freed("eo", e, i))
            do.settle()
            for t in range(T):
                v.wait_ge(sem(f"gathered{t % 2}"), 16 * (t // 2 + 1))
                do(V.scalar_tensor_tensor(R1[0:TP, t, :], gath[t % 2][0:TP, :], gc[:, 10, t:t + 1], R1[0:TP, t, :], ALU.mult, ALU.add), sem("gathered_used"))
                do.settle()
                stats(0, t, R1, 1e-5)
                if t:
                    scaled(0, t - 1, R1, sem("x2_rows"))
                    do.settle()
                    stats(1, t - 1, R2, 1e-5)
            scaled(0, T - 1, R1, sem("x2_rows"))
            do.settle()
            stats(1, T - 1, R2, 1e-5)
            do(V.tensor_copy(small[0:TP, 0:1], AS[0:TP, 0, 0:1]), sem("moe0_read"))

            turned_low("x2")
            v.wait_ge(sem("in_ln"), 32)
            filled(v, "T", "x2", T - 1, 1)
            for t in range(T):
                scaled(1, t, R2, sem("hn_rows"), rows=grow2)
                do.settle()
                for i in range(2):
                    c = slice(i * HALF, (i + 1) * HALF)
                    low(("gcnh", t, i), gH[t][1][0:TP, c], lambda b: b[0:TP, 0:HALF], gH[t][0][0:TP, c], dinv[0:TP, t:t + 1], ALU.mult)
            turned_low("hn")
            v.wait_ge(sem("in_gb"), 16)
            for t in range(T):
                do(V.tensor_tensor(R1[0:TP, t, :], R1[0:TP, t, :], grow[0:TP, :], ALU.add))
            do.settle()
            for t in range(T):
                for i in range(2):
                    filled(v, "gcn", t, i)
                    o = R1[0:TP, t, i * HALF:(i + 1) * HALF]
                    do(V.scalar_tensor_tensor(o, bank("gcn", t, i)[0:TP, 0:HALF], dinv[0:TP, t:t + 1], o, ALU.mult, ALU.add), freed("gcn", t, i))

            for t in range(T):
                kk = kt_[0]
                for i in range(2):
                    filled(v, "mk", t, i)
                    do(V.tensor_copy(kk[0:TP, i * HALF:(i + 1) * HALF], bank("mk", t, i)[0:TP, 0:HALF]), freed("mk", t, i))
                do.settle()
                do(V.tensor_tensor_reduce(sq_[0:TP, :], kk[0:TP, :], kk[0:TP, :], 1.0, 0.0, ALU.mult, ALU.add, small[0:TP, t:t + 1]), sem("k_sums"))
                v.wait_ge(sem("k_norms"), t + 1)
                do(V.tensor_scalar(small[0:TP, t:t + 1], small[0:TP, t:t + 1], 1e-12, None, ALU.max))
                do.settle()
                do(V.reciprocal(small[0:TP, t:t + 1], small[0:TP, t:t + 1]))
                do.settle()
                for i in range(2):
                    filled(v, "mv", t, i)
                    o = prodsum if t == 0 else psum_row
                    do(V.scalar_tensor_tensor(o[0:TP, i * HALF:(i + 1) * HALF], kk[0:TP, i * HALF:(i + 1) * HALF], small[0:TP, t:t + 1],
                                              bank("mv", t, i)[0:TP, 0:HALF], ALU.mult, ALU.mult), freed("mv", t, i))
                do.settle()
                if t:
                    do(V.tensor_tensor(prodsum[0:TP, :], prodsum[0:TP, :], psum_row[0:TP, :], ALU.add), sem("kv_rows") if t == T - 1 else None)
                    do.settle()
            for i in range(2):
                filled(v, "kvsum", i)
                do(V.tensor_copy(kvb[0:TP, i * HALF:(i + 1) * HALF], bank("kvsum", i)[0:TP, 0:HALF]), freed("kvsum", i))
            do.settle()
            filled(v, "mv", T - 1, 1)
            v.wait_ge(sem("in_ln"), 64)
            for t in range(T):
                qq = kt_[1]
                for i in range(2):
                    filled(v, "mq", t, i)
                    do(V.tensor_copy(qq[0:TP, i * HALF:(i + 1) * HALF], bank("mq", t, i)[0:TP, 0:HALF]), freed("mq", t, i))
                do.settle()
                do(V.tensor_tensor_reduce(sq_[0:TP, :], qq[0:TP, :], qq[0:TP, :], 1.0, 0.0, ALU.mult, ALU.add, small[0:TP, 10 + t:11 + t]), sem("q_sums"))
                v.wait_ge(sem("q_norms"), t + 1)
                do(V.tensor_scalar(small[0:TP, 10 + t:11 + t], small[0:TP, 10 + t:11 + t], 1e-12, None, ALU.max))
                do.settle()
                do(V.reciprocal(small[0:TP, 10 + t:11 + t], small[0:TP, 10 + t:11 + t]))
                do.settle()
                do(V.scalar_tensor_tensor(R2[0:TP, t, :], qq[0:TP, :], small[0:TP, 10 + t:11 + t], kvb[0:TP, :], ALU.mult, ALU.mult))
                do.settle()
                stats(0, t, R2, 1e-5)
                if t:
                    scaled(0, t - 1, R2, sem("on_rows"), rows=grow2)
            scaled(0, T - 1, R2, sem("on_rows"), rows=grow2)
            turned_low("on")
            for t in range(T):
                for i in range(2):
                    filled(v, "mproj", t, i)
                    o = R1[0:TP, t, i * HALF:(i + 1) * HALF]
                    do(V.tensor_tensor(o, o, bank("mproj", t, i)[0:TP, 0:HALF], ALU.add), freed("mproj", t, i))
                do.settle()
                if t == 0:
                    filled(v, "T", "on", T - 1, 1)
                stats(0, t, R1, 1e-5)
                if t:
                    scaled(0, t - 1, R1, sem("m1_rows"))

            scaled(0, T - 1, R1, sem("m1_rows"))
            turned_low("m1")
            filled(v, "logits1")
            l0, l1, l2, l3, e1_, lc = (a[0:TP] for a in (L0, L1, L2, L3, esort1, lcol))
            do(V.tensor_copy(l3, bank("logits1")[0:TP, 0:80].rearrange("p (t e) -> p t e", t=T)), freed("logits1"))
            do.settle()
            do(V.tensor_reduce(lc[:, 0, :], l3, AX, ALU.max))
            v.wait_ge(sem("iotas"), 5)
            do(V.tensor_copy(e1_, e1_i[0:TP].rearrange("p (t e) -> p t e", t=T)))
            do.settle()
            do(V.tensor_tensor(l0, l3, wide(lc[:, 0, :], E1), ALU.subtract), sem("shifted1"))
            do(V.tensor_tensor(l1, l3, wide(lc[:, 0, :], E1), ALU.is_equal))
            do.settle()
            do(V.tensor_tensor(l1, l1, e1_, ALU.mult))
            do.settle()
            do(V.tensor_reduce(lc[:, 1, :], l1, AX, ALU.max))
            do.settle()
            do(V.tensor_tensor(l1, e1_, wide(lc[:, 1, :], E1), ALU.is_equal), sem("onehot1"))
            v.wait_ge(sem("exp1"), 1)
            do(V.tensor_reduce(lc[:, 2, :], l2, AX, ALU.add))
            do.settle()
            do(V.reciprocal(lc[:, 3, :], lc[:, 2, :]))
            filled(v, "order1")
            ps = bank("order1")
            tot = ps[0:TP, 80:160].rearrange("p (t e) -> p t e", t=T)
            do(V.tensor_reduce(cnt1[0:TP, :], tot.rearrange("p t e -> p e t"), AX, ALU.add))
            do(V.memset(l0[:, 0, :], 0.0))
            for t in range(1, T):
                do.settle()
                do(V.tensor_tensor(l0[:, t, :], l0[:, t - 1, :], tot[:, t - 1, :], ALU.add))
            do.settle()
            do(V.tensor_tensor(l3, l0, ps[0:TP, 0:80].rearrange("p (t e) -> p t e", t=T), ALU.add), freed("order1"))
            do(V.tensor_scalar(nblk[0:TP, :], cnt1[0:TP, :], float(BLK), 1.0, ALU.is_gt, ALU.add))
            for m in range(2, N // BLK + 1):
                do.settle()
                do(V.scalar_tensor_tensor(nblk[0:TP, :], cnt1[0:TP, :], float(BLK * m), nblk[0:TP, :], ALU.is_gt, ALU.add))
            do(V.memset(first1[0:TP, 0:1], 0.0))
            for e in range(E1):
                do.settle()
                do(V.tensor_tensor(first1[0:TP, e + 1:e + 2], first1[0:TP, e:e + 1], nblk[0:TP, e:e + 1], ALU.add))
            do.settle()
            do(V.tensor_copy(first_i[0:TP, :], first1[0:TP, :]))
            do(V.tensor_scalar(l2, first1[0:TP, 0:E1].unsqueeze(1).to_broadcast([TP, T, E1]), float(BLK), -1.0, ALU.mult, ALU.add))
            do.settle()
            do(V.tensor_tensor(l3, l3, l2, ALU.add))
            do.settle()
            do(V.tensor_tensor(l3, l3, l1, ALU.mult))
            do.settle()
            do(V.tensor_reduce(lc[:, 4, :], l3, AX, ALU.add))
            do.settle()
            do(V.tensor_copy(slot1[0:TP, :], lc[:, 4, :]), sem("slots1"))
            v.wait_ge(sem("scattered1"), 16 * T)
            do(V.tensor_copy(small[0:TP, 0:1], small[0:TP, 1:2]), sem("blocks_known"))
            v.wait_ge(sem("in_b2E"), 16 * E1)
            v.sem_inc(sem("block_out_emptied"), 1)
            v.sem_inc(sem("block_stored"), 16)
            for e in range(E1):
                b0 = v.value_load(first_i[0:1, e:e + 1], min_val=e, max_val=MAXB - 1)
                b1_ = v.value_load(first_i[0:1, e + 1:e + 2], min_val=e + 1, max_val=MAXB)
                with v.Fori(b0, b1_) as b:
                    v.wait_ge(sem("block_out"), b + 1)
                    v.wait_ge(sem("block_stored"), b * 16 + 16)
                    for i in range(2):
                        ins = V.tensor_tensor(oB[:, i * HALF:(i + 1) * HALF], PS[4 + i][:, 0:HALF], b2row[:, e, i * HALF:(i + 1) * HALF], ALU.add)
                    ins.then_inc(sem("block_out_emptied"), 1)
            for t in range(T):
                v.wait_ge(sem(f"in_gath{t % 2}"), 16 * (t // 2 + 1))
                do(V.scalar_tensor_tensor(R1[0:TP, t, :], gath1[t % 2][0:TP, :], lc[:, 3, t:t + 1], R1[0:TP, t, :], ALU.mult, ALU.add), sem("out_rows"))


_INS = ["x", "src", "dst", "L0_gnn_W1", "L0_gnn_a1_src", "L0_gnn_a1_dst", "L0_gnn_b1", "L0_gnn_W2", "L0_gnn_a2_src",
        "L0_gnn_a2_dst", "L0_gnn_b2", "L0_mix_W_qkv", "L0_mix_b_qkv", "L0_mix_W_proj", "L0_mix_b_proj",
        "L0_mix_random_features", "L0_ffn_ln_w", "L0_ffn_w_router", "L0_ffn_wi", "L0_ffn_wo", "L1_gnn_W", "L1_gnn_b",
        "L1_mix_w_qkv", "L1_mix_w_proj", "L1_mix_ln_in_g", "L1_mix_ln_in_b", "L1_mix_ln_out_g", "L1_mix_ln_out_b",
        "L1_ffn_Wg", "L1_ffn_W1", "L1_ffn_b1", "L1_ffn_W2", "L1_ffn_b2"]


def kernel(**inputs):
    import numpy as _np
    import concourse.bacc as _bacc
    from concourse import mybir as _mybir
    from concourse.bass_utils import run_bass_kernel_spmd as _run

    nc = _bacc.Bacc("TRN2", target_bir_lowering=False, num_devices=1)
    arrays, args = {}, []
    for name in _INS:
        a = _np.ascontiguousarray(inputs[name])
        arrays[f"in_{name}_dram"] = a
        args.append(nc.dram_tensor(f"in_{name}_dram", a.shape, _mybir.dt.from_np(a.dtype), kind="ExternalInput").ap())
    args.append(nc.dram_tensor("out_0_dram", (1250, 768), _mybir.dt.float32, kind="ExternalOutput").ap())
    build(nc, *args)
    r = _run(nc, [arrays], core_ids=[0])
    return r.results[0]["out_0_dram"]
```
